# Optimizing a Trainium2 kernel written in Bass

```python
import numpy as np
import jax
import jax.numpy as jnp

def _softmax(x, axis=-1):
    return jax.nn.softmax(x, axis=axis)

def _gelu(x):
    return jax.nn.gelu(x, approximate=True)

def _silu(x):
    return jax.nn.silu(x)

def _sigmoid(x):
    return jax.nn.sigmoid(x)

def _layernorm(x, axis=-1, eps=1e-05):
    m = jnp.mean(x, axis=axis, keepdims=True)
    v = jnp.var(x, axis=axis, keepdims=True)
    return (x - m) / jnp.sqrt(v + eps)

def _scatter_add(tgt, idx, src, axis=0):
    return tgt.at[idx].add(src)

def _segment_sum(src, seg, n):
    return jax.ops.segment_sum(src, seg, n)
kernel_name = 'mk_xattn_ffn_d4_seqx_r8_1718f1'

def setup_inputs(seed: int=0):
    np.random.seed(seed)
    _w = jnp.asarray

    def _rec_inputs():
        import jax
        import jax.numpy as jnp
        _rk = jax.random.key(seed)
        x = -0.0003929 + 0.9999 * jax.random.normal(jax.random.fold_in(_rk, 1), (16, 128, 128), jnp.float32)
        _lenS = 128 - jax.random.randint(jax.random.fold_in(_rk, 7), (16,), 0, max(1, 128 // 4) + 1, jnp.int32)
        _lenS2 = 128 - jax.random.randint(jax.random.fold_in(_rk, 8), (16,), 0, max(1, 128 // 4) + 1, jnp.int32)
        _ctx_1024P = jax.random.normal(jax.random.fold_in(_rk, 11), (16, 16, 128), jnp.float32)
        _ctx_1024c = jax.random.dirichlet(jax.random.fold_in(_rk, 511), 0.3 * jnp.ones((16,), jnp.float32), (16, 128))
        _ctx_1024t = jnp.einsum('bsk,bkd->bsd', _ctx_1024c, _ctx_1024P)
        _ctx_1024t = _ctx_1024t * jax.lax.rsqrt(jnp.mean(jnp.square(_ctx_1024t)) + 1e-12) * 0.953939
        ctx_1024 = -1.39393e-06 + 0.999914 * (_ctx_1024t + 0.3 * jax.random.normal(jax.random.fold_in(_rk, 611), (16, 128, 128), jnp.float32))
        return (x, ctx_1024)
    x, ctx_1024 = _rec_inputs()

    def _L0_xattn_setup():
        import jax, jax.numpy as jnp
        import numpy as np
        HEADS = 16
        EPS = 1e-06

        def _rmsnorm(x, gamma):
            inv = jax.lax.rsqrt(jnp.mean(x * x, axis=-1, keepdims=True) + EPS)
            return x * inv * gamma
        key = jax.random.key(seed)
        ks = jax.random.split(key, 7)
        B, L, Lc, D, CTX = (4, 512, 128, 128, 128)
        hd = D // HEADS
        s = 1.0 / np.sqrt(D)
        return {'x': jax.random.normal(ks[0], (B, L, D), jnp.float32), 'ctx': jax.random.normal(ks[1], (B, Lc, CTX), jnp.float32), 'Wq': jax.random.normal(ks[2], (D, D), jnp.float32) * s, 'Wkv': jax.random.normal(ks[3], (CTX, 2 * D), jnp.float32) * s, 'Wproj': jax.random.normal(ks[4], (D, D), jnp.float32) * s, 'q_gamma': jnp.ones((hd,), jnp.float32), 'k_gamma': jnp.ones((hd,), jnp.float32)}
    _L0_xattn_all = _L0_xattn_setup()
    _L0_xattn_in = {k: v for k, v in _L0_xattn_all.items() if k in ('Wq', 'Wkv', 'Wproj', 'q_gamma', 'k_gamma')}
    del _L0_xattn_all

    def _L0_ffn_setup():
        import jax, jax.numpy as jnp
        import numpy as np
        LN_EPS = 0.001
        EPS = 1e-05
        QB = 128.0

        def ste_round(x):
            return x + jax.lax.stop_gradient(jnp.round(x) - x)
        key = jax.random.key(seed)
        k1, k2 = jax.random.split(key)
        x = jax.random.normal(k1, (4, 1024, 128), dtype=jnp.float32)
        weight = jax.random.normal(k2, (128, 128), dtype=jnp.float32) * 0.02
        ln_gamma = jnp.ones((128,), dtype=jnp.float32)
        ln_beta = jnp.zeros((128,), dtype=jnp.float32)
        return {'x': x, 'weight': weight, 'ln_gamma': ln_gamma, 'ln_beta': ln_beta}
    _L0_ffn_all = _L0_ffn_setup()
    _L0_ffn_in = {k: v for k, v in _L0_ffn_all.items() if k in ('weight', 'ln_gamma', 'ln_beta')}
    del _L0_ffn_all

    def _L1_xattn_setup():
        import jax, jax.numpy as jnp
        import numpy as np
        D_MODEL = 128
        HEADS = 16
        D_HEAD = D_MODEL // HEADS
        SEQ = 256
        C = 2
        K_TOP = int(C * np.log(SEQ))
        key = jax.random.key(seed)
        ks = jax.random.split(key, 5)
        s = 0.02
        return {'Q': jax.random.normal(ks[0], (4, SEQ, D_MODEL), jnp.float32), 'K': jax.random.normal(ks[1], (4, SEQ, D_MODEL), jnp.float32), 'V': jax.random.normal(ks[2], (4, SEQ, D_MODEL), jnp.float32), 'Wq': jax.random.normal(ks[3], (D_MODEL, D_HEAD), jnp.float32) * s, 'bq': jnp.zeros((D_HEAD,), jnp.float32), 'Wout': jax.random.normal(ks[4], (HEADS * D_HEAD, D_MODEL), jnp.float32) * s, 'bout': jnp.zeros((D_MODEL,), jnp.float32)}
    _L1_xattn_all = _L1_xattn_setup()
    _L1_xattn_in = {k: v for k, v in _L1_xattn_all.items() if k in ('Wq', 'bq', 'Wout', 'bout')}
    del _L1_xattn_all

    def _L1_ffn_setup():
        import jax, jax.numpy as jnp
        import numpy as np
        B, S, DIM = (4, 512, 128)
        BASE_COUPLING = 0.1
        NUM_CYCLES = 3

        def _gelu(x):
            return jax.nn.gelu(x, approximate=False)

        def _coupling_net(h, w1, b1, w2, b2, w3, b3, w4, b4):
            h = _gelu(h @ w1 + b1)
            h = _gelu(h @ w2 + b2)
            h = _gelu(h @ w3 + b3)
            return jax.nn.sigmoid(h @ w4 + b4)

        def _global_net(h, w1, b1, w2, b2, w3, b3):
            h = _gelu(h @ w1 + b1)
            h = _gelu(h @ w2 + b2)
            return jax.nn.sigmoid(h @ w3 + b3)

        def _twist(x):
            o_r, o_i, p_r, p_i = jnp.split(x, 4, axis=-1)
            return jnp.concatenate([p_r, -p_i, -o_r, o_i], axis=-1)
        key = jax.random.key(seed)
        ks = jax.random.split(key, 9)
        d = DIM

        def w(k, fan_in, fan_out):
            return jax.random.normal(k, (fan_in, fan_out), dtype=jnp.float32) / np.sqrt(fan_in).astype(np.float32)
        inp = {'x': jax.random.normal(ks[0], (B, S, d), dtype=jnp.float32)}
        cn_dims = [(d, d), (d, d // 2), (d // 2, d // 4), (d // 4, 1)]
        for i, (a, b) in enumerate(cn_dims):
            inp[f'cn_w{i + 1}'] = w(ks[1 + i], a, b)
            inp[f'cn_b{i + 1}'] = jnp.zeros((b,), dtype=jnp.float32)
        gc_dims = [(d, d // 2), (d // 2, d // 4), (d // 4, 1)]
        for i, (a, b) in enumerate(gc_dims):
            inp[f'gc_w{i + 1}'] = w(ks[5 + i], a, b)
            inp[f'gc_b{i + 1}'] = jnp.zeros((b,), dtype=jnp.float32)
        inp['adaptive_range'] = jnp.full((1,), 0.2, dtype=jnp.float32)
        return inp
    _L1_ffn_all = _L1_ffn_setup()
    _L1_ffn_in = {k: v for k, v in _L1_ffn_all.items() if k in ('cn_w1', 'cn_b1', 'cn_w2', 'cn_b2', 'cn_w3', 'cn_b3', 'cn_w4', 'cn_b4', 'gc_w1', 'gc_b1', 'gc_w2', 'gc_b2', 'gc_w3', 'gc_b3', 'adaptive_range')}
    del _L1_ffn_all

    def _L2_xattn_setup():
        import jax, jax.numpy as jnp
        import numpy as np
        D_MODEL = 128
        N_HEADS = 16
        D_K = D_MODEL // N_HEADS
        B, T = (2, 256)
        key = jax.random.key(seed)
        ks = jax.random.split(key, 11)
        s = 1.0 / np.sqrt(D_MODEL)
        return {'q_in': jax.random.normal(ks[0], (B, T, D_MODEL), jnp.float32), 'k_in': jax.random.normal(ks[1], (B, T, D_MODEL), jnp.float32), 'v_in': jax.random.normal(ks[2], (B, T, D_MODEL), jnp.float32), 'Wq': jax.random.normal(ks[3], (D_MODEL, D_MODEL), jnp.float32) * s, 'bq': jnp.zeros((D_MODEL,), jnp.float32), 'Wk': jax.random.normal(ks[4], (D_MODEL, D_MODEL), jnp.float32) * s, 'bk': jnp.zeros((D_MODEL,), jnp.float32), 'Wv': jax.random.normal(ks[5], (D_MODEL, D_MODEL), jnp.float32) * s, 'bv': jnp.zeros((D_MODEL,), jnp.float32), 'Wo': jax.random.normal(ks[6], (D_MODEL, D_MODEL), jnp.float32) * s, 'bo': jnp.zeros((D_MODEL,), jnp.float32)}
    _L2_xattn_all = _L2_xattn_setup()
    _L2_xattn_in = {k: v for k, v in _L2_xattn_all.items() if k in ('Wq', 'bq', 'Wk', 'bk', 'Wv', 'bv', 'Wo', 'bo')}
    del _L2_xattn_all

    def _L2_ffn_setup():
        import jax, jax.numpy as jnp
        import numpy as np
        HIDDEN = 128
        INTER = 512
        N_EXPERTS = 8

        def geglu(x, w1, w2, w3):
            return jax.nn.gelu(x @ w1, approximate=False) * (x @ w2) @ w3
        key = jax.random.key(seed)
        ks = jax.random.split(key, 8)
        s = 0.02
        x = jax.random.normal(ks[0], (2, 256, HIDDEN), dtype=jnp.float32)
        w1s = jax.random.normal(ks[1], (HIDDEN, INTER), dtype=jnp.float32) * s
        w2s = jax.random.normal(ks[2], (HIDDEN, INTER), dtype=jnp.float32) * s
        w3s = jax.random.normal(ks[3], (INTER, HIDDEN), dtype=jnp.float32) * s
        W1 = jax.random.normal(ks[4], (N_EXPERTS, HIDDEN, INTER), dtype=jnp.float32) * s
        W2 = jax.random.normal(ks[5], (N_EXPERTS, HIDDEN, INTER), dtype=jnp.float32) * s
        W3 = jax.random.normal(ks[6], (N_EXPERTS, INTER, HIDDEN), dtype=jnp.float32) * s
        Wg = jax.random.normal(ks[7], (HIDDEN, N_EXPERTS), dtype=jnp.float32) * s
        return {'x': x, 'w1s': w1s, 'w2s': w2s, 'w3s': w3s, 'W1': W1, 'W2': W2, 'W3': W3, 'Wg': Wg}
    _L2_ffn_all = _L2_ffn_setup()
    _L2_ffn_in = {k: v for k, v in _L2_ffn_all.items() if k in ('w1s', 'w2s', 'w3s', 'W1', 'W2', 'W3', 'Wg')}
    del _L2_ffn_all

    def _L3_xattn_setup():
        import jax, jax.numpy as jnp
        import numpy as np
        D_MODEL = 128
        NHEAD = 16
        HEAD_DIM = D_MODEL // NHEAD
        key = jax.random.key(seed)
        ks = jax.random.split(key, 11)
        B, S, D = (4, 256, D_MODEL)
        scale = 1.0 / np.sqrt(D)
        inp = {'q': jax.random.normal(ks[0], (B, S, D), jnp.float32), 'k': jax.random.normal(ks[1], (B, S, D), jnp.float32), 'v': jax.random.normal(ks[2], (B, S, D), jnp.float32), 'Wq': jax.random.normal(ks[3], (D, D), jnp.float32) * scale, 'bq': jnp.zeros((D,), jnp.float32), 'Wk': jax.random.normal(ks[4], (D, D), jnp.float32) * scale, 'bk': jnp.zeros((D,), jnp.float32), 'Wv': jax.random.normal(ks[5], (D, D), jnp.float32) * scale, 'bv': jnp.zeros((D,), jnp.float32), 'Wo': jax.random.normal(ks[6], (D, D), jnp.float32) * scale, 'bo': jnp.zeros((D,), jnp.float32)}
        return inp
    _L3_xattn_all = _L3_xattn_setup()
    _L3_xattn_in = {k: v for k, v in _L3_xattn_all.items() if k in ('Wq', 'bq', 'Wk', 'bk', 'Wv', 'bv', 'Wo', 'bo')}
    del _L3_xattn_all

    def _L3_ffn_setup():
        import jax, jax.numpy as jnp
        import numpy as np
        EPS = 1e-05

        def rmsnorm(x):
            return x * jax.lax.rsqrt(jnp.mean(x * x, axis=-1, keepdims=True) + EPS)

        def act_quant(x):
            scale = 127.0 / jnp.clip(jnp.max(jnp.abs(x), axis=-1, keepdims=True), 1e-05)
            q = jnp.clip(jnp.round(x * scale), -128.0, 127.0) / scale
            return x + jax.lax.stop_gradient(q - x)

        def weight_quant(w):
            scale = 1.0 / jnp.clip(jnp.mean(jnp.abs(w)), 1e-05)
            q = jnp.clip(jnp.round(w * scale), -1.0, 1.0) / scale
            return w + jax.lax.stop_gradient(q - w)

        def bitlinear(x, w, b):
            xq = act_quant(rmsnorm(x))
            wq = weight_quant(w)
            return jnp.einsum('bsd,fd->bsf', xq, wq) + b
        key = jax.random.key(seed)
        k0, k1, k2 = jax.random.split(key, 3)
        B, S, D, F = (2, 1024, 128, 512)
        x = jax.random.normal(k0, (B, S, D), dtype=jnp.float32)
        w1 = jax.random.normal(k1, (F, D), dtype=jnp.float32) * (1.0 / np.sqrt(D))
        b1 = jnp.zeros((F,), dtype=jnp.float32)
        w2 = jax.random.normal(k2, (D, F), dtype=jnp.float32) * (1.0 / np.sqrt(F))
        b2 = jnp.zeros((D,), dtype=jnp.float32)
        return {'x': x, 'w1': w1, 'b1': b1, 'w2': w2, 'b2': b2}
    _L3_ffn_all = _L3_ffn_setup()
    _L3_ffn_in = {k: v for k, v in _L3_ffn_all.items() if k in ('w1', 'b1', 'w2', 'b2')}
    del _L3_ffn_all
    return {'x': x, 'ctx_1024': ctx_1024, 'L0_xattn_Wq': _L0_xattn_in['Wq'], 'L0_xattn_Wkv': _L0_xattn_in['Wkv'], 'L0_xattn_Wproj': _L0_xattn_in['Wproj'], 'L0_xattn_q_gamma': _L0_xattn_in['q_gamma'], 'L0_xattn_k_gamma': _L0_xattn_in['k_gamma'], 'L0_ffn_weight': _L0_ffn_in['weight'], 'L0_ffn_ln_gamma': _L0_ffn_in['ln_gamma'], 'L0_ffn_ln_beta': _L0_ffn_in['ln_beta'], 'L1_xattn_Wq': _L1_xattn_in['Wq'], 'L1_xattn_bq': _L1_xattn_in['bq'], 'L1_xattn_Wout': _L1_xattn_in['Wout'], 'L1_xattn_bout': _L1_xattn_in['bout'], 'L1_ffn_cn_w1': _L1_ffn_in['cn_w1'], 'L1_ffn_cn_b1': _L1_ffn_in['cn_b1'], 'L1_ffn_cn_w2': _L1_ffn_in['cn_w2'], 'L1_ffn_cn_b2': _L1_ffn_in['cn_b2'], 'L1_ffn_cn_w3': _L1_ffn_in['cn_w3'], 'L1_ffn_cn_b3': _L1_ffn_in['cn_b3'], 'L1_ffn_cn_w4': _L1_ffn_in['cn_w4'], 'L1_ffn_cn_b4': _L1_ffn_in['cn_b4'], 'L1_ffn_gc_w1': _L1_ffn_in['gc_w1'], 'L1_ffn_gc_b1': _L1_ffn_in['gc_b1'], 'L1_ffn_gc_w2': _L1_ffn_in['gc_w2'], 'L1_ffn_gc_b2': _L1_ffn_in['gc_b2'], 'L1_ffn_gc_w3': _L1_ffn_in['gc_w3'], 'L1_ffn_gc_b3': _L1_ffn_in['gc_b3'], 'L1_ffn_adaptive_range': _L1_ffn_in['adaptive_range'], 'L2_xattn_Wq': _L2_xattn_in['Wq'], 'L2_xattn_bq': _L2_xattn_in['bq'], 'L2_xattn_Wk': _L2_xattn_in['Wk'], 'L2_xattn_bk': _L2_xattn_in['bk'], 'L2_xattn_Wv': _L2_xattn_in['Wv'], 'L2_xattn_bv': _L2_xattn_in['bv'], 'L2_xattn_Wo': _L2_xattn_in['Wo'], 'L2_xattn_bo': _L2_xattn_in['bo'], 'L2_ffn_w1s': _L2_ffn_in['w1s'], 'L2_ffn_w2s': _L2_ffn_in['w2s'], 'L2_ffn_w3s': _L2_ffn_in['w3s'], 'L2_ffn_W1': _L2_ffn_in['W1'], 'L2_ffn_W2': _L2_ffn_in['W2'], 'L2_ffn_W3': _L2_ffn_in['W3'], 'L2_ffn_Wg': _L2_ffn_in['Wg'], 'L3_xattn_Wq': _L3_xattn_in['Wq'], 'L3_xattn_bq': _L3_xattn_in['bq'], 'L3_xattn_Wk': _L3_xattn_in['Wk'], 'L3_xattn_bk': _L3_xattn_in['bk'], 'L3_xattn_Wv': _L3_xattn_in['Wv'], 'L3_xattn_bv': _L3_xattn_in['bv'], 'L3_xattn_Wo': _L3_xattn_in['Wo'], 'L3_xattn_bo': _L3_xattn_in['bo'], 'L3_ffn_w1': _L3_ffn_in['w1'], 'L3_ffn_b1': _L3_ffn_in['b1'], 'L3_ffn_w2': _L3_ffn_in['w2'], 'L3_ffn_b2': _L3_ffn_in['b2']}

def reference(x, ctx_1024, L0_xattn_Wq, L0_xattn_Wkv, L0_xattn_Wproj, L0_xattn_q_gamma, L0_xattn_k_gamma, L0_ffn_weight, L0_ffn_ln_gamma, L0_ffn_ln_beta, L1_xattn_Wq, L1_xattn_bq, L1_xattn_Wout, L1_xattn_bout, L1_ffn_cn_w1, L1_ffn_cn_b1, L1_ffn_cn_w2, L1_ffn_cn_b2, L1_ffn_cn_w3, L1_ffn_cn_b3, L1_ffn_cn_w4, L1_ffn_cn_b4, L1_ffn_gc_w1, L1_ffn_gc_b1, L1_ffn_gc_w2, L1_ffn_gc_b2, L1_ffn_gc_w3, L1_ffn_gc_b3, L1_ffn_adaptive_range, L2_xattn_Wq, L2_xattn_bq, L2_xattn_Wk, L2_xattn_bk, L2_xattn_Wv, L2_xattn_bv, L2_xattn_Wo, L2_xattn_bo, L2_ffn_w1s, L2_ffn_w2s, L2_ffn_w3s, L2_ffn_W1, L2_ffn_W2, L2_ffn_W3, L2_ffn_Wg, L3_xattn_Wq, L3_xattn_bq, L3_xattn_Wk, L3_xattn_bk, L3_xattn_Wv, L3_xattn_bv, L3_xattn_Wo, L3_xattn_bo, L3_ffn_w1, L3_ffn_b1, L3_ffn_w2, L3_ffn_b2):
    import jax
    import jax.numpy as jnp

    def _L0_xattn_ref(x, ctx, Wq, Wkv, Wproj, q_gamma, k_gamma):
        import jax, jax.numpy as jnp
        import numpy as np
        HEADS = 16
        EPS = 1e-06

        def _rmsnorm(x, gamma):
            inv = jax.lax.rsqrt(jnp.mean(x * x, axis=-1, keepdims=True) + EPS)
            return x * inv * gamma
        B, L, D = x.shape
        Lc = ctx.shape[1]
        H = HEADS
        hd = D // H
        q = (x @ Wq).reshape(B, L, H, hd).transpose(0, 2, 1, 3)
        kv = (ctx @ Wkv).reshape(B, Lc, 2, H, hd).transpose(2, 0, 3, 1, 4)
        k, v = (kv[0], kv[1])
        q = _rmsnorm(q, q_gamma)
        k = _rmsnorm(k, k_gamma)
        scale = 1.0 / np.sqrt(hd)
        attn = jnp.einsum('bhld,bhmd->bhlm', q, k) * scale
        attn = jax.nn.softmax(attn, axis=-1)
        out = jnp.einsum('bhlm,bhmd->bhld', attn, v)
        out = out.transpose(0, 2, 1, 3).reshape(B, L, D)
        return out @ Wproj

    def _L0_ffn_ref(x, weight, ln_gamma, ln_beta):
        import jax, jax.numpy as jnp
        import numpy as np
        LN_EPS = 0.001
        EPS = 1e-05
        QB = 128.0

        def ste_round(x):
            return x + jax.lax.stop_gradient(jnp.round(x) - x)
        mu = jnp.mean(x, axis=-1, keepdims=True)
        var = jnp.var(x, axis=-1, keepdims=True)
        xn = (x - mu) * jax.lax.rsqrt(var + LN_EPS) * ln_gamma + ln_beta
        beta = jnp.mean(jnp.abs(weight))
        w_q = jnp.clip(ste_round(weight / (beta + EPS)), -1.0, 1.0)
        gamma = jnp.max(jnp.abs(xn))
        xq = jnp.clip(xn * QB / gamma, -QB + EPS, QB - EPS)
        y = jnp.einsum('bsd,du->bsu', xq, w_q)
        return y * (gamma * beta / QB)

    def _L1_xattn_ref(Q, K, V, Wq, bq, Wout, bout):
        import jax, jax.numpy as jnp
        import numpy as np
        D_MODEL = 128
        HEADS = 16
        D_HEAD = D_MODEL // HEADS
        SEQ = 256
        C = 2
        K_TOP = int(C * np.log(SEQ))
        B, L, _ = Q.shape
        q = (Q @ Wq + bq).transpose(0, 2, 1)
        k_ = (K @ Wq + bq).transpose(0, 2, 1)
        v = (V @ Wq + bq).transpose(0, 2, 1)
        Qf = jnp.fft.fft(q.astype(jnp.complex64))
        Kf = jnp.fft.fft(k_.astype(jnp.complex64))
        corr = jnp.real(jnp.fft.ifft(Qf * jnp.conj(Kf)))
        corr = corr.mean(axis=(0, 1))
        W_topk, I_topk = jax.lax.top_k(corr, K_TOP)
        W_topk = jax.nn.softmax(W_topk)

        def body(R, ws):
            w, shift = ws
            return (R + w * jnp.roll(v, -shift, axis=-1), None)
        R3, _ = jax.lax.scan(body, jnp.zeros_like(v), (W_topk, I_topk))
        R = jnp.broadcast_to(R3[:, None], (B, HEADS, D_HEAD, L)).reshape(B, L, HEADS * D_HEAD)
        return R @ Wout + bout

    def _L1_ffn_ref(x, cn_w1, cn_b1, cn_w2, cn_b2, cn_w3, cn_b3, cn_w4, cn_b4, gc_w1, gc_b1, gc_w2, gc_b2, gc_w3, gc_b3, adaptive_range):
        import jax, jax.numpy as jnp
        import numpy as np
        B, S, DIM = (4, 512, 128)
        BASE_COUPLING = 0.1
        NUM_CYCLES = 3

        def _gelu(x):
            return jax.nn.gelu(x, approximate=False)

        def _coupling_net(h, w1, b1, w2, b2, w3, b3, w4, b4):
            h = _gelu(h @ w1 + b1)
            h = _gelu(h @ w2 + b2)
            h = _gelu(h @ w3 + b3)
            return jax.nn.sigmoid(h @ w4 + b4)

        def _global_net(h, w1, b1, w2, b2, w3, b3):
            h = _gelu(h @ w1 + b1)
            h = _gelu(h @ w2 + b2)
            return jax.nn.sigmoid(h @ w3 + b3)

        def _twist(x):
            o_r, o_i, p_r, p_i = jnp.split(x, 4, axis=-1)
            return jnp.concatenate([p_r, -p_i, -o_r, o_i], axis=-1)
        global_context = x.mean(axis=1, keepdims=True)
        gf = _global_net(global_context, gc_w1, gc_b1, gc_w2, gc_b2, gc_w3, gc_b3)
        out = x
        for _ in range(NUM_CYCLES):
            tf = _coupling_net(out, cn_w1, cn_b1, cn_w2, cn_b2, cn_w3, cn_b3, cn_w4, cn_b4)
            combined = 0.7 * gf + 0.3 * tf
            coupling = BASE_COUPLING + adaptive_range * (combined - 0.5) * 2.0
            out = out + coupling * _twist(out)
        return out

    def _L2_xattn_ref(q_in, k_in, v_in, Wq, bq, Wk, bk, Wv, bv, Wo, bo):
        import jax, jax.numpy as jnp
        import numpy as np
        D_MODEL = 128
        N_HEADS = 16
        D_K = D_MODEL // N_HEADS
        B, T = (2, 256)
        Bq, Tq, C = q_in.shape
        q = q_in @ Wq + bq
        k = k_in @ Wk + bk
        v = v_in @ Wv + bv
        q = q.reshape(Bq, Tq, N_HEADS, D_K)
        k = k.reshape(Bq, -1, N_HEADS, D_K)
        v = v.reshape(Bq, -1, N_HEADS, D_K)
        scale = 1.0 / np.sqrt(D_K).astype(np.float32)
        attn = jnp.einsum('bqhd,bkhd->bhqk', q, k) * scale
        attn = jax.nn.softmax(attn, axis=-1)
        out = jnp.einsum('bhqk,bkhd->bqhd', attn, v).reshape(Bq, Tq, C)
        return out @ Wo + bo

    def _L2_ffn_ref(x, w1s, w2s, w3s, W1, W2, W3, Wg):
        import jax, jax.numpy as jnp
        import numpy as np
        HIDDEN = 128
        INTER = 512
        N_EXPERTS = 8

        def geglu(x, w1, w2, w3):
            return jax.nn.gelu(x @ w1, approximate=False) * (x @ w2) @ w3
        B, T, C = x.shape
        xf = x.reshape(-1, C)
        shared = geglu(xf, w1s, w2s, w3s)
        logits = xf @ Wg
        idx = jnp.argmax(logits, axis=-1)
        final = jnp.zeros_like(xf)
        for e in range(N_EXPERTS):
            y = geglu(xf, W1[e], W2[e], W3[e])
            final = final + jnp.where((idx == e)[:, None], y, 0.0)
        return (shared + final).reshape(B, T, C)

    def _L3_xattn_ref(q, k, v, Wq, bq, Wk, bk, Wv, bv, Wo, bo):
        import jax, jax.numpy as jnp
        import numpy as np
        D_MODEL = 128
        NHEAD = 16
        HEAD_DIM = D_MODEL // NHEAD
        B, S, D = q.shape
        H, Hd = (NHEAD, HEAD_DIM)
        qh = (q @ Wq.T + bq).reshape(B, S, H, Hd).transpose(0, 2, 1, 3)
        kh = (k @ Wk.T + bk).reshape(B, S, H, Hd).transpose(0, 2, 1, 3)
        vh = (v @ Wv.T + bv).reshape(B, S, H, Hd).transpose(0, 2, 1, 3)
        scores = jnp.einsum('bhqd,bhkd->bhqk', qh, kh) / jnp.sqrt(jnp.float32(Hd))
        attn = jax.nn.softmax(scores, axis=-1)
        out = jnp.einsum('bhqk,bhkd->bhqd', attn, vh)
        out = out.transpose(0, 2, 1, 3).reshape(B, S, D)
        return out @ Wo.T + bo

    def _L3_ffn_ref(x, w1, b1, w2, b2):
        import jax, jax.numpy as jnp
        import numpy as np
        EPS = 1e-05

        def rmsnorm(x):
            return x * jax.lax.rsqrt(jnp.mean(x * x, axis=-1, keepdims=True) + EPS)

        def act_quant(x):
            scale = 127.0 / jnp.clip(jnp.max(jnp.abs(x), axis=-1, keepdims=True), 1e-05)
            q = jnp.clip(jnp.round(x * scale), -128.0, 127.0) / scale
            return x + jax.lax.stop_gradient(q - x)

        def weight_quant(w):
            scale = 1.0 / jnp.clip(jnp.mean(jnp.abs(w)), 1e-05)
            q = jnp.clip(jnp.round(w * scale), -1.0, 1.0) / scale
            return w + jax.lax.stop_gradient(q - w)

        def bitlinear(x, w, b):
            xq = act_quant(rmsnorm(x))
            wq = weight_quant(w)
            return jnp.einsum('bsd,fd->bsf', xq, wq) + b
        h = bitlinear(x, w1, b1)
        h = jax.nn.gelu(h, approximate=False)
        return bitlinear(h, w2, b2)
    x = x + _L0_xattn_ref(_layernorm(x, axis=-1), ctx_1024, L0_xattn_Wq, L0_xattn_Wkv, L0_xattn_Wproj, L0_xattn_q_gamma, L0_xattn_k_gamma)
    x = x + _L0_ffn_ref(_layernorm(x, axis=-1), L0_ffn_weight, L0_ffn_ln_gamma, L0_ffn_ln_beta)
    x = x + _L1_xattn_ref(_layernorm(x, axis=-1), ctx_1024, ctx_1024, L1_xattn_Wq, L1_xattn_bq, L1_xattn_Wout, L1_xattn_bout)
    x = x + _L1_ffn_ref(_layernorm(x, axis=-1), L1_ffn_cn_w1, L1_ffn_cn_b1, L1_ffn_cn_w2, L1_ffn_cn_b2, L1_ffn_cn_w3, L1_ffn_cn_b3, L1_ffn_cn_w4, L1_ffn_cn_b4, L1_ffn_gc_w1, L1_ffn_gc_b1, L1_ffn_gc_w2, L1_ffn_gc_b2, L1_ffn_gc_w3, L1_ffn_gc_b3, L1_ffn_adaptive_range)
    x = x + _L2_xattn_ref(_layernorm(x, axis=-1), ctx_1024, ctx_1024, L2_xattn_Wq, L2_xattn_bq, L2_xattn_Wk, L2_xattn_bk, L2_xattn_Wv, L2_xattn_bv, L2_xattn_Wo, L2_xattn_bo)
    x = x + _L2_ffn_ref(_layernorm(x, axis=-1), L2_ffn_w1s, L2_ffn_w2s, L2_ffn_w3s, L2_ffn_W1, L2_ffn_W2, L2_ffn_W3, L2_ffn_Wg)
    x = x + _L3_xattn_ref(_layernorm(x, axis=-1), ctx_1024, ctx_1024, L3_xattn_Wq, L3_xattn_bq, L3_xattn_Wk, L3_xattn_bk, L3_xattn_Wv, L3_xattn_bv, L3_xattn_Wo, L3_xattn_bo)
    x = x + _L3_ffn_ref(_layernorm(x, axis=-1), L3_ffn_w1, L3_ffn_b1, L3_ffn_w2, L3_ffn_b2)
    return x

_drawn_inputs = setup_inputs


def setup_inputs(seed=0):
    import zlib

    import numpy as np

    out = dict(_drawn_inputs(seed))
    spreads = {'L0_xattn_q_gamma': (1.0, 0.2),
     'L0_xattn_k_gamma': (1.0, 0.2),
     'L0_ffn_ln_gamma': (1.0, 0.584),
     'L0_ffn_ln_beta': (0.0, 0.577),
     'L1_xattn_bq': (0.0, 0.647),
     'L1_xattn_bout': (0.0, 0.1),
     'L1_ffn_cn_b1': (0.0, 0.8),
     'L1_ffn_cn_b2': (0.0, 0.8),
     'L1_ffn_cn_b3': (0.0, 2.0),
     'L1_ffn_gc_b1': (0.0, 0.8),
     'L1_ffn_gc_b2': (0.0, 0.72),
     'L2_xattn_bq': (0.0, 0.701),
     'L2_xattn_bk': (0.0, 2.0),
     'L2_xattn_bv': (0.0, 0.1),
     'L2_xattn_bo': (0.0, 0.1),
     'L3_xattn_bq': (0.0, 2.0),
     'L3_xattn_bk': (0.0, 2.0),
     'L3_xattn_bv': (0.0, 0.8),
     'L3_xattn_bo': (0.0, 0.8),
     'L3_ffn_b1': (0.0, 0.8),
     'L3_ffn_b2': (0.0, 0.8)}
    factors = {'L1_ffn_cn_w1': 7.576,
     'L1_ffn_cn_w2': 5.829,
     'L1_ffn_cn_w3': 6.202,
     'L1_ffn_cn_w4': 5.92,
     'L1_ffn_gc_w1': 5.151,
     'L1_ffn_gc_w2': 3.386,
     'L1_ffn_gc_w3': 3.304,
     'L2_ffn_w1s': 8.0,
     'L2_ffn_w2s': 8.0,
     'L2_ffn_w3s': 8.0,
     'L2_ffn_W1': 8.0,
     'L2_ffn_W2': 8.0,
     'L2_ffn_W3': 8.0,
     'L2_ffn_Wg': 8.0,
     'L3_xattn_Wq': 2.809}
    for name, (base, spread) in spreads.items():
        noise = np.random.default_rng([zlib.crc32(name.encode()), seed]).standard_normal(out[name].shape)
        drawn = base * np.exp(spread * noise) if base else spread * noise
        out[name] = jnp.asarray(drawn.astype(out[name].dtype))
    for name, factor in factors.items():
        out[name] = (out[name] * factor).astype(out[name].dtype)
    return out
```

```python
from contextlib import ExitStack

import numpy as np

import concourse.bass as bass
from concourse import mybir

ALU = mybir.AluOpType
ACT = mybir.ActivationFunctionType
AX = mybir.AxisListType
F32 = mybir.dt.float32
BF16 = mybir.dt.bfloat16
I32 = mybir.dt.int32
U32 = mybir.dt.uint32

P = 128
B = 16
H, HD = 16, 8
CB = 4
NC = B // CB
CW = CB * P
GH = 4
NG = H // GH
VW = HD + 1
NE = 8
FF = 512
FK = FF // P
NX = B + NE - 1
NT = B + NX
EPS = 1e-5
NS = 4
LEAD = 16


def upd(st, b):
    return B * st + b


def past(n):
    return n + 1 + LEAD


def past_dma(n, dmas=1):
    return 16 * dmas * (n + 1 + LEAD)


def slots(g):
    return [(g % 2, GH * (g // 2) + j) for j in range(GH)]


class Chain:

    def __init__(self, eng, sem):
        self.eng, self.sem, self.done = eng, sem, 0
        self.it, self.per, self.at = None, 0, 0

    def step(self, ins):
        ins.then_inc(self.sem, 1)
        self.at += 1
        self.eng.wait_ge(self.sem, self.count())

    def count(self):
        if self.it is None:
            return self.done + self.at
        return self.it * self.per + (self.done + self.at)

    def loop(self, it, per):
        self.done += self.at
        self.it, self.per, self.at = it, per, 0

    def end(self, turns):
        assert self.at == self.per, (self.at, self.per)
        self.done += turns * self.per
        self.it, self.at = None, 0


def make_constants():
    c = {}
    eye = np.eye(P, dtype=np.float32)
    p = np.arange(P)
    c["ident"] = eye
    half, d, place = p // 64, (p % 64) // 8, p % 8
    head = 2 * place + half
    c["headmean"] = (head[:, None] == head[None, :]).astype(np.float32) / HD
    perm = np.zeros((P, P), np.float32)
    perm[head * HD + d, p] = 1.0
    c["perm"] = perm
    c["spread_d"] = np.zeros((P, P), np.float32)
    c["spread_d"][d, p] = 1.0
    sel = np.zeros((P, 8, P), np.float32)
    for h in range(2):
        for part in range(2):
            for k in range(8):
                sel[64 * h + 8 * part + k, k, :] = 1.0
    c["sel"] = sel.reshape(P, 8 * P)
    lag = (-p) % P
    c["tie"] = (lag[:, None] < lag[None, :]).astype(np.float32)
    c["mod8"] = (p[:, None] % HD == p[None, :] % HD).astype(np.float32)
    c["own_batch"] = (p[:, None] // HD == np.arange(B)[None, :]).astype(np.float32)
    tw = np.zeros((P, P), np.float32)
    for to, fr, s in ((0, 2, 1), (1, 3, -1), (2, 0, -1), (3, 1, 1)):
        for k in range(32):
            tw[32 * fr + k, 32 * to + k] = s
    c["twist"] = tw
    c["before"] = (p[:, None] < p[None, :]).astype(np.float32)
    c["first"] = np.broadcast_to(NE - np.arange(NE, dtype=np.float32), (P, NE))
    c["tile_rows"] = np.broadcast_to(P * np.arange(B, dtype=np.float32), (P, B))
    c["tile_no"] = np.broadcast_to(np.arange(NX, dtype=np.float32), (P, NX))
    return c


CONSTS = make_constants()
CORDER = list(CONSTS)
CWIDTH = [CONSTS[k].shape[1] for k in CORDER]

ATT = {0: "L0_xattn", 1: "L2_xattn", 2: "L3_xattn"}
ST_ATT = (0, 4, 6)
ST_FFN0, ST_CORR, ST_TWIST, ST_MOE, ST_BIT = 1, 2, 3, 5, 7
K_TOP = int(2 * np.log(256))
CYCLES = 3
MAGIC = 12582912.0


def norm(st):
    return st if st <= ST_FFN0 else st + 1


def once(*names):
    return {name: i + 1 for i, name in enumerate(names)}


PE1 = once("wmean0", "amaxT", "amax", "qkT", "corrM", "corr", "rank", "rolled", "rolled_out",
           "g1", "g2", "g3", "bit_mean", "bit_wT", "prefix")
DVE1 = once("wabs0", "amax_col", "amax_row", "ternary0", "corr_in", "corr_T", "corr_mm", "corr_negmax",
            "corr_G", "corr_w", "rolled_sb", "gmean", "t_bias", "bit_abs", "bit_tern", "onehot", "prefix_read", "route")
ACT1 = once("corr_exp", "g1", "g2", "g3")


def build_program(nc, I, out):
    with ExitStack() as ctx:
        def sb(name, shape, dt=F32):
            return ctx.enter_context(nc.sbuf_tensor(name, shape, dt))

        def sem(name):
            return ctx.enter_context(nc.semaphore(name))

        def dram(name, shape, dt=F32):
            return nc.dram_tensor(name, shape, dt, kind="Internal").ap()

        bank = [ctx.enter_context(nc.psum_tensor(f"bank{i}", [P, 512], F32)) for i in range(8)]
        x_sb = sb("x_sb", [P, B, P])
        cst = sb("cst", [P, sum(CWIDTH)])
        C = {}
        at = 0
        for k, w in zip(CORDER, CWIDTH):
            C[k] = cst[:, at:at + w]
            at += w
        ident = C["ident"]
        identb = sb("identb", [P, P], BF16)
        selb = sb("selb", [P, 8, P], BF16)
        ones_row = sb("ones_row", [P, P])
        neg_half = sb("neg_half", [P, B])
        eps6 = sb("eps6", [P, 1])

        stats = sb("stats", [P, 6])
        mv = sb("mv", [P, B, 2])
        mvnew = sb("mvnew", [P, 2])
        xnew = sb("xnew", [P, P])
        vareps = sb("vareps", [P, B])
        rstd = sb("rstd", [P, B])
        xn = sb("xn", [P, 2, CB, P])
        xT = sb("xT", [P, 2, CW])

        ctx_in = sb("ctx_in", [P, 2, CB, P])
        wraw = sb("wraw", [P, 12, P])
        wq = sb("wq", [P, 3, P])
        wk = sb("wk", [P, 3, P])
        wvo3 = sb("wvo3", [P, 2, P])
        colraw = sb("colraw", [P, 8])
        colbias = sb("colbias", [P, 8])
        bvrow = sb("bvrow", [P, 3, P])
        borow = sb("borow", [P, 3, P])

        sq = sb("sq", [P, CW])
        rms = sb("rms", [P, CW])
        resid = sb("resid", [P, 2, CW])
        parts = sb("parts", [P, 2, 3, CW], BF16)
        v_out = sb("v_out", [P, 2, CB, H, VW])

        qstk = sb("qstk", [P, NS, 8, P], BF16)
        kstk = sb("kstk", [P, NS, 8, P], BF16)
        v_in = sb("v_in", [P, NS, H, VW])
        negm = sb("negm", [P, 2, 2, 8])
        mpad = sb("mpad", [P, 2, P], BF16)
        mT = sb("mT", [P, 2, P], BF16)
        probs = sb("probs", [P, NG, GH * P])
        rden = sb("rden", [P, H])
        att = sb("att", [P, 2, P])
        attT = sb("attT", [P, 2, P])

        xall = sb("xall", [P, B, P])
        rs1 = sb("rs1", [P, B])
        lnrow = sb("lnrow", [P, 2, P])
        w_f0 = sb("w_f0", [P, P])
        w_t0 = sb("w_t0", [P, 2, P])
        amax = sb("amax", [P, NC])
        sc = sb("sc", [P, 16])
        ones_sq = sb("ones_sq", [P, P])
        mean_sq = sb("mean_sq", [P, P])
        w_c = sb("w_c", [P, HD])
        bq_c = sb("bq_c", [P, HD])
        wout_c = sb("wout_c", [P, P])
        bout_c = sb("bout_c", [P, P])
        q1 = sb("q1", [P, P])
        k1 = sb("k1", [P, P])
        qk1T = sb("qk1T", [P, 2, P])
        mm2 = sb("mm2", [P, 2, P])
        skew = sb("skew", [P, P])
        crow = sb("crow", [P, P])
        cwork = sb("cwork", [P, 3, P])
        rolled = sb("rolled", [P, P])
        ymask = sb("ymask", [P, 2, CB, P])
        w_cn = sb("w_cn", [P, P + 64 + 32 + P])
        w_gc = sb("w_gc", [P, 64 + 32 + P])
        b_l1 = sb("b_l1", [P, 8])
        w4c = sb("w4c", [32, 2])
        tbuf = sb("tbuf", [P, 4, CW])
        h1, tf = tbuf[:, 0:2], tbuf[:, 2:4]
        h2 = sb("h2", [64, 2, CW])
        h3 = ctx_in[0:32].rearrange("p u b d -> p u (b d)")
        tws = sb("tws", [P, 2, CW])
        gx = sb("gx", [P, 4, B])
        acoef = sb("acoef", [P, B])
        wmoe = sb("wmoe", [P, NE + 1, 3 * FF])
        w_g = sb("w_g", [P, NE])
        rt = sb("rt", [P, 8, B, NE])
        rs = sb("rs", [P, 6, B])
        rx = sb("rx", [P, NX * NE])
        etab = sb("etab", [P, NX], I32)
        pos = sb("pos", [P, B], U32)
        xr = sb("xr", [P, 2, P])
        xs = sb("xs", [P, 2, P])
        gl = tws
        gT = ymask[:].rearrange("p u b d -> p u (b d)")
        yo = sb("yo", [P, 2, P])
        yshared = tbuf[:].rearrange("p k (b d) -> p (k b) d", d=P)
        rows_dram = dram("rows_dram", [NT, P, P])
        y_dram = dram("y_dram", [NT * P, P])
        wb = sb("wb", [P, 2, FF])
        wbt = sb("wbt", [P, 2, FF], BF16)
        w1T = sb("w1T", [P, FF], BF16)
        w2T = sb("w2T", [P, FF], BF16)
        b1row = sb("b1row", [P, FF])
        b2row = sb("b2row", [P, P])
        bsc = sb("bsc", [P, 8])
        bq = sb("bq", [P, 2, 8, CB])
        free = wmoe[:].rearrange("p e w -> p (e w)")
        hg = free[:, 0:2 * CB * FF].rearrange("p (u k f) -> p u k f", u=2, k=CB)
        free = free[:, 2 * CB * FF:].bitcast(BF16)
        xq = free[:, 0:2 * CW].rearrange("p (u k d) -> p u k d", u=2, k=CB)
        xqT, hq, hqT = (free[:, k * 2 * CW:(k + 1) * 2 * CW].rearrange("p (u n) -> p u n", u=2) for k in (1, 2, 3))

        corr_dram = dram("corr_dram", [P, 2 * P])
        wlag_dram = dram("wlag_dram", [P, P])

        q_dram = [dram(f"q_stacks{l}", [NC, 2, 6, CB, HD * 8, P], BF16) for l in range(3)]
        k_dram = [dram(f"k_stacks{l}", [NC, 2, 6, CB, HD * 8, P], BF16) for l in range(3)]
        v_dram = [dram(f"v_rows{l}", [B, P, H * VW]) for l in range(3)]

        s_cst, s_x, s_w = sem("s_cst"), sem("s_x"), sem("s_w")
        s_ctx = [sem("s_ctx_even"), sem("s_ctx_odd")]
        s_const = sem("s_const")
        s_wt = sem("s_wt")
        s_wprep = sem("s_wprep")
        s_lead = []

        def item(name, per=1):
            s = sem(name)
            s_lead.append((s, per))
            return s

        s_var, s_rstd = item("s_var"), item("s_rstd")
        s_xn, s_tr, s_xT = item("s_xn"), item("s_tr"), item("s_xT")
        s_proj, s_hi, s_r1, s_mid, s_lo = item("s_proj"), item("s_hi"), item("s_r1"), item("s_mid"), item("s_lo")
        s_sq, s_ms, s_mse, s_inv, s_rms = item("s_sq"), item("s_ms"), item("s_mse"), item("s_inv"), item("s_rms")
        s_stored = [item("s_stored_even", 16 * 6), item("s_stored_odd", 16 * 6)]
        s_vp, s_vb = item("s_vp"), item("s_vb")
        s_vst = [item("s_vst_even", 16), item("s_vst_odd", 16)]
        s_stk = [item(f"s_stk{k}", 16 * 5) for k in range(NS)]
        s_sc, s_max, s_mparts, s_mtp, s_mt = item("s_sc"), item("s_max"), item("s_mparts"), item("s_mtp"), item("s_mt")
        s_st, s_exp, s_av, s_norm = item("s_st"), item("s_exp"), item("s_av"), item("s_norm")
        s_atp, s_atc, s_y, s_xup = item("s_atp"), item("s_atc"), item("s_y"), item("s_xup")
        s_done = sem("s_done")
        s_out = sem("s_out")
        s_rp = item("s_rp")
        s_k1p, s_k1 = item("s_k1p"), item("s_k1")
        s_pe1, s_dve1, s_act1 = sem("s_pe1"), sem("s_dve1"), sem("s_act1")
        s_skew = sem("s_skew")
        s_w5, s_w7, s_zero = sem("s_w5"), sem("s_w7"), sem("s_zero")
        s_rows, s_scat, s_gath, s_ysh = sem("s_rows"), sem("s_scat"), sem("s_gath"), sem("s_ysh")
        s_rl = [item("s_rl_even", 16), item("s_rl_odd", 16)]
        s_xtp, s_xs, s_h, s_gl, s_g, s_gtp, s_gt, s_o, s_yo = (
            item(f"s_moe_{k}") for k in ("xtp", "xs", "h", "gl", "g", "gtp", "gt", "o", "yo"))
        s_yst = [item("s_yst_even", 16), item("s_yst_odd", 16)]
        s_lg = item("s_lg")
        s_bh, s_bb, s_bg, s_bsq, s_bms, s_bpw, s_bq, s_bqb, s_btp, s_bt, s_bo, s_bx = (
            item(f"s_bit_{k}") for k in ("h", "b", "g", "sq", "ms", "pw", "q", "qb", "tp", "t", "o", "x"))
        s_w1 = sem("s_w1")
        s_c1, s_g1, s_c2, s_g2, s_c3, s_g3, s_c4, s_g4, s_cyc, s_twp, s_tws = (
            item(f"s_tw_{k}") for k in ("p1", "g1", "p2", "g2", "p3", "g3", "p4", "g4", "cyc", "twp", "tws"))
        s_dve = sem("s_dve")
        s_sp = sem("s_sp")

        block = ctx.enter_context(nc.Block())

        loads = []

        xcols = xall[:].rearrange("p b t -> p (b t)")
        CN = {1: w_cn[:, 0:P], 2: w_cn[:, P:P + 64], 3: w_cn[0:64, P + 64:P + 96], 4: w_cn[0:32, P + 96:2 * P + 96]}
        GC = {1: w_gc[:, 0:64], 2: w_gc[0:64, 64:96], 3: w_gc[0:32, 96:96 + P]}

        def col(name):
            return I[name].rearrange("(p a) -> p a", a=1)

        def row(name):
            return I[name].rearrange("(a n) -> a n", a=1)

        wsrc = [I["L0_xattn_Wq"], I["L0_xattn_Wkv"][:, 0:P], I["L0_xattn_Wkv"][:, P:2 * P], I["L0_xattn_Wproj"]]
        for l in (1, 2):
            wsrc += [I[f"{ATT[l]}_{w}"] for w in ("Wq", "Wk", "Wv", "Wo")]
        for i, s in enumerate(wsrc):
            loads.append((wraw[:, i, :], s))
        loads += [(colraw[0:HD, 0:1], col("L0_xattn_q_gamma")), (colraw[0:HD, 1:2], col("L0_xattn_k_gamma"))]
        for l in (1, 2):
            loads += [(colraw[:, 2 * l:2 * l + 1], col(f"{ATT[l]}_bq")),
                      (colraw[:, 2 * l + 1:2 * l + 2], col(f"{ATT[l]}_bk")),
                      (bvrow[:, l, :], row(f"{ATT[l]}_bv").broadcast_to([P, P])),
                      (borow[0:1, l, :], row(f"{ATT[l]}_bo"))]

        f0 = [(w_f0[:], I["L0_ffn_weight"]),
              (lnrow[:, 0, :], row("L0_ffn_ln_gamma").broadcast_to([P, P])),
              (lnrow[:, 1, :], row("L0_ffn_ln_beta").broadcast_to([P, P])),
              (w_c[:], I["L1_xattn_Wq"]), (bq_c[:], row("L1_xattn_bq").broadcast_to([P, HD])),
              (wout_c[:], I["L1_xattn_Wout"]), (bout_c[:], row("L1_xattn_bout").broadcast_to([P, P]))]
        loads += f0
        loads1 = [(CN[1], I["L1_ffn_cn_w1"]), (CN[2], I["L1_ffn_cn_w2"]), (CN[3], I["L1_ffn_cn_w3"]),
                  (w4c[:, 0:1], I["L1_ffn_cn_w4"]), (w4c[:, 1:2], I["L1_ffn_gc_w3"]),
                  (GC[1], I["L1_ffn_gc_w1"]), (GC[2], I["L1_ffn_gc_w2"]),
                  (b_l1[:, 0:1], col("L1_ffn_cn_b1")), (b_l1[0:64, 1:2], col("L1_ffn_cn_b2")),
                  (b_l1[0:32, 2:3], col("L1_ffn_cn_b3")),
                  (b_l1[:, 3:4], row("L1_ffn_cn_b4").broadcast_to([P, 1])),
                  (b_l1[0:64, 4:5], col("L1_ffn_gc_b1")), (b_l1[0:32, 5:6], col("L1_ffn_gc_b2")),
                  (b_l1[:, 6:7], row("L1_ffn_gc_b3").broadcast_to([P, 1])),
                  (b_l1[:, 7:8], row("L1_ffn_adaptive_range").broadcast_to([P, 1]))]

        def w3rows(w):
            return w.rearrange("(k p) d -> p k d", p=P)

        def w3tile(e):
            return wmoe[:, e, 2 * FF:3 * FF].rearrange("p (k d) -> p k d", k=FK)

        loads5 = [(wmoe[:, NE, 0:FF], I["L2_ffn_w1s"]), (wmoe[:, NE, FF:2 * FF], I["L2_ffn_w2s"]),
                  (w3tile(NE), w3rows(I["L2_ffn_w3s"])), (w_g[:], I["L2_ffn_Wg"])]
        for e in range(NE):
            loads5 += [(wmoe[:, e, 0:FF], I["L2_ffn_W1"][e]), (wmoe[:, e, FF:2 * FF], I["L2_ffn_W2"][e]),
                       (w3tile(e), w3rows(I["L2_ffn_W3"][e]))]
        loads7 = [(wb[:, 0, :].rearrange("p (k d) -> p k d", k=FK), w3rows(I["L3_ffn_w1"])), (wb[:, 1, :], I["L3_ffn_w2"]),
                  (b1row[:], row("L3_ffn_b1").broadcast_to([P, FF])), (b2row[:], row("L3_ffn_b2").broadcast_to([P, P]))]

        def wv(l):
            return wraw[:, 4 * l + 2, :] if l < 2 else wvo3[:, 0, :]

        def wo(l):
            return wraw[:, 4 * l + 3, :] if l < 2 else wvo3[:, 1, :]

        def kjob(c, l):
            return c * 3 + l

        def qjob(l, c):
            return 3 * NC + l * NC + c

        def tjob_ctx(c):
            return c

        def tjob_q(l, c):
            return tjob(ST_ATT[l], c)

        def tjob(st, c):
            return NC * (1 + st) + c

        def pe_project(pe, n, u, w, xs):
            pe.wait_ge(s_r1, past(n - 2))
            pe.matmul(bank[2 + u][:], w, xs, start=True, stop=True).then_inc(s_proj, 1)

        def pe_meansq(pe, m):
            pe.wait_ge(s_sq, past(m))
            pe.wait_ge(s_mse, past(m - 1))
            pe.matmul(bank[4][:], C["headmean"], sq[:], start=True, stop=True).then_inc(s_ms, 1)

        def act_split(act, n, half_n, u, is_k, bias, m=None):
            order = (0, 1) if is_k else (2, 1)
            if m is not None:
                act.wait_ge(s_proj, past(n))
                act.wait_ge(s_ms, past(m - 1))
                act.activation(sq[:], bank[2 + u][:], ACT.Square).then_inc(s_sq, 1)
                act.wait_ge(s_ms, past(m))
                act.activation(rms[:], bank[4][:], ACT.Sqrt, bias=eps6[:, 0:1]).then_inc(s_mse, 1)
                act.wait_ge(s_rms, past(m))
                src = resid[:, u, :]
            else:
                act.wait_ge(s_proj, past(n))
                src = bank[2 + u][:]
            act.wait_ge(s_stored[u], past_dma(half_n - 1, 6))
            act.activation(parts[:, u, order[0], :], src, ACT.Identity,
                           bias=0.0 if bias is None else bias).then_inc(s_hi, 1)
            act.wait_ge(s_r1, past(n))
            act.activation(parts[:, u, order[1], :], resid[:, u, :], ACT.Identity).then_inc(s_mid, 1)

        def dve_split(dve, n, u, is_k, bias, m=None, gamma=None):
            order = (0, 1, 2) if is_k else (2, 1, 0)
            hi, mid, lo = (parts[:, u, k, :] for k in order)
            r = resid[:, u, :]
            if m is not None:
                dve.wait_ge(s_mse, past(m))
                dve.reciprocal(rms[:], rms[:]).then_inc(s_inv, 1)
                dve.wait_ge(s_inv, past(m))
                dve.scalar_tensor_tensor(out=r, in0=bank[2 + u][:], scalar=gamma, in1=rms[:],
                                         op0=ALU.mult, op1=ALU.mult).then_inc(s_rms, 1)
                dve.wait_ge(s_hi, past(n))
                dve.tensor_tensor(r, r, hi, ALU.subtract).then_inc(s_r1, 1)
            elif bias is None:
                dve.wait_ge(s_hi, past(n))
                dve.tensor_tensor(r, bank[2 + u][:], hi, ALU.subtract).then_inc(s_r1, 1)
            else:
                dve.wait_ge(s_hi, past(n))
                dve.scalar_tensor_tensor(out=r, in0=bank[2 + u][:], scalar=bias, in1=hi,
                                         op0=ALU.add, op1=ALU.subtract).then_inc(s_r1, 1)
            dve.wait_ge(s_mid, past(n))
            dve.tensor_tensor(lo, r, mid, ALU.subtract).then_inc(s_lo, 1)

        def sp_store(sp, n, half_n, u, is_k, dst):
            sp.wait_ge(s_lo, past(n))
            sp.sem_inc(s_sp, 1)
            for half in range(2):
                rows = slice(64 * half, 64 * half + 64)
                for t0, k in ((0, 3), (3, 2), (5, 1)):
                    k0 = 0 if is_k else 3 - k
                    sp.dma_start(dst[half, t0:t0 + k].rearrange("k b p t -> p (k b) t"),
                                 parts[rows, u, k0:k0 + k, :].rearrange("p k (b t) -> p (k b) t", b=CB)
                                 ).then_inc(s_stored[u], 16)

        def sp_load(sp, l, c, k):
            b = c * CB + k
            sp.wait_ge(s_av, past(NG * (B * l + b - NS) + NG - 1))
            sp.sem_inc(s_sp, 1)
            for half in range(2):
                rows = slice(64 * half, 64 * half + 48)
                for stk, src in ((kstk, k_dram), (qstk, q_dram)):
                    sp.dma_start(stk[rows, k].rearrange("p h t -> p (h t)"),
                                 src[l][c, half, :, k].rearrange("k (d h) t -> k d (h t)", h=8)
                                 ).then_inc(s_stk[k], 16)
            sp.dma_start(v_in[:, k].rearrange("p h w -> p (h w)"), v_dram[l][b]).then_inc(s_stk[k], 16)

        def pe_scores(pe, l, b, k, turn, g):
            U = NG * (B * l + b) + g
            if g == 0:
                pe.wait_ge(s_stk[k], past_dma(NC * l + turn, 5))
            pe.wait_ge(s_max, past(U - 2))
            for j, (half, h) in enumerate(slots(g)):
                r = slice(64 * half, 64 * half + 48)
                mm = pe.matmul(bank[g % 2][:, j * P:(j + 1) * P], qstk[r, k, h, :], kstk[r, k, h, :],
                               start=True, stop=True)
            mm.then_inc(s_sc, 1)

        def pe_maxT(pe, l, b, u):
            n = B * l + b
            pe.wait_ge(s_mparts, past(n))
            pe.wait_ge(s_mt, past(n - 1))
            pe.transpose(maxT_ps, mpad[:, u, :], identb[:]).then_inc(s_mtp, 1)

        def pe_scoresT(pe, l, b, k, u, g):
            U = NG * (B * l + b) + g
            if g == 0:
                pe.wait_ge(s_mt, past(B * l + b))
            pe.wait_ge(s_exp, past(U - 2))
            for j, (half, h) in enumerate(slots(g)):
                r = slice(64 * half, 64 * half + 48)
                rm = slice(64 * half, 64 * half + 64)
                o = bank[2 + g % 2][:, j * P:(j + 1) * P]
                pe.matmul(o, kstk[r, k, h, :], qstk[r, k, h, :], start=True, stop=False)
                mm = pe.matmul(o, selb[rm, h, :], mT[rm, u, :], start=False, stop=True)
            mm.then_inc(s_st, 1)

        def pe_values(pe, l, b, k, g):
            U = NG * (B * l + b) + g
            pe.wait_ge(s_exp, past(U))
            if g == 0:
                pe.wait_ge(s_norm, past(B * l + b - 1))
            for j, (half, h2) in enumerate(slots(g)):
                h = 2 * h2 + half
                mm = pe.matmul(o_ps[:, h, :], probs[:, g, j * P:(j + 1) * P], v_in[:, k, h, :],
                               start=True, stop=True)
            mm.then_inc(s_av, 1)

        def pe_attT(pe, l, b, u):
            n = B * l + b
            pe.wait_ge(s_norm, past(n))
            pe.wait_ge(s_atc, past(n - 1))
            pe.transpose(attT_ps, att[:, u, :], ident).then_inc(s_atp, 1)

        def pe_outproj(pe, l, b, u):
            n = B * l + b
            pe.wait_ge(s_atc, past(n))
            pe.wait_ge(s_xup, past(upd(ST_ATT[l], b) - 1))
            if l > 0:
                pe.matmul(y_ps, ones_row[0:1, :], borow[0:1, l, :], start=True, stop=False)
            pe.matmul(y_ps, attT[:, u, :], wo(l), start=(l == 0), stop=True).then_inc(s_y, 1)

        o_ps = bank[4][:, 0:H * VW].rearrange("p (h w) -> p h w", w=VW)
        maxT_ps = bank[5][:, 0:P // 2].bitcast(BF16)
        attT_ps = bank[6][:, 0:P]
        y_ps = bank[7][:, 0:P]

        def dve_max(dve, l, b, u, g):
            U = NG * (B * l + b) + g
            dve.wait_ge(s_sc, past(U))
            half, h0 = slots(g)[0]
            dve.tensor_reduce(negm[:, u, half, h0:h0 + GH], bank[g % 2][:].rearrange("p (h k) -> p h k", h=GH),
                              AX.X, ALU.max, negate=True).then_inc(s_max, 1)

        def dve_maxparts(dve, ch, l, b, u):
            dve.wait_ge(s_max, past(NG * (B * l + b) + NG - 1))
            mp = mpad[:, u, :].rearrange("p (half k h) -> p half k h", half=2, k=8)
            ch.step(dve.tensor_copy(mp[:, :, 0, :], negm[:, u]))
            dve.tensor_tensor(mp[:, :, 1, :], negm[:, u], mp[:, :, 0, :], ALU.subtract).then_inc(s_mparts, 1)

        def dve_norm(dve, ch, l, b, u):
            n = B * l + b
            dve.wait_ge(s_av, past(NG * n + NG - 1))
            o = o_ps
            ch.step(dve.reciprocal(rden[:], o[:, :, HD]))
            dve.wait_ge(s_atp, past(n - 2))
            dve.tensor_tensor(att[:, u, :].rearrange("p (h d) -> p h d", d=HD), o[:, :, 0:HD],
                              rden[:].unsqueeze(2).broadcast_to([P, H, HD]), ALU.mult).then_inc(s_norm, 1)

        def dve_update(dve, ch, l, b):
            n = B * l + b
            dve.wait_ge(s_y, past(n))
            dve.tensor_tensor(xnew[:], x_sb[:, b, :], y_ps, ALU.add).then_inc(s_xup, 1)
            dve.wait_ge(s_xup, past(upd(ST_ATT[l], b)))
            dve_stats(dve, ch, b)

        def dve_stats(dve, ch, b):
            ch.step(dve.bn_stats(stats[:], xnew[:]))
            dve.tensor_scalar(x_sb[:, b, :], xnew[:], 1.0, None, ALU.mult)
            ch.step(dve.bn_aggr(mvnew[:], stats[:]))
            dve.tensor_scalar(mv[:, b, :], mvnew[:], 1.0, None, ALU.mult)

        def act_copies(act, src, dst, wait, n, sig):
            act.wait_ge(wait, past(n))
            act.activation(dst, src, ACT.Copy).then_inc(sig, 1)

        def act_exp(act, l, b, g):
            U = NG * (B * l + b) + g
            act.wait_ge(s_st, past(U))
            act.wait_ge(s_av, past(U - NG))
            act.activation(probs[:, g, :], bank[2 + g % 2][:], ACT.Exp, scale=float(1 / np.sqrt(HD))).then_inc(s_exp, 1)

        def pe_step(pe, l, b, k, turn_next, first=False, last=False):
            u, k_next = k % 2, (k + 1) % NS
            if not last:
                pe_scores(pe, l, b + 1, k_next, turn_next, 0)
            pe_maxT(pe, l, b, u)
            if not first:
                pe_attT(pe, l, b - 1, 1 - u)
            if not last:
                pe_scores(pe, l, b + 1, k_next, turn_next, 1)
            pe_scoresT(pe, l, b, k, u, 0)
            if not first:
                pe_outproj(pe, l, b - 1, 1 - u)
            for g in range(1, NG):
                if not last and g < NG - 1:
                    pe_scores(pe, l, b + 1, k_next, turn_next, g + 1)
                pe_scoresT(pe, l, b, k, u, g)
                pe_values(pe, l, b, k, g - 1)
            pe_values(pe, l, b, k, NG - 1)

        def dve_step(dve, ch, l, b, u, first, last):
            dve_maxparts(dve, ch, l, b, u)
            if not first:
                dve_norm(dve, ch, l, b - 1, 1 - u)
            if not last:
                dve_max(dve, l, b + 1, 1 - u, 0)
                dve_max(dve, l, b + 1, 1 - u, 1)
            if not first:
                dve_update(dve, ch, l, b - 1)
            if not last:
                dve_max(dve, l, b + 1, 1 - u, 2)
                dve_max(dve, l, b + 1, 1 - u, 3)

        def act_step(act, l, b, u, first):
            n = B * l + b
            act_copies(act, maxT_ps, mT[:, u, :], s_mtp, n, s_mt)
            if not first:
                act_copies(act, attT_ps, attT[:, 1 - u, :], s_atp, n - 1, s_atc)
            for g in range(NG):
                act_exp(act, l, b, g)

        def attention_pe(pe, l):
            with pe.Fori(0, NC // 2) as i:
                for u in range(2):
                    c = i * 2 + u
                    pe_columns(pe, tjob_q(l, c), u, xn)
                    pe.wait_ge(s_xT, past(tjob_q(l, c)))
                    pe_project(pe, qjob(l, c), u, wq[:, l, :], xT[:, u, :])
                    if l == 0:
                        pe_meansq(pe, NC + c)
            pe.wait_ge(s_xT, past(tjob_q(l, NC - 1)))
            for g in range(NG):
                pe_scores(pe, l, 0, 0, 0, g)
            pe.wait_ge(s_r1, past(qjob(l, NC - 1)))
            pe_step(pe, l, 0, 0, 0, first=True)
            with pe.Fori(0, NC - 1) as i:
                for k in range(1, CB + 1):
                    pe_step(pe, l, i * CB + k, k % CB, i + (k + 1) // CB)
            for b in range(B - 3, B):
                pe_step(pe, l, b, b % CB, NC - 1, last=b == B - 1)
            pe_attT(pe, l, B - 1, 1)
            pe_outproj(pe, l, B - 1, 1)

        def attention_dve(dve, ch, l):
            dve_rstd(dve, ch, norm(ST_ATT[l]))
            with dve.Fori(0, NC // 2) as i:
                for u in range(2):
                    c = i * 2 + u
                    dve_rows(dve, tjob_q(l, c), c, u)
                    bias = None if l == 0 else colbias[:, 2 * l:2 * l + 1]
                    dve_split(dve, qjob(l, c), u, False, bias, NC + c if l == 0 else None, colbias[:, 0:1])
            for g in range(NG):
                dve_max(dve, l, 0, 0, g)
            dve_step(dve, ch, l, 0, 0, True, False)
            with dve.Fori(0, (B - 2) // 2) as i:
                ch.loop(i, 8)
                dve_step(dve, ch, l, i * 2 + 1, 1, False, False)
                dve_step(dve, ch, l, i * 2 + 2, 0, False, False)
            ch.end((B - 2) // 2)
            dve_step(dve, ch, l, B - 1, 1, False, True)
            dve_norm(dve, ch, l, B - 1, 1)
            dve_update(dve, ch, l, B - 1)

        def attention_act(act, l):
            with act.Fori(0, NC // 2) as i:
                for u in range(2):
                    c = i * 2 + u
                    act.wait_ge(s_vp, past(kjob(NC - 1, 2)))
                    act.wait_ge(s_proj, past(qjob(l, c) - 2))
                    act_columns(act, tjob_q(l, c), u)
                    bias = None if l == 0 else colbias[:, 2 * l:2 * l + 1]
                    act_split(act, qjob(l, c), qjob(l, 0) // 2 + i, u, False, bias, NC + c if l == 0 else None)
            act_step(act, l, 0, 0, True)
            with act.Fori(0, (B - 2) // 2) as i:
                act_step(act, l, i * 2 + 1, 1, False)
                act_step(act, l, i * 2 + 2, 0, False)
            act_step(act, l, B - 1, 1, False)
            act_copies(act, attT_ps, attT[:, 1, :], s_atp, B * l + B - 1, s_atc)

        def attention_sp(sp, l):
            def store(c, u, i):
                sp_store(sp, qjob(l, c), qjob(l, 0) // 2 + i, u, False, q_dram[l][c])
            store(0, 0, 0)
            store(1, 1, 0)
            sp.wait_ge(s_stored[0], past_dma(qjob(l, 0) // 2, 6))
            for k in range(CB):
                sp_load(sp, l, 0, k)
            store(2, 0, 1)
            store(3, 1, 1)
            for u in range(2):
                sp.wait_ge(s_stored[u], past_dma(qjob(l, 0) // 2 + 1, 6))
            with sp.Fori(1, NC) as c:
                for k in range(CB):
                    sp_load(sp, l, c, k)

        def chunk_dram(t, c):
            return t[bass.ds(c * CB, CB)] if not isinstance(c, int) else t[c * CB:(c + 1) * CB]

        def dve_rstd(dve, ch, n):
            ch.step(dve.drain())
            dve.tensor_scalar(vareps[:], mv[:, :, 1], EPS, None, ALU.add).then_inc(s_var, 1)
            dve.wait_ge(s_rstd, past(n))

        def pool_rstd(pool, n):
            pool.wait_ge(s_var, past(n))
            pool.tensor_tensor(rstd[:], vareps[:], neg_half[:, 0:B], ALU.pow).then_inc(s_rstd, 1)

        def dve_rows(dve, t, c, u):
            dve.wait_ge(s_tr, past(t - 2))
            for k in range(CB):
                b = c * CB + k
                ins = dve.tensor_scalar(xn[:, u, k, :], x_sb[:, b, :], mv[:, b, 0:1], rstd[:, bass.ds(b, 1)],
                                        ALU.subtract, ALU.mult)
            ins.then_inc(s_xn, 1)

        def pe_columns(pe, t, u, src):
            pe.wait_ge(s_xn, past(t - NC))
            pe.wait_ge(s_xT, past(t - 2))
            for k in range(CB):
                mm = pe.transpose(bank[u][:, k * P:(k + 1) * P], src[:, u, k, :], ident)
            mm.then_inc(s_tr, 1)

        def act_columns(act, t, u):
            act.wait_ge(s_tr, past(t))
            act.activation(xT[:, u, :], bank[u][:], ACT.Copy).then_inc(s_xT, 1)

        def bank_used(st, c):
            return past(upd(st, (c - 2) * CB + CB - 1))

        def pe_rows(pe, st, c, w, n=P):
            u = c % 2
            pe.wait_ge(s_xT, past(tjob(st, c)))
            for k in range(CB):
                mm = pe.matmul(bank[2 + u][:, k * n:(k + 1) * n], xT[:, u, k * P:(k + 1) * P], w,
                               start=True, stop=True)
            mm.then_inc(s_rp, 1)

        def dve_update_chunk(dve, ch, st, c, rp, scale=None):
            u = c % 2
            dve.wait_ge(s_rp, past(rp))
            for k in range(CB):
                b = c * CB + k
                src = bank[2 + u][:, k * P:(k + 1) * P]
                if scale is None:
                    ins = dve.tensor_tensor(xnew[:], x_sb[:, b, :], src, ALU.add)
                else:
                    ins = dve.scalar_tensor_tensor(out=xnew[:], in0=src, scalar=scale, in1=x_sb[:, b, :],
                                                   op0=ALU.mult, op1=ALU.add)
                ins.then_inc(s_xup, 1)
                dve.wait_ge(s_xup, past(upd(st, b)))
                dve_stats(dve, ch, b)

        def flat(t):
            return t.rearrange("p b d -> p (b d)")

        def over(row, n):
            return row.unsqueeze(1).broadcast_to([P, n, row.shape[1]])

        def ffn0_dve(dve, ch):
            st = ST_FFN0
            dve_rstd(dve, ch, norm(st))
            ch.step(dve.tensor_copy(rs1[:], rstd[:]))
            ch.step(dve.tensor_tensor(vareps[:], mv[:, :, 1], rs1[:], ALU.mult))
            ch.step(dve.tensor_tensor(vareps[:], vareps[:], rs1[:], ALU.mult))
            dve.tensor_scalar(vareps[:], vareps[:], 1e-3, None, ALU.add).then_inc(s_var, 1)
            dve.tensor_reduce(sc[:, 0:1], w_f0[:], AX.X, ALU.add, apply_absolute_value=True).then_inc(s_dve1, 1)
            dve.wait_ge(s_rstd, past(norm(st) + 1))
            ch.step(dve.tensor_tensor(rs1[:], rs1[:], rstd[:], ALU.mult))
            for c in range(NC):
                for k in range(CB):
                    b = c * CB + k
                    ins = dve.tensor_scalar(xall[:, b, :], x_sb[:, b, :], mv[:, b, 0:1], rs1[:, b:b + 1],
                                            ALU.subtract, ALU.mult)
                ch.step(ins)
                xc = xall[:, c * CB:(c + 1) * CB, :]
                ch.step(dve.tensor_tensor(xc, xc, over(lnrow[:, 0, :], CB), ALU.mult))
                ch.step(dve.tensor_tensor(xc, xc, over(lnrow[:, 1, :], CB), ALU.add))
                ch.step(dve.tensor_reduce(amax[:, c:c + 1], flat(xc), AX.X, ALU.max, apply_absolute_value=True))
            dve.tensor_reduce(sc[:, 1:2], amax[:], AX.X, ALU.max).then_inc(s_dve1, 1)
            dve.wait_ge(s_pe1, PE1["amaxT"])
            dve.tensor_reduce(sc[0:1, 2:3], bank[6][0:1, 0:P], AX.X, ALU.max).then_inc(s_dve1, 1)
            beta, gain, lo = sc[:, 3:4], sc[:, 4:5], sc[:, 5:6]
            ch.step(dve.tensor_scalar(beta, bank[5][:, 0:1], 1.0 / (P * P), None, ALU.mult))
            ch.step(dve.tensor_scalar(gain, beta, 1e-5, None, ALU.add))
            ch.step(dve.reciprocal(gain, gain))
            ch.step(dve.tensor_scalar(w_t0[:, 0, :], w_f0[:], gain, 0.5, ALU.mult, ALU.is_gt))
            ch.step(dve.tensor_scalar(w_t0[:, 1, :], w_f0[:], gain, -0.5, ALU.mult, ALU.is_lt))
            ch.step(dve.tensor_tensor(w_t0[:, 0, :], w_t0[:, 0, :], w_t0[:, 1, :], ALU.subtract))
            dve.wait_ge(s_pe1, PE1["amax"])
            gam, to_q, to_y = sc[:, 6:7], sc[:, 7:8], sc[:, 8:9]
            ch.step(dve.tensor_copy(gam, bank[7][:, 0:1]))
            ch.step(dve.reciprocal(to_q, gam))
            ch.step(dve.tensor_scalar(to_q, to_q, 128.0, None, ALU.mult))
            ch.step(dve.tensor_tensor(to_y, gam, beta, ALU.mult))
            ch.step(dve.tensor_scalar(to_y, to_y, 1.0 / 128, None, ALU.mult))
            dve.drain().then_inc(s_dve1, 1)
            lim = float(np.float32(128.0 - 1e-5))

            def rows(c):
                dve.wait_ge(s_tr, past(tjob(st, c) - 2))
                xc = xn[:, c % 2]
                ch.step(dve.tensor_scalar(xc, xall[:, c * CB:(c + 1) * CB, :], to_q, lim, ALU.mult, ALU.min))
                dve.tensor_scalar(xc, xc, -lim, None, ALU.max).then_inc(s_xn, 1)
            rows(0)
            for c in range(NC):
                if c + 1 < NC:
                    rows(c + 1)
                dve_update_chunk(dve, ch, st, c, c, scale=to_y)

        def ffn0_pe(pe):
            pe.wait_ge(s_dve1, DVE1["wabs0"])
            pe.matmul(bank[5][:, 0:1], ones_sq[:], sc[:, 0:1], start=True, stop=True).then_inc(s_pe1, 1)
            pe.wait_ge(s_dve1, DVE1["amax_col"])
            pe.transpose(bank[6][0:1, 0:P], sc[:, 1:2], ident).then_inc(s_pe1, 1)
            pe.wait_ge(s_dve1, DVE1["amax_row"])
            pe.matmul(bank[7][:, 0:1], ones_row[0:1, :], sc[0:1, 2:3], start=True, stop=True).then_inc(s_pe1, 1)
            pe.wait_ge(s_dve1, DVE1["ternary0"])
            for c in range(NC):
                pe_columns(pe, tjob(ST_FFN0, c), c % 2, xn)
                pe.wait_ge(s_xup, bank_used(ST_FFN0, c))
                pe_rows(pe, ST_FFN0, c, w_t0[:, 0, :])

        def columns_act(act, st):
            for c in range(NC):
                act_columns(act, tjob(st, c), c % 2)

        RP_CORR = NC

        def corr_dve(dve, ch):
            st = ST_CORR
            dve_rstd(dve, ch, norm(st))
            for c in range(NC):
                dve_rows(dve, tjob(st, c), c, c % 2)
            for c in range(NC):
                dve.wait_ge(s_rp, past(RP_CORR + c))
                w = CB * HD
                ins = dve.tensor_tensor(q1[:, c * w:(c + 1) * w].rearrange("p (b d) -> p b d", d=HD),
                                        bank[2 + c % 2][:, 0:w].rearrange("p (b d) -> p b d", d=HD),
                                        over(bq_c[:], CB), ALU.add)
                ins.then_inc(s_q1, 1)
            ch.step(dve.drain())
            dve.drain().then_inc(s_dve1, 1)
            dve.wait_ge(s_pe1, PE1["qkT"])
            dve.tensor_copy(flat(qk1T[:]), bank[5][:, 0:2 * P]).then_inc(s_dve1, 1)
            dve.wait_ge(s_pe1, PE1["corrM"])
            dve.tensor_copy(mm2[:], over(bank[6][:, 0:P], 2)).then_inc(s_dve1, 1)
            dve.wait_ge(s_pe1, PE1["corr"])
            ch.step(dve.tensor_copy(crow[:], bank[7][:, 0:P]))
            top, colv, z = sc[:, 10:11], sc[:, 11:12], sc[:, 12:13]
            ch.step(dve.tensor_tensor(cwork[:, 0, :], crow[:], ident, ALU.mult))
            ch.step(dve.tensor_reduce(colv, cwork[:, 0, :], AX.X, ALU.add))
            dve.tensor_reduce(top, crow[:], AX.X, ALU.max, negate=True).then_inc(s_dve1, 1)
            ch.step(dve.tensor_scalar(cwork[:, 1, :], crow[:], colv, None, ALU.is_equal))
            ch.step(dve.tensor_tensor(cwork[:, 1, :], cwork[:, 1, :], C["tie"], ALU.mult))
            ch.step(dve.tensor_scalar(cwork[:, 0, :], crow[:], colv, None, ALU.is_lt))
            dve.tensor_tensor(cwork[:, 0, :], cwork[:, 0, :], cwork[:, 1, :], ALU.add).then_inc(s_dve1, 1)
            dve.wait_ge(s_pe1, PE1["rank"])
            dve.wait_ge(s_act1, ACT1["corr_exp"])
            ch.step(dve.tensor_scalar(cwork[:, 1, :], bank[5][:, 0:P], K_TOP - 0.5, None, ALU.is_lt))
            ch.step(dve.tensor_tensor(cwork[:, 1, :], cwork[:, 1, :], cwork[:, 2, :], ALU.mult))
            ch.step(dve.tensor_reduce(z, cwork[:, 1, :], AX.X, ALU.add))
            ch.step(dve.reciprocal(z, z))
            dve.tensor_scalar(cwork[:, 0, :], cwork[:, 1, :], z, None, ALU.mult).then_inc(s_dve1, 1)
            dve.wait_ge(s_pe1, PE1["rolled"])
            dve.tensor_copy(rolled[:], bank[6][:, 0:P]).then_inc(s_dve1, 1)
            dve.wait_ge(s_pe1, PE1["rolled_out"])
            ch.step(dve.tensor_tensor(crow[:], bank[7][:, 0:P], bout_c[:], ALU.add))

            def rows(c):
                dve.wait_ge(s_rp, past(RP_CORR + NC + c - 2))
                for k in range(CB):
                    b = c * CB + k
                    ins = dve.tensor_scalar(ymask[:, c % 2, k, :], crow[:], C["own_batch"][:, b:b + 1], None, ALU.mult)
                ins.then_inc(s_ym, 1)
            rows(0)
            for c in range(NC):
                if c + 1 < NC:
                    rows(c + 1)
                dve_update_chunk(dve, ch, st, c, RP_CORR + NC + c)

        s_q1, s_ym = item("s_q1"), item("s_ym")

        def corr_pe(pe):
            st = ST_CORR
            for c in range(NC):
                pe_columns(pe, tjob(st, c), c % 2, xn)
                pe.wait_ge(s_q1, past(c - 2))
                pe_rows(pe, st, c, w_c[:], HD)
            pe.wait_ge(s_dve1, DVE1["corr_in"])
            pe.transpose(bank[5][:, 0:P], q1[:], ident)
            pe.transpose(bank[5][:, P:2 * P], k1[:], ident).then_inc(s_pe1, 1)
            pe.wait_ge(s_dve1, DVE1["corr_T"])
            pe.matmul(bank[6][:, 0:P], qk1T[:, 0, :], qk1T[:, 1, :], start=True, stop=True).then_inc(s_pe1, 1)
            pe.wait_ge(s_skew, 32)
            pe.matmul(bank[7][:, 0:P], mean_sq[:], skew[:], start=True, stop=True).then_inc(s_pe1, 1)
            pe.wait_ge(s_dve1, DVE1["corr_G"])
            pe.matmul(bank[5][:, 0:P], ones_sq[:], cwork[:, 0, :], start=True, stop=True).then_inc(s_pe1, 1)
            pe.wait_ge(s_skew, 64)
            pe.matmul(bank[6][:, 0:P], skew[:], k1[:], start=True, stop=True).then_inc(s_pe1, 1)
            pe.wait_ge(s_dve1, DVE1["rolled_sb"])
            pe.matmul(bank[7][:, 0:P], rolled[:], wout_c[:], start=True, stop=True).then_inc(s_pe1, 1)
            for c in range(NC):
                u = c % 2
                pe.wait_ge(s_ym, past(c))
                pe.wait_ge(s_xup, bank_used(st, c))
                pe.matmul(bank[2 + u][:], C["mod8"], flat(ymask[:, u]), start=True, stop=True).then_inc(s_rp, 1)

        def corr_act(act):
            columns_act(act, ST_CORR)
            act.wait_ge(s_dve1, DVE1["corr_negmax"])
            act.activation(cwork[:, 2, :], crow[:], ACT.Exp, bias=sc[:, 10:11]).then_inc(s_act1, 1)

        def corr_sp(sp):
            sp.wait_ge(s_dve1, DVE1["corr_mm"])
            sp.dma_start(corr_dram, mm2[:].rearrange("p a n -> p (a n)")).then_inc(s_skew, 16)
            sp.wait_ge(s_skew, 16)
            sp.dma_start(skew[:], bass.AP(corr_dram.tensor, 0, [[2 * P + 1, P], [1, P]])).then_inc(s_skew, 16)
            sp.wait_ge(s_dve1, DVE1["corr_w"])
            sp.dma_start(wlag_dram, cwork[:, 0, :]).then_inc(s_skew, 16)
            sp.wait_ge(s_skew, 48)
            sp.dma_start(skew[:], bass.AP(wlag_dram.tensor, 0, [[P - 1, P], [1, P]])).then_inc(s_skew, 16)

        def twist_dve(dve, ch):
            st = ST_TWIST
            for k in range(2):
                w = (CN[4], GC[3])[k]
                ch.step(dve.tensor_scalar(w, ones_sq[0:32, :], w4c[:, k:k + 1], None, ALU.mult))
            ar = b_l1[:, 7:8]
            ch.step(dve.tensor_scalar(b_l1[:, 3:4], b_l1[:, 3:4], 0.5, None, ALU.mult))
            ch.step(dve.tensor_scalar(b_l1[:, 6:7], b_l1[:, 6:7], 0.5, None, ALU.mult))
            dve_rstd(dve, ch, norm(st))
            for c in range(NC):
                dve_rows(dve, tjob(st, c), c, c % 2)
            for c in range(NC):
                dve.wait_ge(s_xT, past(tjob(st, c)))
                dve.tensor_reduce(gx[:, 0, c * CB:(c + 1) * CB], xall[:, c * CB:(c + 1) * CB, :], AX.X, ALU.add)
            ch.step(dve.drain())
            dve.tensor_scalar(gx[:, 0, :], gx[:, 0, :], 1.0 / P, None, ALU.mult).then_inc(s_dve1, 1)
            dve.wait_ge(s_act1, ACT1["g3"])
            ch.step(dve.tensor_scalar(acoef[:], gx[:, 3, :], ar, 0.7, ALU.mult, ALU.mult))
            ch.step(dve.tensor_scalar(acoef[:], acoef[:], 0.1, None, ALU.add))
            ch.step(dve.tensor_scalar(sc[:, 13:14], ar, 0.3, None, ALU.mult))
            dve.drain().then_inc(s_dve1, 1)
            for y in range(CYCLES):
                for c in range(NC):
                    n, u = NC * y + c, c % 2
                    cols = xcols[:, c * CW:(c + 1) * CW]
                    t3 = tf[:, u, :].rearrange("p (b t) -> p b t", b=CB)
                    dve.wait_ge(s_g4, past(n))
                    ch.step(dve.scalar_tensor_tensor(out=t3, in0=t3, scalar=sc[:, 13:14],
                                                     in1=acoef[:, c * CB:(c + 1) * CB].unsqueeze(2).broadcast_to([P, CB, P]),
                                                     op0=ALU.mult, op1=ALU.add))
                    dve.wait_ge(s_twp, past(n))
                    ch.step(dve.tensor_tensor(tws[:, u, :], bank[6][:], tf[:, u, :], ALU.mult))
                    dve.tensor_tensor(cols, cols, tws[:, u, :], ALU.add).then_inc(s_cyc, 1)
            for c in range(NC):
                dve_update_chunk(dve, ch, st, c, RP_CORR + 2 * NC + c)

        def twist_pe(pe):
            st = ST_TWIST
            for c in range(NC):
                pe_columns(pe, tjob(st, c), c % 2, xn)
            for k in range(3):
                pe.wait_ge(s_dve1, DVE1["gmean"]) if k == 0 else pe.wait_ge(s_act1, ACT1[f"g{k}"])
                w = GC[k + 1]
                pe.matmul(bank[5][0:w.shape[1], 0:B], w, gx[0:w.shape[0], k, :], start=True, stop=True).then_inc(s_pe1, 1)
            pe.wait_ge(s_act1, ACT1["g3"])
            for y in range(CYCLES):
                for c in range(NC):
                    n, u = NC * y + c, c % 2
                    cols = xcols[:, c * CW:(c + 1) * CW]
                    pe.wait_ge(s_cyc, past(n - NC))
                    pe.wait_ge(s_g1, past(n - 1))
                    pe.matmul(bank[2][:], CN[1], cols, start=True, stop=True).then_inc(s_c1, 1)
                    pe.wait_ge(s_cyc, past(n - 1))
                    pe.matmul(bank[6][:], C["twist"], cols, start=True, stop=True).then_inc(s_twp, 1)
                    pe.wait_ge(s_g1, past(n))
                    pe.matmul(bank[3][0:64, :], CN[2], h1[:, u, :], start=True, stop=True).then_inc(s_c2, 1)
                    pe.wait_ge(s_g2, past(n))
                    pe.matmul(bank[4][0:32, :], CN[3], h2[:, u, :], start=True, stop=True).then_inc(s_c3, 1)
                    pe.wait_ge(s_g3, past(n))
                    pe.wait_ge(s_g4, past(n - 1))
                    pe.matmul(bank[5][:], CN[4], h3[:, u, :], start=True, stop=True).then_inc(s_c4, 1)
            for c in range(NC):
                u = c % 2
                pe.wait_ge(s_cyc, past(NC * (CYCLES - 1) + c))
                pe.wait_ge(s_g4, past(NC * CYCLES - 1))
                pe.wait_ge(s_xup, bank_used(st, c))
                for k in range(CB):
                    b = c * CB + k
                    mm = pe.transpose(bank[2 + u][:, k * P:(k + 1) * P], xall[:, b, :], ident)
                mm.then_inc(s_rp, 1)

        def twist_act(act):
            st = ST_TWIST
            for c in range(NC):
                act.wait_ge(s_tr, past(tjob(st, c)))
                act.activation(xcols[:, c * CW:(c + 1) * CW], bank[c % 2][:], ACT.Copy).then_inc(s_xT, 1)
            for k, (m, f, s) in enumerate(((64, ACT.Gelu, 1.0), (32, ACT.Gelu, 1.0), (P, ACT.Tanh, 0.5))):
                act.wait_ge(s_pe1, PE1[f"g{k + 1}"])
                act.activation(gx[0:m, k + 1, :], bank[5][0:m, 0:B], f, bias=b_l1[0:m, 4 + k:5 + k], scale=s).then_inc(s_act1, 1)
            for n in range(NC * CYCLES):
                u = n % 2
                act.wait_ge(s_c1, past(n))
                act.activation(h1[:, u, :], bank[2][:], ACT.Gelu, bias=b_l1[:, 0:1]).then_inc(s_g1, 1)
                act.wait_ge(s_c2, past(n))
                act.activation(h2[:, u, :], bank[3][0:64, :], ACT.Gelu, bias=b_l1[0:64, 1:2]).then_inc(s_g2, 1)
                act.wait_ge(s_c3, past(n))
                act.activation(h3[:, u, :], bank[4][0:32, :], ACT.Gelu, bias=b_l1[0:32, 2:3]).then_inc(s_g3, 1)
                act.wait_ge(s_c4, past(n))
                act.wait_ge(s_cyc, past(n - 2))
                act.activation(tf[:, u, :], bank[5][:], ACT.Tanh, bias=b_l1[:, 3:4], scale=0.5).then_inc(s_g4, 1)

        def bitw_dve(dve, ch):
            dve.wait_ge(s_w7, 16 * len(loads7))
            dve.tensor_reduce(bsc[:, 0:2], wb[:], AX.X, ALU.add, apply_absolute_value=True).then_inc(s_dve1, 1)
            dve.wait_ge(s_pe1, PE1["bit_mean"])
            ch.step(dve.tensor_scalar(bsc[:, 2:4], bank[5][:, 0:2], 1.0 / (P * FF), 1e-5, ALU.mult, ALU.max))
            ch.step(dve.reciprocal(bsc[:, 4:6], bsc[:, 2:4]))
            for k in range(2):
                ch.step(dve.tensor_scalar(wbt[:, k, :], wb[:, k, :], bsc[:, 4 + k:5 + k], 0.5, ALU.mult, ALU.is_gt))
                ch.step(dve.tensor_scalar(wb[:, k, :], wb[:, k, :], bsc[:, 4 + k:5 + k], -0.5, ALU.mult, ALU.is_lt))
                ins = dve.tensor_tensor(wbt[:, k, :], wbt[:, k, :], wb[:, k, :], ALU.subtract)
                if k == 0:
                    ch.step(ins)
            ins.then_inc(s_dve1, 1)
            dve.wait_ge(s_pe1, PE1["bit_wT"])
            dve.tensor_copy(w1T[:], bank[6][:, 0:FF // 2].bitcast(BF16))
            ch.step(dve.tensor_copy(w2T[:], bank[7][:, 0:FF // 2].bitcast(BF16)))

        def bitw_pe(pe):
            pe.wait_ge(s_dve1, DVE1["bit_abs"])
            pe.matmul(bank[5][:, 0:2], ones_sq[:], bsc[:, 0:2], start=True, stop=True).then_inc(s_pe1, 1)
            pe.wait_ge(s_dve1, DVE1["bit_tern"])
            for k in range(2):
                o = bank[6 + k][:, 0:FF // 2].bitcast(BF16)
                for f in range(FK):
                    mm = pe.transpose(o[:, f * P:(f + 1) * P], wbt[:, k, f * P:(f + 1) * P], identb[:])
            mm.then_inc(s_pe1, 1)

        RP_MOE = RP_CORR + 3 * NC

        def moe_route_dve(dve, ch):
            st = ST_MOE
            dve_rstd(dve, ch, norm(st))
            for c in range(NC):
                for k in range(CB):
                    b = c * CB + k
                    ins = dve.tensor_scalar(xall[:, b, :], x_sb[:, b, :], mv[:, b, 0:1], rstd[:, b:b + 1],
                                            ALU.subtract, ALU.mult)
                ins.then_inc(s_xn, 1)
            lg, eq, hot, tot, sa, sbb, cmp, tmp = (rt[:, k] for k in range(8))
            for c in range(NC):
                dve.wait_ge(s_rp, past(RP_MOE + c))
                dve.tensor_copy(lg[:, c * CB:(c + 1) * CB, :],
                                bank[2 + c % 2][:, 0:CB * NE].rearrange("p (b e) -> p b e", e=NE)).then_inc(s_lg, 1)
            ch.step(dve.drain())

            def of_batch(v):
                return v.unsqueeze(2).broadcast_to([P, B, NE])
            ch.step(dve.tensor_reduce(rs[:, 0, :], lg, AX.X, ALU.max))
            ch.step(dve.tensor_tensor(eq, lg, of_batch(rs[:, 0, :]), ALU.is_equal))
            ch.step(dve.tensor_tensor(eq, eq, over(C["first"], B), ALU.mult))
            ch.step(dve.tensor_reduce(rs[:, 0, :], eq, AX.X, ALU.max))
            dve.tensor_tensor(hot, eq, of_batch(rs[:, 0, :]), ALU.is_equal).then_inc(s_dve1, 1)
            dve.wait_ge(s_pe1, PE1["prefix"])
            earlier = lg
            dve.tensor_copy(earlier, bank[6][:, 0:P].rearrange("p (b e) -> p b e", e=NE))
            dve.tensor_copy(tot, bank[7][:, 0:P].rearrange("p (b e) -> p b e", e=NE)).then_inc(s_dve1, 1)
            dve.wait_ge(s_dve1, DVE1["prefix_read"])
            a = tot
            for step, o in ((1, sa), (2, sbb), (4, sa), (8, sbb)):
                dve.tensor_copy(o[:, 0:step], a[:, 0:step])
                ch.step(dve.tensor_tensor(o[:, step:B], a[:, step:B], a[:, 0:B - step], ALU.add))
                a = o
            n_e = a[:, B - 1, :]
            cm = cmp.rearrange("p b e -> p (b e)").rearrange("p (e k) -> p e k", k=B)
            ch.step(dve.tensor_tensor(cm, n_e.unsqueeze(2).broadcast_to([P, NE, B]), over(C["tile_rows"], NE), ALU.is_gt))
            tiles, e1, e2 = rs[:, 1, 0:NE], rs[:, 2, 0:NE], rs[:, 3, 0:NE]
            ch.step(dve.tensor_reduce(tiles, cm, AX.X, ALU.add))
            s = tiles
            for step, o in ((1, e1), (2, e2), (4, e1)):
                dve.tensor_copy(o[:, 0:step], s[:, 0:step])
                ch.step(dve.tensor_tensor(o[:, step:NE], s[:, step:NE], s[:, 0:NE - step], ALU.add))
                s = o
            start = rs[:, 4, 0:NE]
            ch.step(dve.tensor_tensor(start, e1, tiles, ALU.subtract))
            ch.step(dve.tensor_scalar(start, start, float(P), float(B * P), ALU.mult, ALU.add))
            ch.step(dve.tensor_tensor(a, a, tot, ALU.subtract))
            ch.step(dve.tensor_tensor(a, a, earlier, ALU.add))
            ch.step(dve.tensor_tensor(a, a, over(start, B), ALU.add))
            ch.step(dve.tensor_tensor(a, a, hot, ALU.mult))
            ch.step(dve.tensor_reduce(rs[:, 5, :], a, AX.X, ALU.add))
            dve.tensor_copy(pos[:], rs[:, 5, :])
            x3 = rx[:].rearrange("p (j e) -> p j e", e=NE)
            ch.step(dve.tensor_tensor(x3, C["tile_no"].unsqueeze(2).broadcast_to([P, NX, NE]), over(e1, NX), ALU.is_ge))
            tj = rt[:, 7].rearrange("p b e -> p (b e)")[:, 0:NX]
            ch.step(dve.tensor_reduce(tj, x3, AX.X, ALU.add))
            dve.tensor_scalar(etab[:], tj, float(NE - 1), None, ALU.min).then_inc(s_dve1, 1)

        def moe_route_pe(pe):
            st = ST_MOE
            for c in range(NC):
                u = c % 2
                pe.wait_ge(s_xn, past(tjob(st, c) - NC))
                pe.wait_ge(s_xT, past(tjob(st, c) - 2))
                for k in range(CB):
                    mm = pe.transpose(bank[u][:, k * P:(k + 1) * P], xall[:, c * CB + k, :], ident)
                mm.then_inc(s_tr, 1)
                pe.wait_ge(s_lg, past(c - 2))
                pe_rows(pe, st, c, w_g[:], NE)
            pe.wait_ge(s_dve1, DVE1["onehot"])
            hot = rt[:, 2].rearrange("p b e -> p (b e)")
            pe.matmul(bank[6][:, 0:P], C["before"], hot, start=True, stop=True)
            pe.matmul(bank[7][:, 0:P], ones_sq[:], hot, start=True, stop=True).then_inc(s_pe1, 1)

        def expert(pe, n):
            return pe.value_load(etab[0:1, bass.ds(n - B, 1)] if not isinstance(n, int) else etab[0:1, n - B:n - B + 1],
                                 min_val=0, max_val=NE - 1)

        def wslice(e, at, n):
            if isinstance(e, int):
                return wmoe[:, e, at:at + n]
            return wmoe[:].rearrange("p e w -> p (e w)")[:, bass.ds(e * (3 * FF) + at, n)]

        def pe_tileT(pe, n, u, turn):
            pe.wait_ge(s_rl[u], past_dma(turn))
            pe.wait_ge(s_xs, past(n - 1))
            pe.transpose(bank[6][:, 0:P], xr[:, u, :], ident).then_inc(s_xtp, 1)

        def pe_up(pe, n, u, shared):
            pe.wait_ge(s_xs, past(n))
            pe.wait_ge(s_gl, past(n - 2))
            pe.wait_ge(s_g, past(n - 2))
            e = NE if shared else expert(pe, n)
            pe.matmul(bank[u][:], xs[:, u, :], wslice(e, 0, FF), start=True, stop=True)
            pe.matmul(bank[2 + u][:], xs[:, u, :], wslice(e, FF, FF), start=True, stop=True).then_inc(s_h, 1)

        def pe_gT(pe, n, u):
            pe.wait_ge(s_g, past(n))
            pe.wait_ge(s_gt, past(n - 2))
            for f in range(FK):
                mm = pe.transpose(bank[4 + u][:, f * P:(f + 1) * P], gl[:, u, f * P:(f + 1) * P], ident)
            mm.then_inc(s_gtp, 1)

        def pe_down(pe, n, u, shared):
            pe.wait_ge(s_gt, past(n))
            pe.wait_ge(s_yo, past(n - 1))
            e = NE if shared else expert(pe, n)
            for f in range(FK):
                mm = pe.matmul(bank[7][:, 0:P], gT[:, u, f * P:(f + 1) * P], wslice(e, 2 * FF + f * P, P),
                               start=(f == 0), stop=(f == FK - 1))
            mm.then_inc(s_o, 1)

        def moe_pe(pe):
            def step(j, u, turn, up, down):
                if up is not None:
                    pe_up(pe, j + 1, 1 - u, up)
                if down is not None:
                    pe_down(pe, j - 1, 1 - u, down)
                pe_gT(pe, j, u)
            pe.wait_ge(s_dve1, DVE1["prefix_read"])
            pe_tileT(pe, 0, 0, 0)
            pe_tileT(pe, 1, 1, 0)
            pe_up(pe, 0, 0, True)
            step(0, 0, 0, True, None)
            pe_tileT(pe, 2, 0, 1)
            with pe.Fori(0, (B - 2) // 2) as i:
                step(i * 2 + 1, 1, i, True, True)
                pe_tileT(pe, i * 2 + 3, 1, i + 1)
                step(i * 2 + 2, 0, i, True, True)
                pe_tileT(pe, i * 2 + 4, 0, i + 2)
            pe.wait_ge(s_dve1, DVE1["route"])
            step(B - 1, 1, 0, False, True)
            pe_tileT(pe, B + 1, 1, (B + 1) // 2)
            step(B, 0, 0, False, True)
            pe_tileT(pe, B + 2, 0, (B + 2) // 2)
            with pe.Fori(0, (NX - 3) // 2) as i:
                step(i * 2 + (B + 1), 1, i, False, False)
                pe_tileT(pe, i * 2 + (B + 3), 1, i + (B + 2) // 2)
                step(i * 2 + (B + 2), 0, i, False, False)
                pe_tileT(pe, i * 2 + (B + 4), 0, i + (B + 4) // 2)
            step(NT - 2, 1, 0, False, False)
            step(NT - 1, 0, 0, None, False)
            pe_down(pe, NT - 1, 0, False)

        def act_tile(act, n, u):
            act.wait_ge(s_xtp, past(n))
            act.activation(xs[:, u, :], bank[6][:, 0:P], ACT.Copy).then_inc(s_xs, 1)

        def act_gelu(act, n, u):
            act.wait_ge(s_h, past(n))
            act.wait_ge(s_gtp, past(n - 2))
            act.activation(gl[:, u, :], bank[u][:], ACT.Gelu).then_inc(s_gl, 1)

        def moe_act(act):
            columns_act(act, ST_MOE)
            act_tile(act, 0, 0)
            act_tile(act, 1, 1)
            act_gelu(act, 0, 0)
            with act.Fori(0, (NT - 3) // 2) as i:
                for k in range(2):
                    act_gelu(act, i * 2 + (k + 1), 1 - k)
                    act_tile(act, i * 2 + (k + 2), k)
            act_gelu(act, NT - 2, 1)
            act_tile(act, NT - 1, 0)
            act_gelu(act, NT - 1, 0)

        def moe_dve(dve, ch):
            def mul(n, u):
                dve.wait_ge(s_gl, past(n))
                dve.tensor_tensor(gl[:, u, :], gl[:, u, :], bank[2 + u][:], ALU.mult).then_inc(s_g, 1)

            def copyT(n, u):
                dve.wait_ge(s_gtp, past(n))
                dve.wait_ge(s_o, past(n - 2))
                dve.tensor_copy(gT[:, u, :], bank[4 + u][:]).then_inc(s_gt, 1)

            def down(n, u, turn):
                dve.wait_ge(s_o, past(n))
                dve.wait_ge(s_yst[u], past_dma(turn - 1))
                dve.tensor_copy(yo[:, u, :], bank[7][:, 0:P]).then_inc(s_yo, 1)
            mul(0, 0)
            mul(1, 1)
            copyT(0, 0)
            with dve.Fori(0, (NT - 3) // 2) as i:
                mul(i * 2 + 2, 0)
                down(i * 2, 0, i)
                copyT(i * 2 + 1, 1)
                mul(i * 2 + 3, 1)
                down(i * 2 + 1, 1, i)
                copyT(i * 2 + 2, 0)
            mul(NT - 1, 0)
            down(NT - 3, 0, NT // 2 - 1)
            copyT(NT - 2, 1)
            down(NT - 2, 1, NT // 2 - 1)
            copyT(NT - 1, 0)
            down(NT - 1, 0, NT // 2)
            dve.wait_ge(s_ysh, 16)
            dve.wait_ge(s_gath, 16 * B)
            for c in range(NC):
                xc = xall[:, c * CB:(c + 1) * CB, :]
                ch.step(dve.tensor_tensor(xc, xc, yshared[:, c * CB:(c + 1) * CB, :], ALU.add))
                for k in range(CB):
                    b = c * CB + k
                    dve.tensor_tensor(xnew[:], x_sb[:, b, :], xall[:, b, :], ALU.add).then_inc(s_xup, 1)
                    dve.wait_ge(s_xup, past(upd(ST_MOE, b)))
                    dve_stats(dve, ch, b)

        def moe_sp(sp):
            for c in range(NC):
                sp.wait_ge(s_xn, past(tjob(ST_MOE, c) - NC))
                sp.dma_start(rows_dram[c * CB:(c + 1) * CB].rearrange("b t d -> t b d"),
                             xall[:, c * CB:(c + 1) * CB, :]).then_inc(s_rows, 16)
            sp.wait_ge(s_rows, 16 * NC)

            def load(n, u):
                sp.wait_ge(s_xtp, past(n - 2))
                sp.sem_inc(s_sp, 1)
                sp.dma_start(xr[:, u, :], rows_dram[n]).then_inc(s_rl[u], 16)

            def store(n, u):
                sp.wait_ge(s_yo, past(n))
                sp.sem_inc(s_sp, 1)
                sp.dma_start(y_dram[bass.ds(n * P, P)] if not isinstance(n, int) else y_dram[n * P:(n + 1) * P],
                             yo[:, u, :]).then_inc(s_yst[u], 16)
            load(0, 0)
            load(1, 1)
            load(2, 0)
            load(3, 1)
            with sp.Fori(0, (B - 4) // 2) as i:
                for u in range(2):
                    load(i * 2 + (u + 4), u)
                    store(i * 2 + u, u)
            sp.wait_ge(s_scat, 16 * B)
            with sp.Fori((B - 4) // 2, (NT - 5) // 2) as i:
                for u in range(2):
                    load(i * 2 + (u + 4), u)
                    store(i * 2 + u, u)
            load(NT - 1, 0)
            for n in range(NT - 5, NT):
                store(n, n % 2)
            for u, n in ((0, NT // 2), (1, NT // 2 - 1)):
                sp.wait_ge(s_yst[u], past_dma(n))
            sp.dma_start(yshared[:], y_dram[0:B * P].rearrange("(b t) d -> t b d", t=P)).then_inc(s_ysh, 16)

        def moe_pool(pool):
            pool.wait_ge(s_dve1, DVE1["route"])
            pool.wait_ge(s_zero, 32)
            for b in range(B):
                pool.indirect_dma_start(rows_dram.rearrange("n t d -> (n t) d"),
                                        bass.IndirectOffsetOnAxis(ap=pos[:, b:b + 1], axis=0),
                                        xall[:, b, :], None).then_inc(s_scat, 16)
            pool.wait_ge(s_scat, 16 * B)
            pool.wait_ge(s_rows, 16 * NC)
            for u, n in ((0, NT // 2), (1, NT // 2 - 1)):
                pool.wait_ge(s_yst[u], past_dma(n))
            for b in range(B):
                pool.indirect_dma_start(xall[:, b, :], None, y_dram,
                                        bass.IndirectOffsetOnAxis(ap=pos[:, b:b + 1], axis=0)).then_inc(s_gath, 16)

        def bit_dve(dve, ch):
            st = ST_BIT
            dve_rstd(dve, ch, norm(st))
            ch.step(dve.tensor_copy(rs1[:], rstd[:]))
            ch.step(dve.tensor_tensor(vareps[:], mv[:, :, 1], rs1[:], ALU.mult))
            ch.step(dve.tensor_tensor(vareps[:], vareps[:], rs1[:], ALU.mult))
            dve.tensor_scalar(vareps[:], vareps[:], 1e-5, None, ALU.add).then_inc(s_var, 1)
            dve.wait_ge(s_rstd, past(norm(st) + 1))
            ch.step(dve.tensor_tensor(rs1[:], rs1[:], rstd[:], ALU.mult))

            def quant_scales(q, wm):
                ch.step(dve.tensor_scalar(q[:, 0], q[:, 0], 1e-5, None, ALU.max))
                ch.step(dve.reciprocal(q[:, 1], q[:, 0]))
                ch.step(dve.tensor_scalar(q[:, 1], q[:, 1], 127.0, None, ALU.mult))
                ch.step(dve.tensor_scalar(q[:, 2], q[:, 0], 1.0 / 127, wm, ALU.mult, ALU.mult))

            def rows(c):
                u = c % 2
                q = bq[:, u]
                xc = xn[:, u]
                for k in range(CB):
                    b = c * CB + k
                    ins = dve.tensor_scalar(xc[:, k, :], x_sb[:, b, :], mv[:, b, 0:1], rs1[:, b:b + 1],
                                            ALU.subtract, ALU.mult)
                ch.step(ins)
                ch.step(dve.tensor_reduce(q[:, 0], xc, AX.X, ALU.max, apply_absolute_value=True))
                quant_scales(q, bsc[:, 2:3])
                for k in range(CB):
                    ins = dve.tensor_scalar(xc[:, k, :], xc[:, k, :], q[:, 1, k:k + 1], 127.0, ALU.mult, ALU.min)
                ch.step(ins)
                ch.step(dve.tensor_scalar(xc, xc, -128.0, MAGIC, ALU.max, ALU.add))
                dve.wait_ge(s_tr, past(tjob(st, c) - 2))
                dve.tensor_scalar(xq[:, u], xc, MAGIC, None, ALU.subtract).then_inc(s_xn, 1)

            def inner(c):
                u = c % 2
                q = bq[:, u]
                for k in range(CB):
                    n = c * CB + k
                    dve.wait_ge(s_bh, past(n))
                    dve.scalar_tensor_tensor(out=hg[:, u, k, :], in0=bank[2 + n % 2][:], scalar=q[:, 2, k:k + 1],
                                             in1=b1row[:], op0=ALU.mult, op1=ALU.add).then_inc(s_bb, 1)
                for k in range(CB):
                    n = c * CB + k
                    dve.wait_ge(s_bg, past(n))
                    dve.tensor_reduce(q[:, 3, k:k + 1], hg[:, u, k, :], AX.X, ALU.max, apply_absolute_value=True)
                dve.wait_ge(s_bsq, past(c * CB + CB - 1))
                dve.tensor_scalar(q[:, 5], q[:, 4], 1.0 / FF, 1e-5, ALU.mult, ALU.add).then_inc(s_bms, 1)
                dve.wait_ge(s_bpw, past(c))
                ch.step(dve.tensor_tensor(q[:, 0], q[:, 3], q[:, 6], ALU.mult))
                quant_scales(q, bsc[:, 3:4])
                ch.step(dve.tensor_tensor(q[:, 1], q[:, 1], q[:, 6], ALU.mult))

            def outer(c):
                u = c % 2
                q = bq[:, u]

                def quant(k):
                    hk = hg[:, u, k, :]
                    ch.step(dve.tensor_scalar(hk, hk, q[:, 1, k:k + 1], 127.0, ALU.mult, ALU.min))
                    dve.tensor_scalar(hk, hk, -128.0, MAGIC, ALU.max, ALU.add).then_inc(s_bq, 1)

                def update(k):
                    n = c * CB + k
                    dve.wait_ge(s_bo, past(n))
                    ch.step(dve.scalar_tensor_tensor(out=xall[:, n, :], in0=bank[6 + n % 2][:, 0:P],
                                                     scalar=q[:, 2, k:k + 1], in1=x_sb[:, n, :],
                                                     op0=ALU.mult, op1=ALU.add))
                    dve.tensor_tensor(xall[:, n, :], xall[:, n, :], b2row[:], ALU.add).then_inc(s_bx, 1)
                quant(0)
                quant(1)
                for k in range(CB):
                    update(k)
                    if k + 2 < CB:
                        quant(k + 2)
            for c in range(NC):
                rows(c)
                inner(c)
                outer(c)

        def bit_pe(pe):
            st = ST_BIT
            for c in range(NC):
                u = c % 2
                t = tjob(st, c)
                pe.wait_ge(s_xn, past(t - NC))
                pe.wait_ge(s_xT, past(t - 2))
                o = bank[u][:, 0:CW // 2].bitcast(BF16)
                for k in range(CB):
                    mm = pe.transpose(o[:, k * P:(k + 1) * P], xq[:, u, k, :], identb[:])
                mm.then_inc(s_tr, 1)
                pe.wait_ge(s_xT, past(t))
                for k in range(CB):
                    n = c * CB + k
                    pe.wait_ge(s_bb, past(n - 2))
                    pe.matmul(bank[2 + n % 2][:], xqT[:, u, k * P:(k + 1) * P], w1T[:], start=True, stop=True).then_inc(s_bh, 1)
                for k in range(CB):
                    n = c * CB + k
                    v = n % 2
                    pe.wait_ge(s_bqb, past(n))
                    pe.wait_ge(s_bt, past(n - 2))
                    o = bank[4 + v][:, 0:FF // 2].bitcast(BF16)
                    for f in range(FK):
                        mm = pe.transpose(o[:, f * P:(f + 1) * P], hq[:, v, f * P:(f + 1) * P], identb[:])
                    mm.then_inc(s_btp, 1)
                    pe.wait_ge(s_bt, past(n))
                    pe.wait_ge(s_bx, past(n - 2))
                    for f in range(FK):
                        mm = pe.matmul(bank[6 + v][:, 0:P], hqT[:, v, f * P:(f + 1) * P], w2T[:, f * P:(f + 1) * P],
                                       start=(f == 0), stop=(f == FK - 1))
                    mm.then_inc(s_bo, 1)

        def bit_act(act):
            st = ST_BIT
            for c in range(NC):
                u = c % 2
                act.wait_ge(s_tr, past(tjob(st, c)))
                act.activation(xqT[:, u, :], bank[u][:, 0:CW // 2].bitcast(BF16), ACT.Copy).then_inc(s_xT, 1)
                for k in range(CB):
                    n = c * CB + k
                    act.wait_ge(s_bb, past(n))
                    act.activation(hg[:, u, k, :], hg[:, u, k, :], ACT.Gelu).then_inc(s_bg, 1)
                    act.wait_ge(s_bg, past(n))
                    act.activation(h1[:, 0, :], hg[:, u, k, :], ACT.Square,
                                   accum_out=bq[:, u, 4, k:k + 1]).then_inc(s_bsq, 1)
                for k in range(CB):
                    n = c * CB + k
                    v = n % 2
                    act.wait_ge(s_bq, past(n))
                    act.wait_ge(s_btp, past(n - 2))
                    act.activation(hq[:, v, :], hg[:, u, k, :], ACT.Copy, bias=-MAGIC).then_inc(s_bqb, 1)
                    act.wait_ge(s_btp, past(n))
                    act.activation(hqT[:, v, :], bank[4 + v][:, 0:FF // 2].bitcast(BF16), ACT.Copy).then_inc(s_bt, 1)

        def bit_pool(pool):
            for c in range(NC):
                q = bq[:, c % 2]
                pool.wait_ge(s_bms, past(c))
                pool.tensor_tensor(q[:, 6], q[:, 5], neg_half[:, 0:CB], ALU.pow).then_inc(s_bpw, 1)


        @block.sync
        def _(sp):
            sp.dma_start(cst[:], I["consts"]).then_inc(s_cst, 16)
            sp.dma_start(x_sb[:], I["x"].rearrange("b t d -> t b d")).then_inc(s_x, 16)
            for t, s in loads[0::2]:
                sp.dma_start(t, s).then_inc(s_w, 16)
            with sp.Fori(0, NC // 2) as i:
                for u in range(2):
                    c = i * 2 + u
                    sp.wait_ge(s_tr, past(tjob_ctx(c) - 2))
                    sp.sem_inc(s_sp, 1)
                    sp.dma_start(ctx_in[:, u], chunk_dram(I["ctx_1024"], c).rearrange("b t d -> t b d")).then_inc(s_ctx[u], 16)
                    for l in range(3):
                        n = kjob(c, l)
                        v, half_n = (3 * u + l) % 2, 3 * i + (3 * u + l) // 2
                        sp_store(sp, n, half_n, v, True, k_dram[l][c])
                        sp.wait_ge(s_vb, past(n))
                        sp.sem_inc(s_sp, 1)
                        sp.dma_start(chunk_dram(v_dram[l], c).rearrange("b t w -> t b w"),
                                     v_out[:, v].rearrange("p b h w -> p b (h w)")).then_inc(s_vst[v], 16)
            for v in range(2):
                sp.wait_ge(s_stored[v], past_dma(kjob(NC - 1, 2) // 2, 6))
                sp.wait_ge(s_vst[v], past_dma(kjob(NC - 1, 2) // 2))
            attention_sp(sp, 0)
            corr_sp(sp)
            attention_sp(sp, 1)
            moe_sp(sp)
            attention_sp(sp, 2)
            sp.wait_ge(s_done, 1)
            sp.wait_ge(s_w1, 16 * len(loads1))
            sp.wait_ge(s_w5, 16 * len(loads5))
            sp.wait_ge(s_w7, 16 * len(loads7))
            sp.dma_start(out.rearrange("b t d -> t b d"), xall[:]).then_inc(s_out, 16)
            sp.wait_ge(s_out, 16)

        @block.gpsimd
        def _(pool):
            pool.memset(xall[:], 0.0).then_inc(s_const, 1)
            pool.wait_ge(s_const, 1)
            pool.dma_start(rows_dram[B:NT].rearrange("n t d -> t n d")[:, 0:B], xall[:]).then_inc(s_zero, 16)
            pool.dma_start(rows_dram[2 * B:NT].rearrange("n t d -> t n d"), xall[:, 0:NX - B]).then_inc(s_zero, 16)
            for s, per in s_lead:
                pool.sem_inc(s, LEAD * per)
            pool.memset(neg_half[:], -0.5).then_inc(s_const, 1)
            pool.memset(eps6[:], 1e-6).then_inc(s_const, 1)
            pool.memset(ones_row[:], 1.0).then_inc(s_const, 1)
            pool.memset(ones_sq[:], 1.0).then_inc(s_const, 1)
            pool.memset(mean_sq[:], 1.0 / (B * HD)).then_inc(s_const, 1)
            pool.memset(v_out[:], 1.0).then_inc(s_const, 1)
            pool.memset(mpad[:], 0.0).then_inc(s_const, 1)
            pool.wait_ge(s_const, 8)
            pool.wait_ge(s_zero, 32)
            for k in range(norm(ST_BIT) + 2):
                pool_rstd(pool, k)
                if k == norm(ST_MOE):
                    moe_pool(pool)
            bit_pool(pool)

        @block.scalar
        def _(act):
            for t, s in loads[1::2]:
                act.dma_start(t, s).then_inc(s_w, 16)
            for t, s in loads1:
                act.dma_start(t, s).then_inc(s_w1, 16)
            for t, s in loads5:
                act.dma_start(t, s).then_inc(s_w5, 16)
            for t, s in loads7:
                act.dma_start(t, s).then_inc(s_w7, 16)
            act.wait_ge(s_wprep, 1)
            act.wait_ge(s_const, 8)
            with act.Fori(0, NC // 2) as i:
                for u in range(2):
                    c = i * 2 + u
                    act.wait_ge(s_tr, past(tjob_ctx(c)))
                    act.wait_ge(s_vp, past(kjob(c, 2) - 6))
                    act.activation(xT[:, u, :], bank[u][:], ACT.Copy).then_inc(s_xT, 1)
                    for l in range(3):
                        n = kjob(c, l)
                        bias = None if l == 0 else colbias[:, 2 * l + 1:2 * l + 2]
                        act_split(act, n, 3 * i + (3 * u + l) // 2, (3 * u + l) % 2, True, bias, c if l == 0 else None)
            attention_act(act, 0)
            columns_act(act, ST_FFN0)
            corr_act(act)
            twist_act(act)
            attention_act(act, 1)
            moe_act(act)
            attention_act(act, 2)
            bit_act(act)

        @block.vector
        def _(dve):
            ch = Chain(dve, s_dve)
            dve.wait_ge(s_cst, 16)
            dve.tensor_copy(identb[:], ident)
            dve.tensor_copy(selb[:].rearrange("p h t -> p (h t)"), C["sel"])
            dve.wait_ge(s_x, 16)
            with dve.Fori(0, B) as i:
                ch.loop(i, 3)
                ch.step(dve.tensor_copy(xnew[:], x_sb[:, i, :]))
                dve_stats(dve, ch, i)
            ch.end(B)
            dve.wait_ge(s_w, 16 * len(loads))
            for l in range(2):
                for w, k in ((wq, 0), (wk, 1)):
                    dve.tensor_copy(w[:, l, :].rearrange("p (half d h) -> p half d h", half=2, d=8),
                                    wraw[:, 4 * l + k, :].rearrange("p (h half d) -> p half d h", half=2, d=8))
            dve.wait_ge(s_wt, 1)
            for w, k in ((wq, 0), (wk, 1)):
                dve.tensor_copy(w[:, 2, :].rearrange("p (half d h) -> p half d h", half=2, d=8),
                                bank[0][:, k * P:(k + 1) * P].rearrange("p (h half d) -> p half d h", half=2, d=8))
            dve.tensor_copy(wvo3[:].rearrange("p k n -> p (k n)"), bank[0][:, 2 * P:4 * P])
            dve.tensor_copy(colbias[:, 0:6], bank[1][:, 0:6]).then_inc(s_wprep, 1)
            with dve.Fori(0, NC // 2) as i:
                for u in range(2):
                    c = i * 2 + u
                    dve.wait_ge(s_k1p, past(c))
                    dve.tensor_tensor(k1[:, bass.ds(c * (CB * HD), CB * HD)].rearrange("p (b d) -> p b d", d=HD),
                                      bank[5][:, 0:CB * HD].rearrange("p (b d) -> p b d", d=HD),
                                      over(bq_c[:], CB), ALU.add).then_inc(s_k1, 1)
                    for l in range(3):
                        n = kjob(c, l)
                        v = (3 * u + l) % 2
                        bias = None if l == 0 else colbias[:, 2 * l + 1:2 * l + 2]
                        dve_split(dve, n, v, True, bias, c if l == 0 else None, colbias[:, 1:2])
                        dve.wait_ge(s_vp, past(n))
                        dve.wait_ge(s_vst[v], past_dma(3 * i + (3 * u + l) // 2 - 1))
                        src = bank[6 + v][:].rearrange("p (b h d) -> p b h d", b=CB, d=HD)
                        for k in range(CB):
                            o = v_out[:, v, k, :, 0:HD]
                            s = bank[6 + v][:, k * P:(k + 1) * P].rearrange("p (h d) -> p h d", d=HD)
                            if l == 0:
                                ins = dve.tensor_copy(o, s)
                            else:
                                ins = dve.tensor_tensor(o, s, bvrow[:, l, :].rearrange("p (h d) -> p h d", d=HD), ALU.add)
                        ins.then_inc(s_vb, 1)
            attention_dve(dve, ch, 0)
            ffn0_dve(dve, ch)
            corr_dve(dve, ch)
            dve.wait_ge(s_w1, 16 * len(loads1))
            twist_dve(dve, ch)
            attention_dve(dve, ch, 1)
            bitw_dve(dve, ch)
            moe_route_dve(dve, ch)
            moe_dve(dve, ch)
            attention_dve(dve, ch, 2)
            bit_dve(dve, ch)
            dve.drain().then_inc(s_done, 1)

        @block.tensor
        def _(pe):
            pe.wait_ge(s_cst, 16)
            pe.wait_ge(s_w, 16 * len(loads))
            for k in range(4):
                pe.transpose(bank[0][:, k * P:(k + 1) * P], wraw[:, 8 + k, :], ident)
            pe.matmul(bank[1][:, 2:6], C["perm"], colraw[:, 2:6], start=True, stop=True)
            pe.matmul(bank[1][:, 0:2], C["spread_d"][0:HD, :], colraw[0:HD, 0:2], start=True, stop=True).then_inc(s_wt, 1)
            pe.wait_ge(s_wprep, 1)
            with pe.Fori(0, NC // 2) as i:
                for u in range(2):
                    c = i * 2 + u
                    pe.wait_ge(s_ctx[u], 16 * (i + 1))
                    pe.wait_ge(s_xT, past(tjob_ctx(c) - 2))
                    for k in range(CB):
                        mm = pe.transpose(bank[u][:, k * P:(k + 1) * P], ctx_in[:, u, k, :], ident)
                    mm.then_inc(s_tr, 1)
                    pe.wait_ge(s_xT, past(tjob_ctx(c)))
                    pe.wait_ge(s_k1, past(c - 1))
                    for k in range(CB):
                        mm = pe.matmul(bank[5][:, k * HD:(k + 1) * HD], xT[:, u, k * P:(k + 1) * P], w_c[:],
                                       start=True, stop=True)
                    mm.then_inc(s_k1p, 1)
                    for l in range(3):
                        n = kjob(c, l)
                        v = (3 * u + l) % 2
                        pe_project(pe, n, v, wk[:, l, :], xT[:, u, :])
                        if l == 0:
                            pe_meansq(pe, c)
                        pe.wait_ge(s_vb, past(n - 2))
                        for k in range(CB):
                            mm = pe.matmul(bank[6 + v][:, k * P:(k + 1) * P], xT[:, u, k * P:(k + 1) * P], wv(l),
                                           start=True, stop=True)
                        mm.then_inc(s_vp, 1)
            attention_pe(pe, 0)
            ffn0_pe(pe)
            corr_pe(pe)
            pe.wait_ge(s_w1, 16 * len(loads1))
            twist_pe(pe)
            attention_pe(pe, 1)
            bitw_pe(pe)
            pe.wait_ge(s_w5, 16 * len(loads5))
            moe_route_pe(pe)
            moe_pe(pe)
            attention_pe(pe, 2)
            bit_pe(pe)


def kernel(**inputs):
    import concourse.bacc as _bacc
    from concourse.bass_utils import run_bass_kernel_spmd as _run

    nc = _bacc.Bacc("TRN2", target_bir_lowering=False, num_devices=1)
    arrays, aps = {}, {}
    arrays["consts"] = np.concatenate([CONSTS[k] for k in CORDER], axis=1)
    for name, a in inputs.items():
        arrays[name] = np.ascontiguousarray(a)
    for name, a in arrays.items():
        aps[name] = nc.dram_tensor(f"in_{name}", a.shape, mybir.dt.from_np(a.dtype), kind="ExternalInput").ap()
    out = nc.dram_tensor("out_x", (B, P, P), F32, kind="ExternalOutput").ap()
    build_program(nc, aps, out)
    r = _run(nc, [{f"in_{k}": v for k, v in arrays.items()}], core_ids=[0])
    return r.results[0]["out_x"]
```

```python
from contextlib import ExitStack

import numpy as np

import concourse.bass as bass
from concourse import mybir

ALU = mybir.AluOpType
ACT = mybir.ActivationFunctionType
AX = mybir.AxisListType
F32 = mybir.dt.float32
BF16 = mybir.dt.bfloat16
I32 = mybir.dt.int32
U32 = mybir.dt.uint32

P = 128
B = 16
H, HD = 16, 8
CB = 4
NC = B // CB
CW = CB * P
GH = 4
NG = H // GH
VW = HD + 1
OW = P // GH
NE = 8
FF = 512
FK = FF // P
NX = B + NE - 1
NT = B + NX
EPS = 1e-5
NS = 4
LEAD = 16


def upd(st, b):
    return B * st + b


def past(n):
    return n + 1 + LEAD


def past_dma(n, dmas=1):
    return 16 * dmas * (n + 1 + LEAD)


def slots(g):
    return [(g % 2, GH * (g // 2) + j) for j in range(GH)]


def block_of(g):
    return 2 * (g % 2) + g // 2


class Chain:

    def __init__(self, eng, sem):
        self.eng, self.sem, self.done = eng, sem, 0
        self.it, self.per, self.at = None, 0, 0

    def step(self, ins):
        ins.then_inc(self.sem, 1)
        self.at += 1
        self.eng.wait_ge(self.sem, self.count())

    def count(self):
        if self.it is None:
            return self.done + self.at
        return self.it * self.per + (self.done + self.at)

    def loop(self, it, per):
        self.done += self.at
        self.it, self.per, self.at = it, per, 0

    def end(self, turns):
        assert self.at == self.per, (self.at, self.per)
        self.done += turns * self.per
        self.it, self.at = None, 0


def make_constants():
    c = {}
    eye = np.eye(P, dtype=np.float32)
    p = np.arange(P)
    c["ident"] = eye
    half, d, place = p // 64, (p % 64) // 8, p % 8
    head = 8 * half + place
    c["headmean"] = (head[:, None] == head[None, :]).astype(np.float32) / HD
    perm = np.zeros((P, P), np.float32)
    perm[head * HD + d, p] = 1.0
    c["perm"] = perm
    c["spread_d"] = np.zeros((P, P), np.float32)
    c["spread_d"][d, p] = 1.0
    sel = np.zeros((P, 8, P), np.float32)
    for h in range(2):
        for part in range(2):
            for k in range(8):
                sel[64 * h + 8 * part + k, k, :] = 1.0
    c["sel"] = sel.reshape(P, 8 * P)
    lag = (-p) % P
    c["tie"] = (lag[:, None] < lag[None, :]).astype(np.float32)
    c["mod8"] = (p[:, None] % HD == p[None, :] % HD).astype(np.float32)
    c["own_batch"] = (p[:, None] // HD == np.arange(B)[None, :]).astype(np.float32)
    tw = np.zeros((P, P), np.float32)
    for to, fr, s in ((0, 2, 1), (1, 3, -1), (2, 0, -1), (3, 1, 1)):
        for k in range(32):
            tw[32 * fr + k, 32 * to + k] = s
    c["twist"] = tw
    c["before"] = (p[:, None] < p[None, :]).astype(np.float32)
    c["first"] = np.broadcast_to(NE - np.arange(NE, dtype=np.float32), (P, NE))
    c["tile_rows"] = np.broadcast_to(P * np.arange(B, dtype=np.float32), (P, B))
    c["tile_no"] = np.broadcast_to(np.arange(NX, dtype=np.float32), (P, NX))
    return c


CONSTS = make_constants()
CORDER = list(CONSTS)
CEARLY = 4
CWIDTH = [CONSTS[k].shape[1] for k in CORDER]

ATT = {0: "L0_xattn", 1: "L2_xattn", 2: "L3_xattn"}
ST_ATT = (0, 4, 6)
ST_FFN0, ST_CORR, ST_TWIST, ST_MOE, ST_BIT = 1, 2, 3, 5, 7
K_TOP = int(2 * np.log(256))
CYCLES = 3
MAGIC = 12582912.0


def norm(st):
    return st if st <= ST_FFN0 else st + 1


def once(*names):
    return {name: i + 1 for i, name in enumerate(names)}


PE1 = once("wmean0", "amaxT", "amax", "qkT", "corrM", "corr", "rank", "rolled", "rolled_out",
           "g1", "g2", "g3", "bit_mean", "bit_wT", "prefix")
DVE1 = once("wabs0", "amax_col", "amax_row", "ternary0", "corr_in", "corr_T", "corr_mm", "corr_negmax",
            "corr_G", "corr_w", "rolled_sb", "gmean", "t_bias", "bit_abs", "bit_tern", "onehot", "prefix_read", "route")
ACT1 = once("corr_exp", "g1", "g2", "g3")


def build_program(nc, I, out):
    with ExitStack() as ctx:
        def sb(name, shape, dt=F32):
            return ctx.enter_context(nc.sbuf_tensor(name, shape, dt))

        def sem(name):
            return ctx.enter_context(nc.semaphore(name))

        def dram(name, shape, dt=F32):
            return nc.dram_tensor(name, shape, dt, kind="Internal").ap()

        bank = [ctx.enter_context(nc.psum_tensor(f"bank{i}", [P, 512], F32)) for i in range(8)]
        x_sb = sb("x_sb", [P, B, P])
        cst = sb("cst", [P, sum(CWIDTH)])
        C = {}
        at = 0
        for k, w in zip(CORDER, CWIDTH):
            C[k] = cst[:, at:at + w]
            at += w
        ident = C["ident"]
        identb = sb("identb", [P, P], BF16)
        selb = sb("selb", [P, 8, P], BF16)
        ones_row = sb("ones_row", [P, P])
        neg_half = sb("neg_half", [P, B])
        eps6 = sb("eps6", [P, 1])

        stats = sb("stats", [P, 6])
        stats_all = sb("stats_all", [P, B, 6])
        mv = sb("mv", [P, B, 2])
        mvnew = sb("mvnew", [P, 2])
        xnew = sb("xnew", [P, P])
        vareps = sb("vareps", [P, B])
        rstd = sb("rstd", [P, B])
        xn = sb("xn", [P, 2, CB, P])
        xT = sb("xT", [P, 2, CW])

        ctx_in = sb("ctx_in", [P, 2, CB, P])
        wraw = sb("wraw", [P, 12, P])
        wq = sb("wq", [P, 3, P])
        wk = sb("wk", [P, 3, P])
        wvo3 = sb("wvo3", [P, 2, P])
        colraw = sb("colraw", [P, 8])
        colbias = sb("colbias", [P, 8])
        bvrow = sb("bvrow", [P, 3, P])
        borow = sb("borow", [P, 3, P])

        sq = sb("sq", [P, CW])
        resid = sb("resid", [P, 2, CW])
        parts = sb("parts", [P, 2, 3, CW], BF16)
        v_out = sb("v_out", [P, 2, CB, H, VW])

        stk = sb("stk", [P, NS, 2, 8, P], BF16)
        qstk, kstk = stk[:, :, 0], stk[:, :, 1]
        v_in = sb("v_in", [P, NS, H, VW])
        negm = sb("negm", [P, 2, 2, 8])
        mpad = sb("mpad", [P, 2, P], BF16)
        mT = sb("mT", [P, 2, P], BF16)
        probs = sb("probs", [P, NG, GH * P])
        o_sb = sq
        rden = sb("rden", [P, H])
        att = sb("att", [P, 2, P])
        attT = sb("attT", [P, 2, P])

        xall = sb("xall", [P, B, P])
        rs1 = sb("rs1", [P, B])
        lnrow = sb("lnrow", [P, 2, P])
        w_f0 = sb("w_f0", [P, P])
        w_t0 = sb("w_t0", [P, 2, P])
        amax = sb("amax", [P, NC])
        sc = sb("sc", [P, 16])
        ones_sq = sb("ones_sq", [P, P])
        mean_sq = sb("mean_sq", [P, P])
        w_c = sb("w_c", [P, HD])
        bq_c = sb("bq_c", [P, HD])
        wout_c = sb("wout_c", [P, P])
        bout_c = sb("bout_c", [P, P])
        q1 = sb("q1", [P, P])
        k1 = sb("k1", [P, P])
        qk1T = sb("qk1T", [P, 2, P])
        mm2 = sb("mm2", [P, 2, P])
        skew = sb("skew", [P, P])
        crow = sb("crow", [P, P])
        cwork = sb("cwork", [P, 3, P])
        rolled = sb("rolled", [P, P])
        ymask = sb("ymask", [P, 2, CB, P])
        w_cn = sb("w_cn", [P, P + 64 + 32 + P])
        w_gc = sb("w_gc", [P, 64 + 32 + P])
        b_l1 = sb("b_l1", [P, 8])
        w4c = sb("w4c", [32, 2])
        tbuf = sb("tbuf", [P, 4, CW])
        h1, tf = tbuf[:, 0:2], tbuf[:, 2:4]
        h2 = sb("h2", [64, 2, CW])
        h3 = ctx_in[0:32].rearrange("p u b d -> p u (b d)")
        tws = sb("tws", [P, 2, CW])
        gx = sb("gx", [P, 4, B])
        acoef = sb("acoef", [P, B])
        wmoe = sb("wmoe", [P, NE + 1, 3 * FF])
        w_g = sb("w_g", [P, NE])
        rt = sb("rt", [P, 8, B, NE])
        rs = sb("rs", [P, 6, B])
        rx = sb("rx", [P, NX * NE])
        etab = sb("etab", [P, NX], I32)
        pos = sb("pos", [P, B], U32)
        xr = sb("xr", [P, 2, P])
        xs = sb("xs", [P, 2, P])
        gl = tws
        gT = ymask[:].rearrange("p u b d -> p u (b d)")
        yo = sb("yo", [P, 2, P])
        yshared = tbuf[:].rearrange("p k (b d) -> p (k b) d", d=P)
        rows_dram = dram("rows_dram", [NT, P, P])
        y_dram = dram("y_dram", [NT * P, P])
        wb = sb("wb", [P, 2, FF])
        wbt = sb("wbt", [P, 2, FF], BF16)
        w1T = sb("w1T", [P, FF], BF16)
        w2T = sb("w2T", [P, FF], BF16)
        b1row = sb("b1row", [P, FF])
        b2row = sb("b2row", [P, P])
        bsc = sb("bsc", [P, 8])
        bq = sb("bq", [P, 2, 8, CB])
        free = wmoe[:].rearrange("p e w -> p (e w)")
        hg = free[:, 0:2 * CB * FF].rearrange("p (u k f) -> p u k f", u=2, k=CB)
        free = free[:, 2 * CB * FF:].bitcast(BF16)
        xq = free[:, 0:2 * CW].rearrange("p (u k d) -> p u k d", u=2, k=CB)
        xqT, hq, hqT = (free[:, k * 2 * CW:(k + 1) * 2 * CW].rearrange("p (u n) -> p u n", u=2) for k in (1, 2, 3))

        corr_dram = dram("corr_dram", [P, 2 * P])
        wlag_dram = dram("wlag_dram", [P, P])

        qk_dram = [dram(f"qk_stacks{l}", [2, NC, 6, CB, P, P], BF16) for l in range(3)]
        v_dram = [dram(f"v_rows{l}", [B, P, H * VW]) for l in range(3)]

        s_cst, s_cst2 = sem("s_cst"), sem("s_cst2")
        s_x, s_w, s_wmid = sem("s_x"), sem("s_w"), sem("s_wmid")
        s_ctx = [sem("s_ctx_even"), sem("s_ctx_odd")]
        s_const = sem("s_const")
        s_wt = sem("s_wt")
        s_wprep = sem("s_wprep")
        s_lead = []

        def item(name, per=1):
            s = sem(name)
            s_lead.append((s, per))
            return s

        s_var, s_rstd = item("s_var"), item("s_rstd")
        s_xn, s_tr, s_xT = item("s_xn"), item("s_tr"), item("s_xT")
        s_proj, s_hi, s_r1, s_mid, s_lo = item("s_proj"), item("s_hi"), item("s_r1"), item("s_mid"), item("s_lo")
        s_sq, s_ms, s_mse, s_inv, s_rms = item("s_sq"), item("s_ms"), item("s_mse"), item("s_inv"), item("s_rms")
        s_stored = [item("s_stored_even", 16 * 3), item("s_stored_odd", 16 * 3)]
        s_vp, s_vb = item("s_vp"), item("s_vb")
        s_vst = [item("s_vst_even", 16), item("s_vst_odd", 16)]
        s_stk = [item(f"s_stk{k}", 16 * 5) for k in range(NS)]
        s_sc, s_max, s_mparts, s_mtp, s_mt = item("s_sc"), item("s_max"), item("s_mparts"), item("s_mtp"), item("s_mt")
        s_xb = sem("s_xb")
        s_oc, s_or = item("s_oc"), item("s_or")
        s_st, s_exp, s_av, s_norm = item("s_st"), item("s_exp"), item("s_av"), item("s_norm")
        s_atp, s_atc, s_y, s_xup = item("s_atp"), item("s_atc"), item("s_y"), item("s_xup")
        s_done = sem("s_done")
        s_out = sem("s_out")
        s_rp = item("s_rp")
        s_k1p, s_k1 = item("s_k1p"), item("s_k1")
        s_pe1, s_dve1, s_act1 = sem("s_pe1"), sem("s_dve1"), sem("s_act1")
        s_skew = sem("s_skew")
        s_w5, s_w7, s_zero = sem("s_w5"), sem("s_w7"), sem("s_zero")
        s_rows, s_scat, s_gath, s_ysh = sem("s_rows"), sem("s_scat"), sem("s_gath"), sem("s_ysh")
        s_rl = [item("s_rl_even", 16), item("s_rl_odd", 16)]
        s_xtp, s_xs, s_h, s_gl, s_g, s_gtp, s_gt, s_o, s_yo = (
            item(f"s_moe_{k}") for k in ("xtp", "xs", "h", "gl", "g", "gtp", "gt", "o", "yo"))
        s_yst = [item("s_yst_even", 16), item("s_yst_odd", 16)]
        s_lg = item("s_lg")
        s_bh, s_bb, s_bg, s_bsq, s_bms, s_bpw, s_bq, s_bqb, s_btp, s_bt, s_bo, s_bx = (
            item(f"s_bit_{k}") for k in ("h", "b", "g", "sq", "ms", "pw", "q", "qb", "tp", "t", "o", "x"))
        s_w1 = sem("s_w1")
        s_c1, s_g1, s_c2, s_g2, s_c3, s_g3, s_c4, s_g4, s_cyc, s_twp, s_tws = (
            item(f"s_tw_{k}") for k in ("p1", "g1", "p2", "g2", "p3", "g3", "p4", "g4", "cyc", "twp", "tws"))
        s_dve = sem("s_dve")
        s_sp = sem("s_sp")

        block = ctx.enter_context(nc.Block())

        loads = []

        xcols = xall[:].rearrange("p b t -> p (b t)")
        CN = {1: w_cn[:, 0:P], 2: w_cn[:, P:P + 64], 3: w_cn[0:64, P + 64:P + 96], 4: w_cn[0:32, P + 96:2 * P + 96]}
        GC = {1: w_gc[:, 0:64], 2: w_gc[0:64, 64:96], 3: w_gc[0:32, 96:96 + P]}

        def col(name):
            return I[name].rearrange("(p a) -> p a", a=1)

        def row(name):
            return I[name].rearrange("(a n) -> a n", a=1)

        wsrc = [I["L0_xattn_Wq"], I["L0_xattn_Wkv"][:, 0:P], I["L0_xattn_Wkv"][:, P:2 * P], I["L0_xattn_Wproj"]]
        for l in (1, 2):
            wsrc += [I[f"{ATT[l]}_{w}"] for w in ("Wq", "Wk", "Wv", "Wo")]
        for i, s in enumerate(wsrc):
            loads.append((wraw[:, i, :], s))
        loads += [(colraw[0:HD, 0:1], col("L0_xattn_q_gamma")), (colraw[0:HD, 1:2], col("L0_xattn_k_gamma"))]
        for l in (1, 2):
            loads += [(colraw[:, 2 * l:2 * l + 1], col(f"{ATT[l]}_bq")),
                      (colraw[:, 2 * l + 1:2 * l + 2], col(f"{ATT[l]}_bk")),
                      (bvrow[:, l, :], row(f"{ATT[l]}_bv").broadcast_to([P, P]))]
        loads += [(w_c[:], I["L1_xattn_Wq"]), (bq_c[:], row("L1_xattn_bq").broadcast_to([P, HD]))]

        loads_mid = [(w_f0[:], I["L0_ffn_weight"]),
              (lnrow[:, 0, :], row("L0_ffn_ln_gamma").broadcast_to([P, P])),
              (lnrow[:, 1, :], row("L0_ffn_ln_beta").broadcast_to([P, P])),
              (wout_c[:], I["L1_xattn_Wout"]), (bout_c[:], row("L1_xattn_bout").broadcast_to([P, P]))]
        loads_mid += [(borow[:, l, :], row(f"{ATT[l]}_bo").broadcast_to([P, P])) for l in (1, 2)]
        loads1 = [(CN[1], I["L1_ffn_cn_w1"]), (CN[2], I["L1_ffn_cn_w2"]), (CN[3], I["L1_ffn_cn_w3"]),
                  (w4c[:, 0:1], I["L1_ffn_cn_w4"]), (w4c[:, 1:2], I["L1_ffn_gc_w3"]),
                  (GC[1], I["L1_ffn_gc_w1"]), (GC[2], I["L1_ffn_gc_w2"]),
                  (b_l1[:, 0:1], col("L1_ffn_cn_b1")), (b_l1[0:64, 1:2], col("L1_ffn_cn_b2")),
                  (b_l1[0:32, 2:3], col("L1_ffn_cn_b3")),
                  (b_l1[:, 3:4], row("L1_ffn_cn_b4").broadcast_to([P, 1])),
                  (b_l1[0:64, 4:5], col("L1_ffn_gc_b1")), (b_l1[0:32, 5:6], col("L1_ffn_gc_b2")),
                  (b_l1[:, 6:7], row("L1_ffn_gc_b3").broadcast_to([P, 1])),
                  (b_l1[:, 7:8], row("L1_ffn_adaptive_range").broadcast_to([P, 1]))]

        def w3rows(w):
            return w.rearrange("(k p) d -> p k d", p=P)

        def w3tile(e):
            return wmoe[:, e, 2 * FF:3 * FF].rearrange("p (k d) -> p k d", k=FK)

        loads5 = [(wmoe[:, NE, 0:FF], I["L2_ffn_w1s"]), (wmoe[:, NE, FF:2 * FF], I["L2_ffn_w2s"]),
                  (w3tile(NE), w3rows(I["L2_ffn_w3s"])), (w_g[:], I["L2_ffn_Wg"])]
        for e in range(NE):
            loads5 += [(wmoe[:, e, 0:FF], I["L2_ffn_W1"][e]), (wmoe[:, e, FF:2 * FF], I["L2_ffn_W2"][e]),
                       (w3tile(e), w3rows(I["L2_ffn_W3"][e]))]
        loads7 = [(wb[:, 0, :].rearrange("p (k d) -> p k d", k=FK), w3rows(I["L3_ffn_w1"])), (wb[:, 1, :], I["L3_ffn_w2"]),
                  (b1row[:], row("L3_ffn_b1").broadcast_to([P, FF])), (b2row[:], row("L3_ffn_b2").broadcast_to([P, P]))]

        def wv(l):
            return wraw[:, 4 * l + 2, :] if l < 2 else wvo3[:, 0, :]

        def wo(l):
            return wraw[:, 4 * l + 3, :] if l < 2 else wvo3[:, 1, :]

        K_ORDER = (1, 2, 0)

        def kjob(c, l):
            return c * 3 + K_ORDER.index(l)

        def qjob(l, c):
            return 3 * NC + l * NC + c

        def tjob_ctx(c):
            return c

        def tjob_q(l, c):
            return tjob(ST_ATT[l], c)

        def tjob(st, c):
            return NC * (1 + st) + c

        def pe_project(pe, n, ps, w, xs):
            pe.matmul(ps, w, xs, start=True, stop=True).then_inc(s_proj, 1)

        def pe_meansq(pe, m):
            pe.wait_ge(s_sq, past(m))
            pe.wait_ge(s_mse, past(m - 1))
            pe.matmul(bank[4][:], C["headmean"], sq[:], start=True, stop=True).then_inc(s_ms, 1)

        def act_square(act, n, ps, m):
            act.wait_ge(s_proj, past(n))
            act.wait_ge(s_ms, past(m - 1))
            act.activation(sq[:], ps, ACT.Square).then_inc(s_sq, 1)

        def act_root(act, n, m):
            act.wait_ge(s_ms, past(m))
            act.wait_ge(s_lo, past(n - 2))
            act.activation(resid[:, n % 2, :], bank[4][:], ACT.Sqrt, bias=eps6[:, 0:1]).then_inc(s_mse, 1)

        def act_hi(act, n, is_k, ps, bias, m=None):
            if m is None:
                act.wait_ge(s_proj, past(n))
            else:
                act.wait_ge(s_rms, past(m))
            act.wait_ge(s_stored[n % 2], past_dma(n // 2 - 1, 3))
            act.activation(parts[:, n % 2, 0 if is_k else 2, :], ps if m is None else resid[:, n % 2, :],
                           ACT.Identity, bias=0.0 if bias is None else bias).then_inc(s_hi, 1)

        def act_mid(act, n):
            act.wait_ge(s_r1, past(n))
            act.activation(parts[:, n % 2, 1, :], resid[:, n % 2, :], ACT.Identity).then_inc(s_mid, 1)

        def dve_heads(dve, n, ps, m, gamma):
            r = resid[:, n % 2, :]
            dve.wait_ge(s_mse, past(m))
            dve.reciprocal(r, r).then_inc(s_inv, 1)
            dve.wait_ge(s_inv, past(m))
            dve.scalar_tensor_tensor(out=r, in0=ps, scalar=gamma, in1=r, op0=ALU.mult, op1=ALU.mult).then_inc(s_rms, 1)

        def dve_r1(dve, n, is_k, ps, bias, m=None):
            r, hi = resid[:, n % 2, :], parts[:, n % 2, 0 if is_k else 2, :]
            dve.wait_ge(s_hi, past(n))
            if bias is None:
                dve.tensor_tensor(r, ps if m is None else r, hi, ALU.subtract).then_inc(s_r1, 1)
            else:
                dve.scalar_tensor_tensor(out=r, in0=ps, scalar=bias, in1=hi,
                                         op0=ALU.add, op1=ALU.subtract).then_inc(s_r1, 1)

        def dve_lo(dve, n, is_k):
            dve.wait_ge(s_mid, past(n))
            dve.tensor_tensor(parts[:, n % 2, 2 if is_k else 0, :], resid[:, n % 2, :], parts[:, n % 2, 1, :],
                              ALU.subtract).then_inc(s_lo, 1)

        def sp_store(sp, n, is_k, dst):
            u = n % 2
            sp.wait_ge(s_lo, past(n))
            for t0, k in ((0, 3), (3, 2), (5, 1)):
                k0 = 0 if is_k else 3 - k
                sp.dma_start(dst[t0:t0 + k].rearrange("k b p t -> p (k b) t"),
                             parts[:, u, k0:k0 + k, :].rearrange("p k (b t) -> p (k b) t", b=CB)
                             ).then_inc(s_stored[u], 16)

        def sp_load(sp, l, c, k):
            b = c * CB + k
            sp.wait_ge(s_av, past(NG * (B * l + b - NS) + NG - 1))
            sp.sem_inc(s_sp, 1)
            for half in range(2):
                for w in range(2):
                    sp.dma_start(stk[64 * half:64 * half + 48, k, w].rearrange("p h t -> p (h t)"),
                                 qk_dram[l][w, c, :, k, 64 * half:64 * half + 64].rearrange("s (d h) t -> s d (h t)", h=8)
                                 ).then_inc(s_stk[k], 16)
            sp.dma_start(v_in[:, k].rearrange("p h w -> p (h w)"), v_dram[l][b]).then_inc(s_stk[k], 16)

        def pe_scores(pe, l, b, k, turn, pair):
            U = NG * (B * l + b) + 2 * pair
            if pair == 0:
                pe.wait_ge(s_stk[k], past_dma(NC * l + turn, 5))
            pe.wait_ge(s_max, past(U - 1))
            for j in range(GH):
                for half in range(2):
                    h = GH * pair + j
                    r = slice(64 * half, 64 * half + 48)
                    mm = pe.matmul(bank[half][:, j * P:(j + 1) * P], qstk[r, k, h, :], kstk[r, k, h, :],
                                   start=True, stop=True)
                    if j == GH - 1:
                        mm.then_inc(s_sc, 1)

        def pe_maxT(pe, l, b, u):
            n = B * l + b
            pe.wait_ge(s_mparts, past(n))
            pe.wait_ge(s_mt, past(n - 1))
            pe.transpose(maxT_ps, mpad[:, u, :], identb[:]).then_inc(s_mtp, 1)

        def pe_scoresT(pe, l, b, k, u, pair):
            U = NG * (B * l + b) + 2 * pair
            if pair == 0:
                pe.wait_ge(s_mt, past(B * l + b))
            pe.wait_ge(s_exp, past(U - 1))
            for j in range(GH):
                h = GH * pair + j
                for half in range(2):
                    r = slice(64 * half, 64 * half + 48)
                    pe.matmul(bank[2 + half][:, j * P:(j + 1) * P], kstk[r, k, h, :], qstk[r, k, h, :],
                              start=True, stop=False)
                for half in range(2):
                    rm = slice(64 * half, 64 * half + 64)
                    mm = pe.matmul(bank[2 + half][:, j * P:(j + 1) * P], selb[rm, h, :], mT[rm, u, :],
                                   start=False, stop=True)
                    if j == GH - 1:
                        mm.then_inc(s_st, 1)

        def pe_values(pe, l, b, k, g):
            U = NG * (B * l + b) + g
            pe.wait_ge(s_exp, past(U))
            if g == 0:
                pe.wait_ge(s_oc, past(B * l + b - 1))
            blk = block_of(g)
            for j in range(GH):
                mm = pe.matmul(bank[4][OW * j:OW * j + VW, blk * P:(blk + 1) * P], v_in[:, k, GH * blk + j, :],
                               probs[:, g, j * P:(j + 1) * P], start=True, stop=True)
            mm.then_inc(s_av, 1)

        def pe_rows_of_heads(pe, l, b):
            n = B * l + b
            pe.wait_ge(s_oc, past(n))
            pe.wait_ge(s_norm, past(n - 1))
            for g in range(NG):
                mm = pe.transpose(bank[6][:, g * P:(g + 1) * P], o_sb[:, g * P:(g + 1) * P], ident)
            mm.then_inc(s_or, 1)

        def pe_attT(pe, l, b, u):
            n = B * l + b
            pe.wait_ge(s_norm, past(n))
            pe.wait_ge(s_xup, past(upd(ST_ATT[l], b) - 1))
            pe.transpose(attT_ps, att[:, u, :], ident).then_inc(s_atp, 1)

        def pe_outproj(pe, l, b, u):
            n = B * l + b
            pe.wait_ge(s_atc, past(n))
            pe.matmul(y_ps, attT[:, u, :], wo(l), start=True, stop=True).then_inc(s_y, 1)

        o_ps = bank[6][:].rearrange("p (h w) -> p h w", w=OW)
        maxT_ps = bank[5][:, 0:P // 2].bitcast(BF16)
        attT_ps = bank[7][:, 0:P]
        y_ps = bank[7][:, P:2 * P]

        def dve_max(dve, l, b, u, g):
            U = NG * (B * l + b) + g
            dve.wait_ge(s_sc, past(U))
            half, h0 = slots(g)[0]
            dve.tensor_reduce(negm[:, u, half, h0:h0 + GH], bank[g % 2][:].rearrange("p (h k) -> p h k", h=GH),
                              AX.X, ALU.max, negate=True).then_inc(s_max, 1)

        def dve_maxparts(dve, ch, l, b, u):
            dve.wait_ge(s_max, past(NG * (B * l + b) + NG - 1))
            mp = mpad[:, u, :].rearrange("p (half k h) -> p half k h", half=2, k=8)
            ch.step(dve.tensor_copy(mp[:, :, 0, :], negm[:, u]))
            dve.tensor_tensor(mp[:, :, 1, :], negm[:, u], mp[:, :, 0, :], ALU.subtract).then_inc(s_mparts, 1)

        def dve_norm(dve, ch, l, b, u):
            n = B * l + b
            dve.wait_ge(s_or, past(n))
            o = o_ps
            ch.step(dve.reciprocal(rden[:], o[:, :, HD]))
            dve.wait_ge(s_atp, past(n - 2))
            dve.tensor_tensor(att[:, u, :].rearrange("p (h d) -> p h d", d=HD), o[:, :, 0:HD],
                              rden[:].unsqueeze(2).broadcast_to([P, H, HD]), ALU.mult).then_inc(s_norm, 1)

        def dve_update(dve, ch, l, b):
            n = B * l + b
            dve.wait_ge(s_y, past(n))
            dve.tensor_tensor(xnew[:], x_sb[:, b, :], y_ps, ALU.add).then_inc(s_xup, 1)
            dve.wait_ge(s_xup, past(upd(ST_ATT[l], b)))
            dve_stats(dve, ch, b)

        def dve_stats(dve, ch, b):
            ch.step(dve.bn_stats(stats[:], xnew[:]))
            dve.tensor_scalar(x_sb[:, b, :], xnew[:], 1.0, None, ALU.mult)
            ch.step(dve.bn_aggr(mvnew[:], stats[:]))
            dve.tensor_scalar(mv[:, b, :], mvnew[:], 1.0, None, ALU.mult)

        def dve_stats_of(dve, ch, batches):
            for b in batches:
                ins = dve.bn_stats(stats_all[:, b, :], x_sb[:, b, :])
            ch.step(ins)
            for b in batches:
                dve.bn_aggr(mv[:, b, :], stats_all[:, b, :])

        def act_copies(act, src, dst, wait, n, sig):
            act.wait_ge(wait, past(n))
            act.activation(dst, src, ACT.Copy).then_inc(sig, 1)

        def act_exp(act, l, b, g):
            U = NG * (B * l + b) + g
            act.wait_ge(s_st, past(U))
            act.wait_ge(s_av, past(U - NG))
            act.activation(probs[:, g, :], bank[2 + g % 2][:], ACT.Exp, scale=float(1 / np.sqrt(HD))).then_inc(s_exp, 1)

        def pe_step(pe, l, b, k, turn_next, first=False, last=False):
            u, k_next = k % 2, (k + 1) % NS

            pe_scoresT(pe, l, b, k, u, 0)
            if not last:
                pe_scores(pe, l, b + 1, k_next, turn_next, 0)
            if not first:
                pe_rows_of_heads(pe, l, b - 1)
            pe_values(pe, l, b, k, 0)
            pe_values(pe, l, b, k, 1)
            if not last:
                pe_scores(pe, l, b + 1, k_next, turn_next, 1)
            if not first:
                pe_attT(pe, l, b - 1, 1 - u)
            pe_scoresT(pe, l, b, k, u, 1)
            if not first:
                pe_outproj(pe, l, b - 1, 1 - u)
            if not last:
                pe_maxT(pe, l, b + 1, 1 - u)
            pe_values(pe, l, b, k, 2)
            pe_values(pe, l, b, k, 3)

        def dve_step(dve, ch, l, b, u, first, last):
            if not last:
                dve_max(dve, l, b + 1, 1 - u, 0)
                dve_max(dve, l, b + 1, 1 - u, 1)
            if not first:
                dve_norm(dve, ch, l, b - 1, 1 - u)
            if not last:
                dve_max(dve, l, b + 1, 1 - u, 2)
                dve_max(dve, l, b + 1, 1 - u, 3)
                dve_maxparts(dve, ch, l, b + 1, 1 - u)
            if not first:
                dve_update(dve, ch, l, b - 1)

        def act_step(act, l, b, u, first, last):
            n = B * l + b
            if not first:
                act_copies(act, bank[4][:], o_sb[:], s_av, NG * n - 1, s_oc)
            act_exp(act, l, b, 0)
            act_exp(act, l, b, 1)
            if not first:
                act_copies(act, attT_ps, attT[:, 1 - u, :], s_atp, n - 1, s_atc)
            act_exp(act, l, b, 2)
            act_exp(act, l, b, 3)
            if not last:
                act_copies(act, maxT_ps, mT[:, 1 - u, :], s_mtp, n + 1, s_mt)

        def attention_pe(pe, l):
            pe_columns(pe, tjob_q(l, 0), 0, xn)
            for c in range(NC):
                u, n = c % 2, qjob(l, c)
                if c + 1 < NC:
                    pe_columns(pe, tjob_q(l, c + 1), 1 - u, xn)
                pe.wait_ge(s_xT, past(tjob_q(l, c)))
                pe.wait_ge(s_r1, past(n - 2))
                pe_project(pe, n, bank[2 + u][:], wq[:, l, :], xT[:, u, :])
                if l == 0:
                    pe_meansq(pe, NC + c)
            pe.wait_ge(s_xT, past(tjob_q(l, NC - 1)))
            for pair in range(2):
                pe_scores(pe, l, 0, 0, 0, pair)
            pe.wait_ge(s_r1, past(qjob(l, NC - 1)))
            pe_maxT(pe, l, 0, 0)
            pe_step(pe, l, 0, 0, 0, first=True)
            with pe.Fori(0, NC - 1) as i:
                for k in range(1, CB + 1):
                    pe_step(pe, l, i * CB + k, k % CB, i + (k + 1) // CB)
            for b in range(B - 3, B):
                pe_step(pe, l, b, b % CB, NC - 1, last=b == B - 1)
            pe_rows_of_heads(pe, l, B - 1)
            pe_attT(pe, l, B - 1, 1)
            pe_outproj(pe, l, B - 1, 1)

        def attention_dve(dve, ch, l):
            dve_rstd(dve, ch, norm(ST_ATT[l]))
            dve_rows(dve, tjob_q(l, 0), 0, 0)
            dve_rows(dve, tjob_q(l, 1), 1, 1)
            bias = None if l == 0 else colbias[:, 2 * l:2 * l + 1]

            def rows(c):
                if c < NC:
                    dve_rows(dve, tjob_q(l, c), c, c % 2)
            for c in range(NC):
                n, ps = qjob(l, c), bank[2 + c % 2][:]
                if l == 0:
                    dve_heads(dve, n, ps, NC + c, colbias[:, 0:1])
                    if c > 0:
                        dve_lo(dve, n - 1, False)
                    rows(c + 2)
                    dve_r1(dve, n, False, ps, None, NC + c)
                else:
                    dve_r1(dve, n, False, ps, bias)
                    rows(c + 2)
                    dve_lo(dve, n, False)
            if l == 0:
                dve_lo(dve, qjob(l, NC - 1), False)
            if l > 0:
                dve.wait_ge(s_xb, l)
            ch.step(dve.memset(bank[4][:], 0.0))
            for g in range(NG):
                dve_max(dve, l, 0, 0, g)
            dve_maxparts(dve, ch, l, 0, 0)
            dve_step(dve, ch, l, 0, 0, True, False)
            with dve.Fori(0, (B - 2) // 2) as i:
                ch.loop(i, 8)
                dve_step(dve, ch, l, i * 2 + 1, 1, False, False)
                dve_step(dve, ch, l, i * 2 + 2, 0, False, False)
            ch.end((B - 2) // 2)
            dve_step(dve, ch, l, B - 1, 1, False, True)
            dve_norm(dve, ch, l, B - 1, 1)
            dve_update(dve, ch, l, B - 1)

        def attention_act(act, l):
            act.wait_ge(s_vp, past(3 * NC - 1))

            def columns(c):
                if c < NC:
                    act.wait_ge(s_proj, past(qjob(l, c) - 2))
                    act_columns(act, tjob_q(l, c), c % 2)

            def squares(c):
                if l == 0 and c < NC:
                    act_square(act, qjob(l, c), bank[2 + c % 2][:], NC + c)
                    act_root(act, qjob(l, c), NC + c)
            bias = None if l == 0 else colbias[:, 2 * l:2 * l + 1]
            columns(0)
            squares(0)
            columns(1)
            for c in range(NC):
                squares(c + 1)
                act_hi(act, qjob(l, c), False, bank[2 + c % 2][:], bias, NC + c if l == 0 else None)
                act_mid(act, qjob(l, c))
                columns(c + 2)
            act_copies(act, maxT_ps, mT[:, 0, :], s_mtp, B * l, s_mt)
            act_step(act, l, 0, 0, True, False)
            with act.Fori(0, (B - 2) // 2) as i:
                act_step(act, l, i * 2 + 1, 1, False, False)
                act_step(act, l, i * 2 + 2, 0, False, False)
            act_step(act, l, B - 1, 1, False, True)
            act_copies(act, bank[4][:], o_sb[:], s_av, NG * B * (l + 1) - 1, s_oc)
            act_copies(act, attT_ps, attT[:, 1, :], s_atp, B * l + B - 1, s_atc)

        def attention_sp(sp, l):
            def store(c):
                sp_store(sp, qjob(l, c), False, qk_dram[l][0, c])
            store(0)
            sp.wait_ge(s_stored[0], past_dma(qjob(l, 0) // 2, 3))
            for k in range(CB):
                sp_load(sp, l, 0, k)
            for c in range(1, NC):
                store(c)
            for u in range(2):
                sp.wait_ge(s_stored[u], past_dma(qjob(l, 0) // 2 + 1, 3))
            with sp.Fori(1, NC) as c:
                for k in range(CB):
                    sp_load(sp, l, c, k)

        def chunk_dram(t, c):
            return t[bass.ds(c * CB, CB)] if not isinstance(c, int) else t[c * CB:(c + 1) * CB]

        def dve_rstd(dve, ch, n):
            ch.step(dve.drain())
            dve.tensor_scalar(vareps[:], mv[:, :, 1], EPS, None, ALU.add).then_inc(s_var, 1)
            dve.wait_ge(s_rstd, past(n))

        def pool_rstd(pool, n):
            pool.wait_ge(s_var, past(n))
            pool.tensor_tensor(rstd[:], vareps[:], neg_half[:, 0:B], ALU.pow).then_inc(s_rstd, 1)

        def dve_rows(dve, t, c, u):
            dve.wait_ge(s_tr, past(t - 2))
            for k in range(CB):
                b = c * CB + k
                ins = dve.tensor_scalar(xn[:, u, k, :], x_sb[:, b, :], mv[:, b, 0:1], rstd[:, bass.ds(b, 1)],
                                        ALU.subtract, ALU.mult)
            ins.then_inc(s_xn, 1)

        def pe_columns(pe, t, u, src):
            pe.wait_ge(s_xn, past(t - NC))
            pe.wait_ge(s_xT, past(t - 2))
            for k in range(CB):
                mm = pe.transpose(bank[u][:, k * P:(k + 1) * P], src[:, u, k, :], ident)
            mm.then_inc(s_tr, 1)

        def act_columns(act, t, u):
            act.wait_ge(s_tr, past(t))
            act.activation(xT[:, u, :], bank[u][:], ACT.Copy).then_inc(s_xT, 1)

        def bank_used(st, c):
            return past(upd(st, (c - 2) * CB + CB - 1))

        def pe_rows(pe, st, c, w, n=P):
            u = c % 2
            pe.wait_ge(s_xT, past(tjob(st, c)))
            for k in range(CB):
                mm = pe.matmul(bank[2 + u][:, k * n:(k + 1) * n], xT[:, u, k * P:(k + 1) * P], w,
                               start=True, stop=True)
            mm.then_inc(s_rp, 1)

        def dve_update_chunk(dve, ch, st, c, rp, scale=None):
            u = c % 2
            dve.wait_ge(s_rp, past(rp))
            bs = slice(c * CB, (c + 1) * CB)
            src, xc = bank[2 + u][:], x_sb[:, bs, :].rearrange("p b d -> p (b d)")
            if scale is None:
                ins = dve.tensor_tensor(xc, xc, src, ALU.add)
            else:
                ins = dve.scalar_tensor_tensor(out=xc, in0=src, scalar=scale, in1=xc, op0=ALU.mult, op1=ALU.add)
            ins.then_inc(s_xup, CB)
            dve.wait_ge(s_xup, past(upd(st, c * CB + CB - 1)))
            dve_stats_of(dve, ch, range(c * CB, (c + 1) * CB))

        def flat(t):
            return t.rearrange("p b d -> p (b d)")

        def over(row, n):
            return row.unsqueeze(1).broadcast_to([P, n, row.shape[1]])

        def ffn0_dve(dve, ch):
            st = ST_FFN0
            dve.wait_ge(s_wmid, 16 * len(loads_mid))
            dve_rstd(dve, ch, norm(st))
            ch.step(dve.tensor_copy(rs1[:], rstd[:]))
            ch.step(dve.tensor_tensor(vareps[:], mv[:, :, 1], rs1[:], ALU.mult))
            ch.step(dve.tensor_tensor(vareps[:], vareps[:], rs1[:], ALU.mult))
            dve.tensor_scalar(vareps[:], vareps[:], 1e-3, None, ALU.add).then_inc(s_var, 1)
            dve.tensor_reduce(sc[:, 0:1], w_f0[:], AX.X, ALU.add, apply_absolute_value=True).then_inc(s_dve1, 1)
            dve.wait_ge(s_rstd, past(norm(st) + 1))
            ch.step(dve.tensor_tensor(rs1[:], rs1[:], rstd[:], ALU.mult))
            for c in range(NC):
                for k in range(CB):
                    b = c * CB + k
                    ins = dve.tensor_scalar(xall[:, b, :], x_sb[:, b, :], mv[:, b, 0:1], rs1[:, b:b + 1],
                                            ALU.subtract, ALU.mult)
                ch.step(ins)
                xc = xall[:, c * CB:(c + 1) * CB, :]
                ch.step(dve.tensor_tensor(xc, xc, over(lnrow[:, 0, :], CB), ALU.mult))
                ch.step(dve.tensor_tensor(xc, xc, over(lnrow[:, 1, :], CB), ALU.add))
                ch.step(dve.tensor_reduce(amax[:, c:c + 1], flat(xc), AX.X, ALU.max, apply_absolute_value=True))
            dve.tensor_reduce(sc[:, 1:2], amax[:], AX.X, ALU.max).then_inc(s_dve1, 1)
            dve.wait_ge(s_pe1, PE1["amaxT"])
            dve.tensor_reduce(sc[0:1, 2:3], bank[6][0:1, 0:P], AX.X, ALU.max).then_inc(s_dve1, 1)
            beta, gain, lo = sc[:, 3:4], sc[:, 4:5], sc[:, 5:6]
            ch.step(dve.tensor_scalar(beta, bank[5][:, 0:1], 1.0 / (P * P), None, ALU.mult))
            ch.step(dve.tensor_scalar(gain, beta, 1e-5, None, ALU.add))
            ch.step(dve.reciprocal(gain, gain))
            ch.step(dve.tensor_scalar(w_t0[:, 0, :], w_f0[:], gain, 0.5, ALU.mult, ALU.is_gt))
            ch.step(dve.tensor_scalar(w_t0[:, 1, :], w_f0[:], gain, -0.5, ALU.mult, ALU.is_lt))
            ch.step(dve.tensor_tensor(w_t0[:, 0, :], w_t0[:, 0, :], w_t0[:, 1, :], ALU.subtract))
            dve.wait_ge(s_pe1, PE1["amax"])
            gam, to_q, to_y = sc[:, 6:7], sc[:, 7:8], sc[:, 8:9]
            ch.step(dve.tensor_copy(gam, bank[7][:, 0:1]))
            ch.step(dve.reciprocal(to_q, gam))
            ch.step(dve.tensor_scalar(to_q, to_q, 128.0, None, ALU.mult))
            ch.step(dve.tensor_tensor(to_y, gam, beta, ALU.mult))
            ch.step(dve.tensor_scalar(to_y, to_y, 1.0 / 128, None, ALU.mult))
            dve.drain().then_inc(s_dve1, 1)
            lim = float(np.float32(128.0 - 1e-5))

            def rows(c):
                dve.wait_ge(s_tr, past(tjob(st, c) - 2))
                xc = xn[:, c % 2]
                ch.step(dve.tensor_scalar(xc, xall[:, c * CB:(c + 1) * CB, :], to_q, lim, ALU.mult, ALU.min))
                dve.tensor_scalar(xc, xc, -lim, None, ALU.max).then_inc(s_xn, 1)
            rows(0)
            for c in range(NC):
                if c + 1 < NC:
                    rows(c + 1)
                dve_update_chunk(dve, ch, st, c, c, scale=to_y)

        def ffn0_pe(pe):
            pe.wait_ge(s_wmid, 16 * len(loads_mid))
            pe.wait_ge(s_dve1, DVE1["wabs0"])
            pe.matmul(bank[5][:, 0:1], ones_sq[:], sc[:, 0:1], start=True, stop=True).then_inc(s_pe1, 1)
            pe.wait_ge(s_dve1, DVE1["amax_col"])
            pe.transpose(bank[6][0:1, 0:P], sc[:, 1:2], ident).then_inc(s_pe1, 1)
            pe.wait_ge(s_dve1, DVE1["amax_row"])
            pe.matmul(bank[7][:, 0:1], ones_row[0:1, :], sc[0:1, 2:3], start=True, stop=True).then_inc(s_pe1, 1)
            pe.wait_ge(s_dve1, DVE1["ternary0"])
            for c in range(NC):
                pe_columns(pe, tjob(ST_FFN0, c), c % 2, xn)
                pe.wait_ge(s_xup, bank_used(ST_FFN0, c))
                pe_rows(pe, ST_FFN0, c, w_t0[:, 0, :])

        def columns_act(act, st):
            for c in range(NC):
                act_columns(act, tjob(st, c), c % 2)

        RP_CORR = NC

        def corr_dve(dve, ch):
            st = ST_CORR
            dve_rstd(dve, ch, norm(st))
            for c in range(NC):
                dve_rows(dve, tjob(st, c), c, c % 2)
            for c in range(NC):
                dve.wait_ge(s_rp, past(RP_CORR + c))
                w = CB * HD
                ins = dve.tensor_tensor(q1[:, c * w:(c + 1) * w].rearrange("p (b d) -> p b d", d=HD),
                                        bank[2 + c % 2][:, 0:w].rearrange("p (b d) -> p b d", d=HD),
                                        over(bq_c[:], CB), ALU.add)
                ins.then_inc(s_q1, 1)
            ch.step(dve.drain())
            dve.drain().then_inc(s_dve1, 1)
            dve.wait_ge(s_pe1, PE1["qkT"])
            dve.tensor_copy(flat(qk1T[:]), bank[5][:, 0:2 * P]).then_inc(s_dve1, 1)
            dve.wait_ge(s_pe1, PE1["corrM"])
            dve.tensor_copy(mm2[:], over(bank[6][:, 0:P], 2)).then_inc(s_dve1, 1)
            dve.wait_ge(s_pe1, PE1["corr"])
            ch.step(dve.tensor_copy(crow[:], bank[7][:, 0:P]))
            top, colv, z = sc[:, 10:11], sc[:, 11:12], sc[:, 12:13]
            ch.step(dve.tensor_tensor(cwork[:, 0, :], crow[:], ident, ALU.mult))
            ch.step(dve.tensor_reduce(colv, cwork[:, 0, :], AX.X, ALU.add))
            dve.tensor_reduce(top, crow[:], AX.X, ALU.max, negate=True).then_inc(s_dve1, 1)
            ch.step(dve.tensor_scalar(cwork[:, 1, :], crow[:], colv, None, ALU.is_equal))
            ch.step(dve.tensor_tensor(cwork[:, 1, :], cwork[:, 1, :], C["tie"], ALU.mult))
            ch.step(dve.tensor_scalar(cwork[:, 0, :], crow[:], colv, None, ALU.is_lt))
            dve.tensor_tensor(cwork[:, 0, :], cwork[:, 0, :], cwork[:, 1, :], ALU.add).then_inc(s_dve1, 1)
            dve.wait_ge(s_pe1, PE1["rank"])
            dve.wait_ge(s_act1, ACT1["corr_exp"])
            ch.step(dve.tensor_scalar(cwork[:, 1, :], bank[5][:, 0:P], K_TOP - 0.5, None, ALU.is_lt))
            ch.step(dve.tensor_tensor(cwork[:, 1, :], cwork[:, 1, :], cwork[:, 2, :], ALU.mult))
            ch.step(dve.tensor_reduce(z, cwork[:, 1, :], AX.X, ALU.add))
            ch.step(dve.reciprocal(z, z))
            dve.tensor_scalar(cwork[:, 0, :], cwork[:, 1, :], z, None, ALU.mult).then_inc(s_dve1, 1)
            dve.wait_ge(s_pe1, PE1["rolled"])
            dve.tensor_copy(rolled[:], bank[6][:, 0:P]).then_inc(s_dve1, 1)
            dve.wait_ge(s_pe1, PE1["rolled_out"])
            ch.step(dve.tensor_tensor(crow[:], bank[7][:, 0:P], bout_c[:], ALU.add))

            def rows(c):
                dve.wait_ge(s_rp, past(RP_CORR + NC + c - 2))
                for k in range(CB):
                    b = c * CB + k
                    ins = dve.tensor_scalar(ymask[:, c % 2, k, :], crow[:], C["own_batch"][:, b:b + 1], None, ALU.mult)
                ins.then_inc(s_ym, 1)
            rows(0)
            for c in range(NC):
                if c + 1 < NC:
                    rows(c + 1)
                dve_update_chunk(dve, ch, st, c, RP_CORR + NC + c)

        s_q1, s_ym = item("s_q1"), item("s_ym")

        def corr_pe(pe):
            st = ST_CORR
            for c in range(NC):
                pe_columns(pe, tjob(st, c), c % 2, xn)
                pe.wait_ge(s_q1, past(c - 2))
                pe_rows(pe, st, c, w_c[:], HD)
            pe.wait_ge(s_dve1, DVE1["corr_in"])
            pe.transpose(bank[5][:, 0:P], q1[:], ident)
            pe.transpose(bank[5][:, P:2 * P], k1[:], ident).then_inc(s_pe1, 1)
            pe.wait_ge(s_dve1, DVE1["corr_T"])
            pe.matmul(bank[6][:, 0:P], qk1T[:, 0, :], qk1T[:, 1, :], start=True, stop=True).then_inc(s_pe1, 1)
            pe.wait_ge(s_skew, 32)
            pe.matmul(bank[7][:, 0:P], mean_sq[:], skew[:], start=True, stop=True).then_inc(s_pe1, 1)
            pe.wait_ge(s_dve1, DVE1["corr_G"])
            pe.matmul(bank[5][:, 0:P], ones_sq[:], cwork[:, 0, :], start=True, stop=True).then_inc(s_pe1, 1)
            pe.wait_ge(s_skew, 64)
            pe.matmul(bank[6][:, 0:P], skew[:], k1[:], start=True, stop=True).then_inc(s_pe1, 1)
            pe.wait_ge(s_dve1, DVE1["rolled_sb"])
            pe.matmul(bank[7][:, 0:P], rolled[:], wout_c[:], start=True, stop=True).then_inc(s_pe1, 1)
            for c in range(NC):
                u = c % 2
                pe.wait_ge(s_ym, past(c))
                pe.wait_ge(s_xup, bank_used(st, c))
                pe.matmul(bank[2 + u][:], C["mod8"], flat(ymask[:, u]), start=True, stop=True).then_inc(s_rp, 1)

        def corr_act(act):
            columns_act(act, ST_CORR)
            act.wait_ge(s_dve1, DVE1["corr_negmax"])
            act.activation(cwork[:, 2, :], crow[:], ACT.Exp, bias=sc[:, 10:11]).then_inc(s_act1, 1)

        def corr_sp(sp):
            sp.wait_ge(s_dve1, DVE1["corr_mm"])
            sp.dma_start(corr_dram, mm2[:].rearrange("p a n -> p (a n)")).then_inc(s_skew, 16)
            sp.wait_ge(s_skew, 16)
            sp.dma_start(skew[:], bass.AP(corr_dram.tensor, 0, [[2 * P + 1, P], [1, P]])).then_inc(s_skew, 16)
            sp.wait_ge(s_dve1, DVE1["corr_w"])
            sp.dma_start(wlag_dram, cwork[:, 0, :]).then_inc(s_skew, 16)
            sp.wait_ge(s_skew, 48)
            sp.dma_start(skew[:], bass.AP(wlag_dram.tensor, 0, [[P - 1, P], [1, P]])).then_inc(s_skew, 16)

        def twist_dve(dve, ch):
            st = ST_TWIST
            for k in range(2):
                w = (CN[4], GC[3])[k]
                ch.step(dve.tensor_scalar(w, ones_sq[0:32, :], w4c[:, k:k + 1], None, ALU.mult))
            ar = b_l1[:, 7:8]
            ch.step(dve.tensor_scalar(b_l1[:, 3:4], b_l1[:, 3:4], 0.5, None, ALU.mult))
            ch.step(dve.tensor_scalar(b_l1[:, 6:7], b_l1[:, 6:7], 0.5, None, ALU.mult))
            dve_rstd(dve, ch, norm(st))
            for c in range(NC):
                dve_rows(dve, tjob(st, c), c, c % 2)
            for c in range(NC):
                dve.wait_ge(s_xT, past(tjob(st, c)))
                dve.tensor_reduce(gx[:, 0, c * CB:(c + 1) * CB], xall[:, c * CB:(c + 1) * CB, :], AX.X, ALU.add)
            ch.step(dve.drain())
            dve.tensor_scalar(gx[:, 0, :], gx[:, 0, :], 1.0 / P, None, ALU.mult).then_inc(s_dve1, 1)
            dve.wait_ge(s_act1, ACT1["g3"])
            ch.step(dve.tensor_scalar(acoef[:], gx[:, 3, :], ar, 0.7, ALU.mult, ALU.mult))
            ch.step(dve.tensor_scalar(acoef[:], acoef[:], 0.1, None, ALU.add))
            ch.step(dve.tensor_scalar(sc[:, 13:14], ar, 0.3, None, ALU.mult))
            dve.drain().then_inc(s_dve1, 1)
            for y in range(CYCLES):
                for c in range(NC):
                    n, u = NC * y + c, c % 2
                    cols = xcols[:, c * CW:(c + 1) * CW]
                    t3 = tf[:, u, :].rearrange("p (b t) -> p b t", b=CB)
                    dve.wait_ge(s_g4, past(n))
                    ch.step(dve.scalar_tensor_tensor(out=t3, in0=t3, scalar=sc[:, 13:14],
                                                     in1=acoef[:, c * CB:(c + 1) * CB].unsqueeze(2).broadcast_to([P, CB, P]),
                                                     op0=ALU.mult, op1=ALU.add))
                    dve.wait_ge(s_twp, past(n))
                    ch.step(dve.tensor_tensor(tws[:, u, :], bank[6][:], tf[:, u, :], ALU.mult))
                    dve.tensor_tensor(cols, cols, tws[:, u, :], ALU.add).then_inc(s_cyc, 1)
            for c in range(NC):
                dve_update_chunk(dve, ch, st, c, RP_CORR + 2 * NC + c)

        def twist_pe(pe):
            st = ST_TWIST
            for c in range(NC):
                pe_columns(pe, tjob(st, c), c % 2, xn)
            for k in range(3):
                pe.wait_ge(s_dve1, DVE1["gmean"]) if k == 0 else pe.wait_ge(s_act1, ACT1[f"g{k}"])
                w = GC[k + 1]
                pe.matmul(bank[5][0:w.shape[1], 0:B], w, gx[0:w.shape[0], k, :], start=True, stop=True).then_inc(s_pe1, 1)
            pe.wait_ge(s_act1, ACT1["g3"])
            for y in range(CYCLES):
                for c in range(NC):
                    n, u = NC * y + c, c % 2
                    cols = xcols[:, c * CW:(c + 1) * CW]
                    pe.wait_ge(s_cyc, past(n - NC))
                    pe.wait_ge(s_g1, past(n - 1))
                    pe.matmul(bank[2][:], CN[1], cols, start=True, stop=True).then_inc(s_c1, 1)
                    pe.wait_ge(s_cyc, past(n - 1))
                    pe.matmul(bank[6][:], C["twist"], cols, start=True, stop=True).then_inc(s_twp, 1)
                    pe.wait_ge(s_g1, past(n))
                    pe.matmul(bank[3][0:64, :], CN[2], h1[:, u, :], start=True, stop=True).then_inc(s_c2, 1)
                    pe.wait_ge(s_g2, past(n))
                    pe.matmul(bank[4][0:32, :], CN[3], h2[:, u, :], start=True, stop=True).then_inc(s_c3, 1)
                    pe.wait_ge(s_g3, past(n))
                    pe.wait_ge(s_g4, past(n - 1))
                    pe.matmul(bank[5][:], CN[4], h3[:, u, :], start=True, stop=True).then_inc(s_c4, 1)
            for c in range(NC):
                u = c % 2
                pe.wait_ge(s_cyc, past(NC * (CYCLES - 1) + c))
                pe.wait_ge(s_g4, past(NC * CYCLES - 1))
                pe.wait_ge(s_xup, bank_used(st, c))
                for k in range(CB):
                    b = c * CB + k
                    mm = pe.transpose(bank[2 + u][:, k * P:(k + 1) * P], xall[:, b, :], ident)
                mm.then_inc(s_rp, 1)

        def twist_act(act):
            st = ST_TWIST
            for c in range(NC):
                act.wait_ge(s_tr, past(tjob(st, c)))
                act.activation(xcols[:, c * CW:(c + 1) * CW], bank[c % 2][:], ACT.Copy).then_inc(s_xT, 1)
            for k, (m, f, s) in enumerate(((64, ACT.Gelu, 1.0), (32, ACT.Gelu, 1.0), (P, ACT.Tanh, 0.5))):
                act.wait_ge(s_pe1, PE1[f"g{k + 1}"])
                act.activation(gx[0:m, k + 1, :], bank[5][0:m, 0:B], f, bias=b_l1[0:m, 4 + k:5 + k], scale=s).then_inc(s_act1, 1)
            for n in range(NC * CYCLES):
                u = n % 2
                act.wait_ge(s_c1, past(n))
                act.activation(h1[:, u, :], bank[2][:], ACT.Gelu, bias=b_l1[:, 0:1]).then_inc(s_g1, 1)
                act.wait_ge(s_c2, past(n))
                act.activation(h2[:, u, :], bank[3][0:64, :], ACT.Gelu, bias=b_l1[0:64, 1:2]).then_inc(s_g2, 1)
                act.wait_ge(s_c3, past(n))
                act.activation(h3[:, u, :], bank[4][0:32, :], ACT.Gelu, bias=b_l1[0:32, 2:3]).then_inc(s_g3, 1)
                act.wait_ge(s_c4, past(n))
                act.wait_ge(s_cyc, past(n - 2))
                act.activation(tf[:, u, :], bank[5][:], ACT.Tanh, bias=b_l1[:, 3:4], scale=0.5).then_inc(s_g4, 1)

        def bitw_dve(dve, ch):
            dve.wait_ge(s_w7, 16 * len(loads7))
            dve.tensor_reduce(bsc[:, 0:2], wb[:], AX.X, ALU.add, apply_absolute_value=True).then_inc(s_dve1, 1)
            dve.wait_ge(s_pe1, PE1["bit_mean"])
            ch.step(dve.tensor_scalar(bsc[:, 2:4], bank[5][:, 0:2], 1.0 / (P * FF), 1e-5, ALU.mult, ALU.max))
            ch.step(dve.reciprocal(bsc[:, 4:6], bsc[:, 2:4]))
            for k in range(2):
                ch.step(dve.tensor_scalar(wbt[:, k, :], wb[:, k, :], bsc[:, 4 + k:5 + k], 0.5, ALU.mult, ALU.is_gt))
                ch.step(dve.tensor_scalar(wb[:, k, :], wb[:, k, :], bsc[:, 4 + k:5 + k], -0.5, ALU.mult, ALU.is_lt))
                ins = dve.tensor_tensor(wbt[:, k, :], wbt[:, k, :], wb[:, k, :], ALU.subtract)
                if k == 0:
                    ch.step(ins)
            ins.then_inc(s_dve1, 1)
            dve.wait_ge(s_pe1, PE1["bit_wT"])
            dve.tensor_copy(w1T[:], bank[6][:, 0:FF // 2].bitcast(BF16))
            ch.step(dve.tensor_copy(w2T[:], bank[7][:, 0:FF // 2].bitcast(BF16)))

        def bitw_pe(pe):
            pe.wait_ge(s_dve1, DVE1["bit_abs"])
            pe.matmul(bank[5][:, 0:2], ones_sq[:], bsc[:, 0:2], start=True, stop=True).then_inc(s_pe1, 1)
            pe.wait_ge(s_dve1, DVE1["bit_tern"])
            for k in range(2):
                o = bank[6 + k][:, 0:FF // 2].bitcast(BF16)
                for f in range(FK):
                    mm = pe.transpose(o[:, f * P:(f + 1) * P], wbt[:, k, f * P:(f + 1) * P], identb[:])
            mm.then_inc(s_pe1, 1)

        RP_MOE = RP_CORR + 3 * NC

        def moe_route_dve(dve, ch):
            st = ST_MOE
            dve_rstd(dve, ch, norm(st))
            for c in range(NC):
                for k in range(CB):
                    b = c * CB + k
                    ins = dve.tensor_scalar(xall[:, b, :], x_sb[:, b, :], mv[:, b, 0:1], rstd[:, b:b + 1],
                                            ALU.subtract, ALU.mult)
                ins.then_inc(s_xn, 1)
            lg, eq, hot, tot, sa, sbb, cmp, tmp = (rt[:, k] for k in range(8))
            for c in range(NC):
                dve.wait_ge(s_rp, past(RP_MOE + c))
                dve.tensor_copy(lg[:, c * CB:(c + 1) * CB, :],
                                bank[2 + c % 2][:, 0:CB * NE].rearrange("p (b e) -> p b e", e=NE)).then_inc(s_lg, 1)
            ch.step(dve.drain())

            def of_batch(v):
                return v.unsqueeze(2).broadcast_to([P, B, NE])
            ch.step(dve.tensor_reduce(rs[:, 0, :], lg, AX.X, ALU.max))
            ch.step(dve.tensor_tensor(eq, lg, of_batch(rs[:, 0, :]), ALU.is_equal))
            ch.step(dve.tensor_tensor(eq, eq, over(C["first"], B), ALU.mult))
            ch.step(dve.tensor_reduce(rs[:, 0, :], eq, AX.X, ALU.max))
            dve.tensor_tensor(hot, eq, of_batch(rs[:, 0, :]), ALU.is_equal).then_inc(s_dve1, 1)
            dve.wait_ge(s_pe1, PE1["prefix"])
            earlier = lg
            dve.tensor_copy(earlier, bank[6][:, 0:P].rearrange("p (b e) -> p b e", e=NE))
            dve.tensor_copy(tot, bank[7][:, 0:P].rearrange("p (b e) -> p b e", e=NE)).then_inc(s_dve1, 1)
            dve.wait_ge(s_dve1, DVE1["prefix_read"])
            a = tot
            for step, o in ((1, sa), (2, sbb), (4, sa), (8, sbb)):
                dve.tensor_copy(o[:, 0:step], a[:, 0:step])
                ch.step(dve.tensor_tensor(o[:, step:B], a[:, step:B], a[:, 0:B - step], ALU.add))
                a = o
            n_e = a[:, B - 1, :]
            cm = cmp.rearrange("p b e -> p (b e)").rearrange("p (e k) -> p e k", k=B)
            ch.step(dve.tensor_tensor(cm, n_e.unsqueeze(2).broadcast_to([P, NE, B]), over(C["tile_rows"], NE), ALU.is_gt))
            tiles, e1, e2 = rs[:, 1, 0:NE], rs[:, 2, 0:NE], rs[:, 3, 0:NE]
            ch.step(dve.tensor_reduce(tiles, cm, AX.X, ALU.add))
            s = tiles
            for step, o in ((1, e1), (2, e2), (4, e1)):
                dve.tensor_copy(o[:, 0:step], s[:, 0:step])
                ch.step(dve.tensor_tensor(o[:, step:NE], s[:, step:NE], s[:, 0:NE - step], ALU.add))
                s = o
            start = rs[:, 4, 0:NE]
            ch.step(dve.tensor_tensor(start, e1, tiles, ALU.subtract))
            ch.step(dve.tensor_scalar(start, start, float(P), float(B * P), ALU.mult, ALU.add))
            ch.step(dve.tensor_tensor(a, a, tot, ALU.subtract))
            ch.step(dve.tensor_tensor(a, a, earlier, ALU.add))
            ch.step(dve.tensor_tensor(a, a, over(start, B), ALU.add))
            ch.step(dve.tensor_tensor(a, a, hot, ALU.mult))
            ch.step(dve.tensor_reduce(rs[:, 5, :], a, AX.X, ALU.add))
            dve.tensor_copy(pos[:], rs[:, 5, :])
            x3 = rx[:].rearrange("p (j e) -> p j e", e=NE)
            ch.step(dve.tensor_tensor(x3, C["tile_no"].unsqueeze(2).broadcast_to([P, NX, NE]), over(e1, NX), ALU.is_ge))
            tj = rt[:, 7].rearrange("p b e -> p (b e)")[:, 0:NX]
            ch.step(dve.tensor_reduce(tj, x3, AX.X, ALU.add))
            dve.tensor_scalar(etab[:], tj, float(NE - 1), None, ALU.min).then_inc(s_dve1, 1)

        def moe_route_pe(pe):
            st = ST_MOE
            for c in range(NC):
                u = c % 2
                pe.wait_ge(s_xn, past(tjob(st, c) - NC))
                pe.wait_ge(s_xT, past(tjob(st, c) - 2))
                for k in range(CB):
                    mm = pe.transpose(bank[u][:, k * P:(k + 1) * P], xall[:, c * CB + k, :], ident)
                mm.then_inc(s_tr, 1)
                pe.wait_ge(s_lg, past(c - 2))
                pe_rows(pe, st, c, w_g[:], NE)
            pe.wait_ge(s_dve1, DVE1["onehot"])
            hot = rt[:, 2].rearrange("p b e -> p (b e)")
            pe.matmul(bank[6][:, 0:P], C["before"], hot, start=True, stop=True)
            pe.matmul(bank[7][:, 0:P], ones_sq[:], hot, start=True, stop=True).then_inc(s_pe1, 1)

        def expert(pe, n):
            return pe.value_load(etab[0:1, bass.ds(n - B, 1)] if not isinstance(n, int) else etab[0:1, n - B:n - B + 1],
                                 min_val=0, max_val=NE - 1)

        def wslice(e, at, n):
            if isinstance(e, int):
                return wmoe[:, e, at:at + n]
            return wmoe[:].rearrange("p e w -> p (e w)")[:, bass.ds(e * (3 * FF) + at, n)]

        def pe_tileT(pe, n, u, turn):
            pe.wait_ge(s_rl[u], past_dma(turn))
            pe.wait_ge(s_xs, past(n - 1))
            pe.transpose(bank[6][:, 0:P], xr[:, u, :], ident).then_inc(s_xtp, 1)

        def pe_up(pe, n, u, shared):
            pe.wait_ge(s_xs, past(n))
            pe.wait_ge(s_gl, past(n - 2))
            pe.wait_ge(s_g, past(n - 2))
            e = NE if shared else expert(pe, n)
            pe.matmul(bank[u][:], xs[:, u, :], wslice(e, 0, FF), start=True, stop=True)
            pe.matmul(bank[2 + u][:], xs[:, u, :], wslice(e, FF, FF), start=True, stop=True).then_inc(s_h, 1)

        def pe_gT(pe, n, u):
            pe.wait_ge(s_g, past(n))
            pe.wait_ge(s_gt, past(n - 2))
            for f in range(FK):
                mm = pe.transpose(bank[4 + u][:, f * P:(f + 1) * P], gl[:, u, f * P:(f + 1) * P], ident)
            mm.then_inc(s_gtp, 1)

        def pe_down(pe, n, u, shared):
            pe.wait_ge(s_gt, past(n))
            pe.wait_ge(s_yo, past(n - 1))
            e = NE if shared else expert(pe, n)
            for f in range(FK):
                mm = pe.matmul(bank[7][:, 0:P], gT[:, u, f * P:(f + 1) * P], wslice(e, 2 * FF + f * P, P),
                               start=(f == 0), stop=(f == FK - 1))
            mm.then_inc(s_o, 1)

        def moe_pe(pe):
            def step(j, u, turn, up, down):
                if up is not None:
                    pe_up(pe, j + 1, 1 - u, up)
                if down is not None:
                    pe_down(pe, j - 1, 1 - u, down)
                pe_gT(pe, j, u)
            pe.wait_ge(s_dve1, DVE1["prefix_read"])
            pe_tileT(pe, 0, 0, 0)
            pe_tileT(pe, 1, 1, 0)
            pe_up(pe, 0, 0, True)
            step(0, 0, 0, True, None)
            pe_tileT(pe, 2, 0, 1)
            with pe.Fori(0, (B - 2) // 2) as i:
                step(i * 2 + 1, 1, i, True, True)
                pe_tileT(pe, i * 2 + 3, 1, i + 1)
                step(i * 2 + 2, 0, i, True, True)
                pe_tileT(pe, i * 2 + 4, 0, i + 2)
            pe.wait_ge(s_dve1, DVE1["route"])
            step(B - 1, 1, 0, False, True)
            pe_tileT(pe, B + 1, 1, (B + 1) // 2)
            step(B, 0, 0, False, True)
            pe_tileT(pe, B + 2, 0, (B + 2) // 2)
            with pe.Fori(0, (NX - 3) // 2) as i:
                step(i * 2 + (B + 1), 1, i, False, False)
                pe_tileT(pe, i * 2 + (B + 3), 1, i + (B + 2) // 2)
                step(i * 2 + (B + 2), 0, i, False, False)
                pe_tileT(pe, i * 2 + (B + 4), 0, i + (B + 4) // 2)
            step(NT - 2, 1, 0, False, False)
            step(NT - 1, 0, 0, None, False)
            pe_down(pe, NT - 1, 0, False)

        def act_tile(act, n, u):
            act.wait_ge(s_xtp, past(n))
            act.activation(xs[:, u, :], bank[6][:, 0:P], ACT.Copy).then_inc(s_xs, 1)

        def act_gelu(act, n, u):
            act.wait_ge(s_h, past(n))
            act.wait_ge(s_gtp, past(n - 2))
            act.activation(gl[:, u, :], bank[u][:], ACT.Gelu).then_inc(s_gl, 1)

        def moe_act(act):
            columns_act(act, ST_MOE)
            act_tile(act, 0, 0)
            act_tile(act, 1, 1)
            act_gelu(act, 0, 0)
            with act.Fori(0, (NT - 3) // 2) as i:
                for k in range(2):
                    act_gelu(act, i * 2 + (k + 1), 1 - k)
                    act_tile(act, i * 2 + (k + 2), k)
            act_gelu(act, NT - 2, 1)
            act_tile(act, NT - 1, 0)
            act_gelu(act, NT - 1, 0)

        def moe_dve(dve, ch):
            def mul(n, u):
                dve.wait_ge(s_gl, past(n))
                dve.tensor_tensor(gl[:, u, :], gl[:, u, :], bank[2 + u][:], ALU.mult).then_inc(s_g, 1)

            def copyT(n, u):
                dve.wait_ge(s_gtp, past(n))
                dve.wait_ge(s_o, past(n - 2))
                dve.tensor_copy(gT[:, u, :], bank[4 + u][:]).then_inc(s_gt, 1)

            def down(n, u, turn):
                dve.wait_ge(s_o, past(n))
                dve.wait_ge(s_yst[u], past_dma(turn - 1))
                dve.tensor_copy(yo[:, u, :], bank[7][:, 0:P]).then_inc(s_yo, 1)
            mul(0, 0)
            mul(1, 1)
            copyT(0, 0)
            with dve.Fori(0, (NT - 3) // 2) as i:
                mul(i * 2 + 2, 0)
                down(i * 2, 0, i)
                copyT(i * 2 + 1, 1)
                mul(i * 2 + 3, 1)
                down(i * 2 + 1, 1, i)
                copyT(i * 2 + 2, 0)
            mul(NT - 1, 0)
            down(NT - 3, 0, NT // 2 - 1)
            copyT(NT - 2, 1)
            down(NT - 2, 1, NT // 2 - 1)
            copyT(NT - 1, 0)
            down(NT - 1, 0, NT // 2)
            dve.wait_ge(s_ysh, 16)
            dve.wait_ge(s_gath, 16 * B)
            for c in range(NC):
                xc = xall[:, c * CB:(c + 1) * CB, :]
                ch.step(dve.tensor_tensor(xc, xc, yshared[:, c * CB:(c + 1) * CB, :], ALU.add))
                xs4 = x_sb[:, c * CB:(c + 1) * CB, :]
                dve.tensor_tensor(xs4, xs4, xc, ALU.add).then_inc(s_xup, CB)
                dve.wait_ge(s_xup, past(upd(ST_MOE, c * CB + CB - 1)))
                dve_stats_of(dve, ch, range(c * CB, (c + 1) * CB))

        def moe_sp(sp):
            for c in range(NC):
                sp.wait_ge(s_xn, past(tjob(ST_MOE, c) - NC))
                sp.dma_start(rows_dram[c * CB:(c + 1) * CB].rearrange("b t d -> t b d"),
                             xall[:, c * CB:(c + 1) * CB, :]).then_inc(s_rows, 16)
            sp.wait_ge(s_rows, 16 * NC)

            def load(n, u):
                sp.wait_ge(s_xtp, past(n - 2))
                sp.sem_inc(s_sp, 1)
                sp.dma_start(xr[:, u, :], rows_dram[n]).then_inc(s_rl[u], 16)

            def store(n, u):
                sp.wait_ge(s_yo, past(n))
                sp.sem_inc(s_sp, 1)
                sp.dma_start(y_dram[bass.ds(n * P, P)] if not isinstance(n, int) else y_dram[n * P:(n + 1) * P],
                             yo[:, u, :]).then_inc(s_yst[u], 16)
            load(0, 0)
            load(1, 1)
            load(2, 0)
            load(3, 1)
            with sp.Fori(0, (B - 4) // 2) as i:
                for u in range(2):
                    load(i * 2 + (u + 4), u)
                    store(i * 2 + u, u)
            sp.wait_ge(s_scat, 16 * B)
            with sp.Fori((B - 4) // 2, (NT - 5) // 2) as i:
                for u in range(2):
                    load(i * 2 + (u + 4), u)
                    store(i * 2 + u, u)
            load(NT - 1, 0)
            for n in range(NT - 5, NT):
                store(n, n % 2)
            for u, n in ((0, NT // 2), (1, NT // 2 - 1)):
                sp.wait_ge(s_yst[u], past_dma(n))
            sp.dma_start(yshared[:], y_dram[0:B * P].rearrange("(b t) d -> t b d", t=P)).then_inc(s_ysh, 16)

        def moe_pool(pool):
            pool.wait_ge(s_dve1, DVE1["route"])
            pool.wait_ge(s_zero, 32)
            for b in range(B):
                pool.indirect_dma_start(rows_dram.rearrange("n t d -> (n t) d"),
                                        bass.IndirectOffsetOnAxis(ap=pos[:, b:b + 1], axis=0),
                                        xall[:, b, :], None).then_inc(s_scat, 16)
            pool.wait_ge(s_scat, 16 * B)
            pool.wait_ge(s_rows, 16 * NC)
            for u, n in ((0, NT // 2), (1, NT // 2 - 1)):
                pool.wait_ge(s_yst[u], past_dma(n))
            for b in range(B):
                pool.indirect_dma_start(xall[:, b, :], None, y_dram,
                                        bass.IndirectOffsetOnAxis(ap=pos[:, b:b + 1], axis=0)).then_inc(s_gath, 16)

        def bit_dve(dve, ch):
            st = ST_BIT
            dve_rstd(dve, ch, norm(st))
            ch.step(dve.tensor_copy(rs1[:], rstd[:]))
            ch.step(dve.tensor_tensor(vareps[:], mv[:, :, 1], rs1[:], ALU.mult))
            ch.step(dve.tensor_tensor(vareps[:], vareps[:], rs1[:], ALU.mult))
            dve.tensor_scalar(vareps[:], vareps[:], 1e-5, None, ALU.add).then_inc(s_var, 1)
            dve.wait_ge(s_rstd, past(norm(st) + 1))
            ch.step(dve.tensor_tensor(rs1[:], rs1[:], rstd[:], ALU.mult))

            def quant_scales(q, wm):
                ch.step(dve.tensor_scalar(q[:, 0], q[:, 0], 1e-5, None, ALU.max))
                ch.step(dve.reciprocal(q[:, 1], q[:, 0]))
                ch.step(dve.tensor_scalar(q[:, 1], q[:, 1], 127.0, None, ALU.mult))
                ch.step(dve.tensor_scalar(q[:, 2], q[:, 0], 1.0 / 127, wm, ALU.mult, ALU.mult))

            def rows(c):
                u = c % 2
                q = bq[:, u]
                xc = xn[:, u]
                for k in range(CB):
                    b = c * CB + k
                    ins = dve.tensor_scalar(xc[:, k, :], x_sb[:, b, :], mv[:, b, 0:1], rs1[:, b:b + 1],
                                            ALU.subtract, ALU.mult)
                ch.step(ins)
                ch.step(dve.tensor_reduce(q[:, 0], xc, AX.X, ALU.max, apply_absolute_value=True))
                quant_scales(q, bsc[:, 2:3])
                for k in range(CB):
                    ins = dve.tensor_scalar(xc[:, k, :], xc[:, k, :], q[:, 1, k:k + 1], 127.0, ALU.mult, ALU.min)
                ch.step(ins)
                ch.step(dve.tensor_scalar(xc, xc, -128.0, MAGIC, ALU.max, ALU.add))
                dve.wait_ge(s_tr, past(tjob(st, c) - 2))
                dve.tensor_scalar(xq[:, u], xc, MAGIC, None, ALU.subtract).then_inc(s_xn, 1)

            def inner(c):
                u = c % 2
                q = bq[:, u]
                for k in range(CB):
                    n = c * CB + k
                    dve.wait_ge(s_bh, past(n))
                    dve.scalar_tensor_tensor(out=hg[:, u, k, :], in0=bank[2 + n % 2][:], scalar=q[:, 2, k:k + 1],
                                             in1=b1row[:], op0=ALU.mult, op1=ALU.add).then_inc(s_bb, 1)
                for k in range(CB):
                    n = c * CB + k
                    dve.wait_ge(s_bg, past(n))
                    dve.tensor_reduce(q[:, 3, k:k + 1], hg[:, u, k, :], AX.X, ALU.max, apply_absolute_value=True)
                dve.wait_ge(s_bsq, past(c * CB + CB - 1))
                dve.tensor_scalar(q[:, 5], q[:, 4], 1.0 / FF, 1e-5, ALU.mult, ALU.add).then_inc(s_bms, 1)
                dve.wait_ge(s_bpw, past(c))
                ch.step(dve.tensor_tensor(q[:, 0], q[:, 3], q[:, 6], ALU.mult))
                quant_scales(q, bsc[:, 3:4])
                ch.step(dve.tensor_tensor(q[:, 1], q[:, 1], q[:, 6], ALU.mult))

            def outer(c):
                u = c % 2
                q = bq[:, u]

                def quant(k):
                    hk = hg[:, u, k, :]
                    ch.step(dve.tensor_scalar(hk, hk, q[:, 1, k:k + 1], 127.0, ALU.mult, ALU.min))
                    dve.tensor_scalar(hk, hk, -128.0, MAGIC, ALU.max, ALU.add).then_inc(s_bq, 1)

                def update(k):
                    n = c * CB + k
                    dve.wait_ge(s_bo, past(n))
                    ch.step(dve.scalar_tensor_tensor(out=xall[:, n, :], in0=bank[6 + n % 2][:, 0:P],
                                                     scalar=q[:, 2, k:k + 1], in1=x_sb[:, n, :],
                                                     op0=ALU.mult, op1=ALU.add))
                    dve.tensor_tensor(xall[:, n, :], xall[:, n, :], b2row[:], ALU.add).then_inc(s_bx, 1)
                quant(0)
                quant(1)
                for k in range(CB):
                    update(k)
                    if k + 2 < CB:
                        quant(k + 2)
            for c in range(NC):
                rows(c)
                inner(c)
                outer(c)

        def bit_pe(pe):
            st = ST_BIT
            for c in range(NC):
                u = c % 2
                t = tjob(st, c)
                pe.wait_ge(s_xn, past(t - NC))
                pe.wait_ge(s_xT, past(t - 2))
                o = bank[u][:, 0:CW // 2].bitcast(BF16)
                for k in range(CB):
                    mm = pe.transpose(o[:, k * P:(k + 1) * P], xq[:, u, k, :], identb[:])
                mm.then_inc(s_tr, 1)
                pe.wait_ge(s_xT, past(t))
                for k in range(CB):
                    n = c * CB + k
                    pe.wait_ge(s_bb, past(n - 2))
                    pe.matmul(bank[2 + n % 2][:], xqT[:, u, k * P:(k + 1) * P], w1T[:], start=True, stop=True).then_inc(s_bh, 1)
                for k in range(CB):
                    n = c * CB + k
                    v = n % 2
                    pe.wait_ge(s_bqb, past(n))
                    pe.wait_ge(s_bt, past(n - 2))
                    o = bank[4 + v][:, 0:FF // 2].bitcast(BF16)
                    for f in range(FK):
                        mm = pe.transpose(o[:, f * P:(f + 1) * P], hq[:, v, f * P:(f + 1) * P], identb[:])
                    mm.then_inc(s_btp, 1)
                    pe.wait_ge(s_bt, past(n))
                    pe.wait_ge(s_bx, past(n - 2))
                    for f in range(FK):
                        mm = pe.matmul(bank[6 + v][:, 0:P], hqT[:, v, f * P:(f + 1) * P], w2T[:, f * P:(f + 1) * P],
                                       start=(f == 0), stop=(f == FK - 1))
                    mm.then_inc(s_bo, 1)

        def bit_act(act):
            st = ST_BIT
            for c in range(NC):
                u = c % 2
                act.wait_ge(s_tr, past(tjob(st, c)))
                act.activation(xqT[:, u, :], bank[u][:, 0:CW // 2].bitcast(BF16), ACT.Copy).then_inc(s_xT, 1)
                for k in range(CB):
                    n = c * CB + k
                    act.wait_ge(s_bb, past(n))
                    act.activation(hg[:, u, k, :], hg[:, u, k, :], ACT.Gelu).then_inc(s_bg, 1)
                    act.wait_ge(s_bg, past(n))
                    act.activation(h1[:, 0, :], hg[:, u, k, :], ACT.Square,
                                   accum_out=bq[:, u, 4, k:k + 1]).then_inc(s_bsq, 1)
                for k in range(CB):
                    n = c * CB + k
                    v = n % 2
                    act.wait_ge(s_bq, past(n))
                    act.wait_ge(s_btp, past(n - 2))
                    act.activation(hq[:, v, :], hg[:, u, k, :], ACT.Copy, bias=-MAGIC).then_inc(s_bqb, 1)
                    act.wait_ge(s_btp, past(n))
                    act.activation(hqT[:, v, :], bank[4 + v][:, 0:FF // 2].bitcast(BF16), ACT.Copy).then_inc(s_bt, 1)

        def bit_pool(pool):
            for c in range(NC):
                q = bq[:, c % 2]
                pool.wait_ge(s_bms, past(c))
                pool.tensor_tensor(q[:, 6], q[:, 5], neg_half[:, 0:CB], ALU.pow).then_inc(s_bpw, 1)


        @block.sync
        def _(sp):
            def context(c):
                if c < NC:
                    sp.wait_ge(s_tr, past(tjob_ctx(c) - 2))
                    sp.dma_start(ctx_in[:, c % 2], chunk_dram(I["ctx_1024"], c).rearrange("b t d -> t b d")
                                 ).then_inc(s_ctx[c % 2], 16)
            early = sum(CWIDTH[:CEARLY])
            sp.dma_start(cst[:, 0:early], I["consts"][:, 0:early]).then_inc(s_cst, 16)
            context(0)
            for t, s in loads[0::2]:
                sp.dma_start(t, s).then_inc(s_w, 16)
            context(1)
            sp.dma_start(x_sb[:], I["x"].rearrange("b t d -> t b d")).then_inc(s_x, 16)
            sp.dma_start(cst[:, early:], I["consts"][:, early:]).then_inc(s_cst2, 16)

            def store_k(c, l):
                sp_store(sp, kjob(c, l), True, qk_dram[l][1, c])

            def store_v(c, l):
                n = kjob(c, l)
                sp.wait_ge(s_vb, past(n))
                sp.dma_start(chunk_dram(v_dram[l], c).rearrange("b t w -> t b w"),
                             v_out[:, n % 2].rearrange("p b h w -> p b (h w)")).then_inc(s_vst[n % 2], 16)
            for c in range(NC):
                if c > 0:
                    store_k(c - 1, 0)
                for l in (1, 2):
                    store_v(c, l)
                    store_k(c, l)
                context(c + 2)
                store_v(c, 0)
            store_k(NC - 1, 0)
            for v in range(2):
                sp.wait_ge(s_stored[v], past_dma((3 * NC - 1) // 2, 3))
                sp.wait_ge(s_vst[v], past_dma((3 * NC - 1) // 2))
            attention_sp(sp, 0)
            corr_sp(sp)
            attention_sp(sp, 1)
            moe_sp(sp)
            attention_sp(sp, 2)
            sp.wait_ge(s_done, 1)
            sp.wait_ge(s_w1, 16 * len(loads1))
            sp.wait_ge(s_w5, 16 * len(loads5))
            sp.wait_ge(s_w7, 16 * len(loads7))
            sp.dma_start(out.rearrange("b t d -> t b d"), xall[:]).then_inc(s_out, 16)
            sp.wait_ge(s_out, 16)

        @block.gpsimd
        def _(pool):
            for s, per in s_lead:
                pool.sem_inc(s, LEAD * per)
            pool.memset(neg_half[:], -0.5).then_inc(s_const, 1)
            pool.memset(eps6[:], 1e-6).then_inc(s_const, 1)
            pool.memset(v_out[:], 1.0).then_inc(s_const, 1)
            pool.memset(ones_row[:], 1.0).then_inc(s_const, 1)
            pool.memset(ones_sq[:], 1.0).then_inc(s_const, 1)
            pool.memset(mean_sq[:], 1.0 / (B * HD)).then_inc(s_const, 1)
            pool.memset(mpad[:], 0.0).then_inc(s_const, 1)
            pool.memset(xall[:], 0.0).then_inc(s_const, 1)
            pool.wait_ge(s_const, 8)
            pool.dma_start(rows_dram[B:NT].rearrange("n t d -> t n d")[:, 0:B], xall[:]).then_inc(s_zero, 16)
            pool.dma_start(rows_dram[2 * B:NT].rearrange("n t d -> t n d"), xall[:, 0:NX - B]).then_inc(s_zero, 16)
            for group, s_group in ((loads_mid, s_wmid), (loads1, s_w1), (loads7, s_w7)):
                for t, s in group:
                    pool.dma_start(t, s).then_inc(s_group, 16)
            pool.wait_ge(s_zero, 32)
            pool.wait_ge(s_wmid, 16 * len(loads_mid))
            for k in range(norm(ST_BIT) + 2):
                pool_rstd(pool, k)
                if k == 0:
                    for t, s in loads5:
                        pool.dma_start(t, s).then_inc(s_w5, 16)
                for l in (1, 2):
                    if k == norm(ST_ATT[l]):
                        pool.wait_ge(s_xn, past(tjob_q(l, NC - 1) - NC))
                        pool.tensor_tensor(x_sb[:], x_sb[:], over(borow[:, l, :], B), ALU.add).then_inc(s_xb, 1)
                if k == norm(ST_MOE):
                    moe_pool(pool)
            bit_pool(pool)

        @block.scalar
        def _(act):
            for t, s in loads[1::2]:
                act.dma_start(t, s).then_inc(s_w, 16)
            def ctx_columns(c):
                if c < NC:
                    act.wait_ge(s_tr, past(tjob_ctx(c)))
                    act.wait_ge(s_vp, past(3 * (c - 1) - 1))
                    act.activation(xT[:, c % 2, :], bank[c % 2][:], ACT.Copy).then_inc(s_xT, 1)

            def kb(l):
                return colbias[:, 2 * l + 1:2 * l + 2]
            ctx_columns(0)
            act.wait_ge(s_const, 8)
            act.wait_ge(s_wprep, 1)
            for c in range(NC + 1):
                if c > 0:
                    act_hi(act, kjob(c - 1, 0), True, None, None, c - 1)
                if c < NC:
                    act_hi(act, kjob(c, 1), True, bank[2][:], kb(1))
                if c > 0:
                    act_mid(act, kjob(c - 1, 0))
                if c < NC:
                    act_square(act, kjob(c, 0), bank[5][:], c)
                    act_mid(act, kjob(c, 1))
                    act_hi(act, kjob(c, 2), True, bank[3][:], kb(2))
                    ctx_columns(c + 1)
                    act_mid(act, kjob(c, 2))
                    act_root(act, kjob(c, 0), c)
            attention_act(act, 0)
            columns_act(act, ST_FFN0)
            corr_act(act)
            twist_act(act)
            attention_act(act, 1)
            moe_act(act)
            attention_act(act, 2)
            bit_act(act)

        @block.vector
        def _(dve):
            ch = Chain(dve, s_dve)
            dve.wait_ge(s_cst, 16)
            dve.tensor_copy(identb[:], ident)
            dve.wait_ge(s_w, 16 * len(loads))
            for l in range(2):
                for w, k in ((wq, 0), (wk, 1)):
                    dve.tensor_copy(w[:, l, :].rearrange("p (half d h) -> p half d h", half=2, d=8),
                                    wraw[:, 4 * l + k, :].rearrange("p (half h d) -> p half d h", half=2, d=8))
            dve.wait_ge(s_wt, 1)
            for w, k in ((wq, 0), (wk, 1)):
                dve.tensor_copy(w[:, 2, :].rearrange("p (half d h) -> p half d h", half=2, d=8),
                                bank[6][:, k * P:(k + 1) * P].rearrange("p (half h d) -> p half d h", half=2, d=8))
            dve.tensor_copy(wvo3[:].rearrange("p k n -> p (k n)"), bank[6][:, 2 * P:4 * P])
            dve.tensor_copy(colbias[:, 0:6], bank[7][:, 0:6]).then_inc(s_wprep, 1)
            dve.wait_ge(s_const, 8)

            def values(c, l):
                n = kjob(c, l)
                v = n % 2
                dve.wait_ge(s_vp, past(n))
                dve.wait_ge(s_vst[v], past_dma(n // 2 - 1))
                for k in range(CB):
                    o = v_out[:, v, k, :, 0:HD]
                    s = bank[6 + v][:, k * P:(k + 1) * P].rearrange("p (h d) -> p h d", d=HD)
                    if l == 0:
                        ins = dve.tensor_copy(o, s)
                    else:
                        ins = dve.tensor_tensor(o, s, bvrow[:, l, :].rearrange("p (h d) -> p h d", d=HD), ALU.add)
                ins.then_inc(s_vb, 1)
            for c in range(NC + 1):
                if c < NC:
                    dve.wait_ge(s_k1p, past(c))
                    dve.tensor_tensor(k1[:, c * (CB * HD):(c + 1) * (CB * HD)].rearrange("p (b d) -> p b d", d=HD),
                                      bank[4][:, 0:CB * HD].rearrange("p (b d) -> p b d", d=HD),
                                      over(bq_c[:], CB), ALU.add).then_inc(s_k1, 1)
                if c > 0:
                    dve_r1(dve, kjob(c - 1, 0), True, None, None, c - 1)
                if c < NC:
                    dve_r1(dve, kjob(c, 1), True, bank[2][:], colbias[:, 3:4])
                if c > 0:
                    dve_lo(dve, kjob(c - 1, 0), True)
                if c < NC:
                    values(c, 1)
                    dve_lo(dve, kjob(c, 1), True)
                    dve_r1(dve, kjob(c, 2), True, bank[3][:], colbias[:, 5:6])
                    values(c, 2)
                    dve_lo(dve, kjob(c, 2), True)
                    dve_heads(dve, kjob(c, 0), bank[5][:], c, colbias[:, 1:2])
                    values(c, 0)
                if c == 1:
                    dve.wait_ge(s_x, 16)
                    dve_stats_of(dve, ch, range(B))
            dve.wait_ge(s_cst2, 16)
            dve.tensor_copy(selb[:].rearrange("p h t -> p (h t)"), C["sel"])
            attention_dve(dve, ch, 0)
            ffn0_dve(dve, ch)
            corr_dve(dve, ch)
            dve.wait_ge(s_w1, 16 * len(loads1))
            twist_dve(dve, ch)
            attention_dve(dve, ch, 1)
            bitw_dve(dve, ch)
            moe_route_dve(dve, ch)
            moe_dve(dve, ch)
            attention_dve(dve, ch, 2)
            bit_dve(dve, ch)
            dve.drain().then_inc(s_done, 1)

        @block.tensor
        def _(pe):
            pe.wait_ge(s_cst, 16)
            def ctx_columns(c):
                if c < NC:
                    pe.wait_ge(s_ctx[c % 2], 16 * (c // 2 + 1))
                    pe.wait_ge(s_xT, past(tjob_ctx(c) - 2))
                    for k in range(CB):
                        mm = pe.transpose(bank[c % 2][:, k * P:(k + 1) * P], ctx_in[:, c % 2, k, :], ident)
                    mm.then_inc(s_tr, 1)

            def values(c, l):
                n = kjob(c, l)
                pe.wait_ge(s_vb, past(n - 2))
                for k in range(CB):
                    mm = pe.matmul(bank[6 + n % 2][:, k * P:(k + 1) * P], xT[:, c % 2, k * P:(k + 1) * P], wv(l),
                                   start=True, stop=True)
                mm.then_inc(s_vp, 1)
            ctx_columns(0)
            pe.wait_ge(s_w, 16 * len(loads))
            for k in range(4):
                pe.transpose(bank[6][:, k * P:(k + 1) * P], wraw[:, 8 + k, :], ident)
            pe.matmul(bank[7][:, 2:6], C["perm"], colraw[:, 2:6], start=True, stop=True)
            pe.matmul(bank[7][:, 0:2], C["spread_d"][0:HD, :], colraw[0:HD, 0:2], start=True, stop=True).then_inc(s_wt, 1)
            pe.wait_ge(s_wprep, 1)
            for c in range(NC):
                xs = xT[:, c % 2, :]
                pe.wait_ge(s_xT, past(tjob_ctx(c)))
                pe.wait_ge(s_mse, past(c - 1))
                for k in range(CB):
                    mm = pe.matmul(bank[4][:, k * HD:(k + 1) * HD], xs[:, k * P:(k + 1) * P], w_c[:],
                                   start=True, stop=True)
                mm.then_inc(s_k1p, 1)
                for l in (1, 2):
                    pe.wait_ge(s_r1, past(kjob(c - 1, l)))
                    pe_project(pe, kjob(c, l), bank[1 + l][:], wk[:, l, :], xs)
                pe.wait_ge(s_rms, past(c - 1))
                pe_project(pe, kjob(c, 0), bank[5][:], wk[:, 0, :], xs)
                ctx_columns(c + 1)
                values(c, 1)
                pe.wait_ge(s_k1, past(c))
                pe_meansq(pe, c)
                values(c, 2)
                values(c, 0)
            attention_pe(pe, 0)
            ffn0_pe(pe)
            corr_pe(pe)
            pe.wait_ge(s_w1, 16 * len(loads1))
            twist_pe(pe)
            attention_pe(pe, 1)
            bitw_pe(pe)
            pe.wait_ge(s_w5, 16 * len(loads5))
            moe_route_pe(pe)
            moe_pe(pe)
            attention_pe(pe, 2)
            bit_pe(pe)


def kernel(**inputs):
    import concourse.bacc as _bacc
    from concourse.bass_utils import run_bass_kernel_spmd as _run

    nc = _bacc.Bacc("TRN2", target_bir_lowering=False, num_devices=1)
    arrays, aps = {}, {}
    arrays["consts"] = np.concatenate([CONSTS[k] for k in CORDER], axis=1)
    for name, a in inputs.items():
        arrays[name] = np.ascontiguousarray(a)
    for name, a in arrays.items():
        aps[name] = nc.dram_tensor(f"in_{name}", a.shape, mybir.dt.from_np(a.dtype), kind="ExternalInput").ap()
    out = nc.dram_tensor("out_x", (B, P, P), F32, kind="ExternalOutput").ap()
    build_program(nc, aps, out)
    r = _run(nc, [{f"in_{k}": v for k, v in arrays.items()}], core_ids=[0])
    return r.results[0]["out_x"]
```

```python
from contextlib import ExitStack

import numpy as np

import concourse.bass as bass
from concourse import mybir

ALU = mybir.AluOpType
ACT = mybir.ActivationFunctionType
AX = mybir.AxisListType
F32 = mybir.dt.float32
BF16 = mybir.dt.bfloat16
I32 = mybir.dt.int32
U32 = mybir.dt.uint32

P = 128
B = 16
H, HD = 16, 8
CB = 4
NC = B // CB
CW = CB * P
GH = 4
NG = H // GH
VW = HD + 1
OW = P // GH
NE = 8
FF = 512
FK = FF // P
NX = B + NE - 1
NT = B + NX
T1 = B // 2
T2 = T1 + NX
EPS = 1e-5
NS = 4
NP = 3
LEAD = 16


def upd(st, b):
    return B * st + b


def past(n):
    return n + 1 + LEAD


def past_dma(n, dmas=1):
    return 16 * dmas * (n + 1 + LEAD)


def slots(g):
    return [(g % 2, GH * (g // 2) + j) for j in range(GH)]


def block_of(g):
    return 2 * (g % 2) + g // 2


class Chain:

    def __init__(self, eng, sem):
        self.eng, self.sem, self.done = eng, sem, 0
        self.it, self.per, self.at = None, 0, 0

    def step(self, ins):
        ins.then_inc(self.sem, 1)
        self.at += 1
        self.eng.wait_ge(self.sem, self.count())

    def count(self):
        if self.it is None:
            return self.done + self.at
        return self.it * self.per + (self.done + self.at)

    def loop(self, it, per):
        self.done += self.at
        self.it, self.per, self.at = it, per, 0

    def end(self, turns):
        assert self.at == self.per, (self.at, self.per)
        self.done += turns * self.per
        self.it, self.at = None, 0


def make_constants():
    c = {}
    eye = np.eye(P, dtype=np.float32)
    p = np.arange(P)
    c["ident"] = eye
    half, d, place = p // 64, (p % 64) // 8, p % 8
    head = 8 * half + place
    c["headmean"] = (head[:, None] == head[None, :]).astype(np.float32) / HD
    perm = np.zeros((P, P), np.float32)
    perm[head * HD + d, p] = 1.0
    c["perm"] = perm
    c["spread_d"] = np.zeros((P, P), np.float32)
    c["spread_d"][d, p] = 1.0
    sel = np.zeros((P, 8, P), np.float32)
    for h in range(2):
        for part in range(2):
            for k in range(8):
                sel[64 * h + 8 * part + k, k, :] = 1.0
    c["sel"] = sel.reshape(P, 8 * P)
    lag = (-p) % P
    c["tie"] = (lag[:, None] < lag[None, :]).astype(np.float32)
    c["mod8"] = (p[:, None] % HD == p[None, :] % HD).astype(np.float32)
    c["own_batch"] = (p[:, None] // HD == np.arange(B)[None, :]).astype(np.float32)
    tw = np.zeros((P, P), np.float32)
    for to, fr, s in ((0, 2, 1), (1, 3, -1), (2, 0, -1), (3, 1, 1)):
        for k in range(32):
            tw[32 * fr + k, 32 * to + k] = s
    c["twist"] = tw
    c["before"] = (p[:, None] < p[None, :]).astype(np.float32)
    c["first"] = np.broadcast_to(NE - np.arange(NE, dtype=np.float32), (P, NE))
    c["tile_rows"] = np.broadcast_to(P * np.arange(B, dtype=np.float32), (P, B))
    c["tile_no"] = np.broadcast_to(np.arange(NX, dtype=np.float32), (P, NX))
    return c


CONSTS = make_constants()
CORDER = list(CONSTS)
CEARLY = 4
CWIDTH = [CONSTS[k].shape[1] for k in CORDER]

ATT = {0: "L0_xattn", 1: "L2_xattn", 2: "L3_xattn"}
ST_ATT = (0, 4, 6)
ST_FFN0, ST_CORR, ST_TWIST, ST_MOE, ST_BIT = 1, 2, 3, 5, 7
K_TOP = int(2 * np.log(256))
CYCLES = 3
MAGIC = 12582912.0


def norm(st):
    return st if st <= ST_FFN0 else st + 1


def once(*names):
    return {name: i + 1 for i, name in enumerate(names)}


PE1 = once("wmean0", "amaxT", "amax", "qkT", "corrM", "corr", "rank", "rolled", "rolled_out",
           "g1", "g2", "g3", "bit_mean", "bit_wT", "prefix")
DVE1 = once("wabs0", "amax_col", "amax_row", "ternary0", "corr_in", "corr_T", "corr_mm", "corr_negmax",
            "corr_G", "corr_w", "rolled_sb", "gmean", "t_bias", "bit_abs", "bit_tern", "bit_copies", "onehot", "prefix_read", "route")
ACT1 = once("corr_exp", "g1", "g2", "g3")


def build_program(nc, I, out):
    with ExitStack() as ctx:
        def sb(name, shape, dt=F32):
            return ctx.enter_context(nc.sbuf_tensor(name, shape, dt))

        def sem(name):
            return ctx.enter_context(nc.semaphore(name))

        def dram(name, shape, dt=F32):
            return nc.dram_tensor(name, shape, dt, kind="Internal").ap()

        bank = [ctx.enter_context(nc.psum_tensor(f"bank{i}", [P, 512], F32)) for i in range(8)]
        x_sb = sb("x_sb", [P, B, P])
        cst = sb("cst", [P, sum(CWIDTH)])
        C = {}
        at = 0
        for k, w in zip(CORDER, CWIDTH):
            C[k] = cst[:, at:at + w]
            at += w
        ident = C["ident"]
        identb = sb("identb", [P, P], BF16)
        ones_row = sb("ones_row", [P, P])
        neg_half = sb("neg_half", [P, B])
        eps6 = sb("eps6", [P, 1])

        stats = sb("stats", [P, 6])
        stats_all = sb("stats_all", [P, B, 6])
        mv = sb("mv", [P, B, 2])
        mvnew = sb("mvnew", [P, 2])
        xnew = sb("xnew", [P, P])
        vareps = sb("vareps", [P, B])
        rstd = sb("rstd", [P, B])
        xn = sb("xn", [P, 2, CB, P])
        xT = sb("xT", [P, 2, CW])

        ctx_in = sb("ctx_in", [P, 2, CB, P])
        wraw = sb("wraw", [P, 12, P])
        wq = sb("wq", [P, 3, P])
        wk = sb("wk", [P, 3, P])
        wvo3 = sb("wvo3", [P, 2, P])
        colraw = sb("colraw", [P, 8])
        colbias = sb("colbias", [P, 8])
        bvrow = sb("bvrow", [P, 3, P])
        borow = sb("borow", [P, 3, P])

        sq = sb("sq", [P, CW])
        resid = sb("resid", [P, 2, CW])
        parts = sb("parts", [P, NP, 3, CW], BF16)
        v_out = sb("v_out", [P, 2, CB, H, VW])

        stk = sb("stk", [P, NS, 2, 8, P], BF16)
        qstk, kstk = stk[:, :, 0], stk[:, :, 1]
        v_in = sb("v_in", [P, NS, H, VW])
        negm = sb("negm", [P, 2, 2, 8])
        mpad = sb("mpad", [P, 2, P], BF16)
        probs = sb("probs", [P, NG, GH * P])
        o_sb = sq
        rden = sb("rden", [P, H])
        att = sb("att", [P, 2, P])
        attT = sb("attT", [P, 2, P])

        xall = sb("xall", [P, B, P])
        rs1 = sb("rs1", [P, B])
        lnrow = sb("lnrow", [P, 2, P])
        w_f0 = sb("w_f0", [P, P])
        w_t0 = sb("w_t0", [P, 2, P])
        amax = sb("amax", [P, NC])
        sc = sb("sc", [P, 16])
        ones_sq = sb("ones_sq", [P, P])
        mean_sq = sb("mean_sq", [P, P])
        w_c = sb("w_c", [P, HD])
        bq_c = sb("bq_c", [P, HD])
        wout_c = sb("wout_c", [P, P])
        bout_c = sb("bout_c", [P, P])
        q1 = sb("q1", [P, P])
        k1 = sb("k1", [P, P])
        qk1T = sb("qk1T", [P, 2, P])
        mm2 = sb("mm2", [P, 2, P])
        skew = sb("skew", [P, P])
        crow = sb("crow", [P, P])
        cwork = sb("cwork", [P, 3, P])
        rolled = sb("rolled", [P, P])
        ymask = sb("ymask", [P, 2, CB, P])
        w_cn = sb("w_cn", [P, P + 64 + 32 + P])
        w_gc = sb("w_gc", [P, 64 + 32 + P])
        b_l1 = sb("b_l1", [P, 8])
        w4c = sb("w4c", [32, 2])
        tbuf = sb("tbuf", [P, 4, CW])
        h1, tf = tbuf[:, 0:2], tbuf[:, 2:4]
        h2 = parts[:].rearrange("p a b n -> p (a b n)").bitcast(F32)[0:64, 0:2 * CW].rearrange("p (u n) -> p u n", u=2)
        h3 = ctx_in[0:32].rearrange("p u b d -> p u (b d)")
        tws = sb("tws", [P, 2, CW])
        gx = sb("gx", [P, 4, B])
        acoef = sb("acoef", [P, B])
        wmoe = sb("wmoe", [P, NE + 1, 3 * FF])
        w_g = sb("w_g", [P, NE])
        rt = sb("rt", [P, 8, B, NE])
        rs = sb("rs", [P, 6, B])
        rx = sb("rx", [P, NX * NE])
        etab = sb("etab", [P, NX], I32)
        pos = sb("pos", [P, B], U32)
        pos_y = sb("pos_y", [P, B], U32)
        xr = sb("xr", [P, 2, P])
        xs = sb("xs", [P, 2, P])
        gl = tws
        gT = ymask[:].rearrange("p u b d -> p u (b d)")
        yo = sb("yo", [P, 2, P])
        ygath = tbuf[:].rearrange("p k (b d) -> p (k b) d", d=P)
        rows_dram = dram("rows_dram", [NT, P, P])
        y_dram = dram("y_dram", [NX * P, P])
        wb = sb("wb", [P, 2, FF])
        wbt = sb("wbt", [P, 2, FF], BF16)
        w1T = sb("w1T", [P, FF], BF16)
        w2T = sb("w2T", [P, FF], BF16)
        b1row = sb("b1row", [P, FF])
        b2row = sb("b2row", [P, P])
        bsc = sb("bsc", [P, 8])
        bq = sb("bq", [P, 3, 8, CB])
        free = wmoe[:].rearrange("p e w -> p (e w)")
        hg = free[:, 0:2 * CB * FF].rearrange("p (u k f) -> p u k f", u=2, k=CB)
        free = free[:, 2 * CB * FF:].bitcast(BF16)
        xq = free[:, 0:2 * CW].rearrange("p (u k d) -> p u k d", u=2, k=CB)
        xqT, hq, hqT = (free[:, k * 2 * CW:(k + 1) * 2 * CW].rearrange("p (u n) -> p u n", u=2) for k in (1, 2, 3))

        corr_dram = dram("corr_dram", [P, 2 * P])
        wlag_dram = dram("wlag_dram", [P, P])

        qk_dram = [dram(f"qk_stacks{l}", [2, NC, 6, CB, P, P], BF16) for l in range(3)]
        v_dram = [dram(f"v_rows{l}", [B, P, H * VW]) for l in range(3)]

        s_cst, s_cst2 = sem("s_cst"), sem("s_cst2")
        s_x, s_w, s_wmid = sem("s_x"), sem("s_w"), sem("s_wmid")
        s_ctx = [sem("s_ctx_even"), sem("s_ctx_odd")]
        s_const = sem("s_const")
        s_wt = sem("s_wt")
        s_wprep = sem("s_wprep")
        s_lead = []

        def item(name, per=1):
            s = sem(name)
            s_lead.append((s, per))
            return s

        s_var, s_rstd = item("s_var"), item("s_rstd")
        s_xn, s_tr, s_xT = item("s_xn"), item("s_tr"), item("s_xT")
        s_proj, s_hi, s_r1, s_mid, s_lo = item("s_proj"), item("s_hi"), item("s_r1"), item("s_mid"), item("s_lo")
        s_sq, s_ms, s_mse, s_inv, s_rms = item("s_sq"), item("s_ms"), item("s_mse"), item("s_inv"), item("s_rms")
        s_stored = [item(f"s_stored{k}", 16 * 3) for k in range(NP)]
        s_vp, s_vb = item("s_vp"), item("s_vb")
        s_vst = [item("s_vst_even", 16), item("s_vst_odd", 16)]
        s_stk = [item(f"s_stk{k}", 16 * 5) for k in range(NS)]
        s_sc, s_max, s_mparts, s_mtp, s_mt = item("s_sc"), item("s_max"), item("s_mparts"), item("s_mtp"), item("s_mt")
        s_mt2, s_mz = item("s_mt2"), item("s_mz")
        s_xb = sem("s_xb")
        s_oc, s_or = item("s_oc"), item("s_or")
        s_st, s_exp, s_av, s_norm = item("s_st"), item("s_exp"), item("s_av"), item("s_norm")
        s_atp, s_atc, s_y, s_xup = item("s_atp"), item("s_atc"), item("s_y"), item("s_xup")
        s_done = sem("s_done")
        s_out = sem("s_out")
        s_rp = item("s_rp")
        s_k1p, s_k1 = item("s_k1p"), item("s_k1")
        s_pe1, s_dve1, s_act1 = sem("s_pe1"), sem("s_dve1"), sem("s_act1")
        s_skew = sem("s_skew")
        s_w5, s_w7, s_zero = sem("s_w5"), sem("s_w7"), sem("s_zero")
        s_rows, s_scat = sem("s_rows"), sem("s_scat")
        s_gath = [sem(f"s_gath{c}") for c in range(NC)]
        s_rl = [item("s_rl_even", 16), item("s_rl_odd", 16)]
        s_xtp, s_xs, s_h, s_gl, s_g, s_gtp, s_gt, s_o, s_yo = (
            item(f"s_moe_{k}") for k in ("xtp", "xs", "h", "gl", "g", "gtp", "gt", "o", "yo"))
        s_yst = [item("s_yst_even", 16), item("s_yst_odd", 16)]
        s_lg = item("s_lg")
        s_bh, s_bb, s_bg, s_bsq, s_bms, s_bpw, s_bq, s_bqb, s_btp, s_bt, s_bo, s_bx = (
            item(f"s_bit_{k}") for k in ("h", "b", "g", "sq", "ms", "pw", "q", "qb", "tp", "t", "o", "x"))
        s_bclip = sem("s_bit_clip")
        s_w1 = sem("s_w1")
        s_c1, s_g1, s_c2, s_g2, s_c3, s_g3, s_c4, s_g4, s_cyc, s_twp, s_tws = (
            item(f"s_tw_{k}") for k in ("p1", "g1", "p2", "g2", "p3", "g3", "p4", "g4", "cyc", "twp", "tws"))
        s_dve = sem("s_dve")
        s_sp = sem("s_sp")

        block = ctx.enter_context(nc.Block())

        loads = []

        xcols = xall[:].rearrange("p b t -> p (b t)")
        CN = {1: w_cn[:, 0:P], 2: w_cn[:, P:P + 64], 3: w_cn[0:64, P + 64:P + 96], 4: w_cn[0:32, P + 96:2 * P + 96]}
        GC = {1: w_gc[:, 0:64], 2: w_gc[0:64, 64:96], 3: w_gc[0:32, 96:96 + P]}

        def col(name):
            return I[name].rearrange("(p a) -> p a", a=1)

        def row(name):
            return I[name].rearrange("(a n) -> a n", a=1)

        wsrc = [I["L0_xattn_Wq"], I["L0_xattn_Wkv"][:, 0:P], I["L0_xattn_Wkv"][:, P:2 * P], I["L0_xattn_Wproj"]]
        for l in (1, 2):
            wsrc += [I[f"{ATT[l]}_{w}"] for w in ("Wq", "Wk", "Wv", "Wo")]
        for i, s in enumerate(wsrc):
            loads.append((wraw[:, i, :], s))
        loads += [(colraw[0:HD, 0:1], col("L0_xattn_q_gamma")), (colraw[0:HD, 1:2], col("L0_xattn_k_gamma"))]
        for l in (1, 2):
            loads += [(colraw[:, 2 * l:2 * l + 1], col(f"{ATT[l]}_bq")),
                      (colraw[:, 2 * l + 1:2 * l + 2], col(f"{ATT[l]}_bk")),
                      (bvrow[:, l, :], row(f"{ATT[l]}_bv").broadcast_to([P, P]))]
        loads += [(w_c[:], I["L1_xattn_Wq"]), (bq_c[:], row("L1_xattn_bq").broadcast_to([P, HD]))]

        loads_mid = [(w_f0[:], I["L0_ffn_weight"]),
              (lnrow[:, 0, :], row("L0_ffn_ln_gamma").broadcast_to([P, P])),
              (lnrow[:, 1, :], row("L0_ffn_ln_beta").broadcast_to([P, P])),
              (wout_c[:], I["L1_xattn_Wout"]), (bout_c[:], row("L1_xattn_bout").broadcast_to([P, P]))]
        loads_mid += [(borow[:, l, :], row(f"{ATT[l]}_bo").broadcast_to([P, P])) for l in (1, 2)]
        loads1 = [(CN[1], I["L1_ffn_cn_w1"]), (CN[2], I["L1_ffn_cn_w2"]), (CN[3], I["L1_ffn_cn_w3"]),
                  (w4c[:, 0:1], I["L1_ffn_cn_w4"]), (w4c[:, 1:2], I["L1_ffn_gc_w3"]),
                  (GC[1], I["L1_ffn_gc_w1"]), (GC[2], I["L1_ffn_gc_w2"]),
                  (b_l1[:, 0:1], col("L1_ffn_cn_b1")), (b_l1[0:64, 1:2], col("L1_ffn_cn_b2")),
                  (b_l1[0:32, 2:3], col("L1_ffn_cn_b3")),
                  (b_l1[:, 3:4], row("L1_ffn_cn_b4").broadcast_to([P, 1])),
                  (b_l1[0:64, 4:5], col("L1_ffn_gc_b1")), (b_l1[0:32, 5:6], col("L1_ffn_gc_b2")),
                  (b_l1[:, 6:7], row("L1_ffn_gc_b3").broadcast_to([P, 1])),
                  (b_l1[:, 7:8], row("L1_ffn_adaptive_range").broadcast_to([P, 1]))]

        def w3rows(w):
            return w.rearrange("(k p) d -> p k d", p=P)

        def w3tile(e):
            return wmoe[:, e, 2 * FF:3 * FF].rearrange("p (k d) -> p k d", k=FK)

        loads5 = [(wmoe[:, NE, 0:FF], I["L2_ffn_w1s"]), (wmoe[:, NE, FF:2 * FF], I["L2_ffn_w2s"]),
                  (w3tile(NE), w3rows(I["L2_ffn_w3s"])), (w_g[:], I["L2_ffn_Wg"])]
        for e in range(NE):
            loads5 += [(wmoe[:, e, 0:FF], I["L2_ffn_W1"][e]), (wmoe[:, e, FF:2 * FF], I["L2_ffn_W2"][e]),
                       (w3tile(e), w3rows(I["L2_ffn_W3"][e]))]
        loads7 = [(wb[:, 0, :].rearrange("p (k d) -> p k d", k=FK), w3rows(I["L3_ffn_w1"])), (wb[:, 1, :], I["L3_ffn_w2"]),
                  (b1row[:], row("L3_ffn_b1").broadcast_to([P, FF])), (b2row[:], row("L3_ffn_b2").broadcast_to([P, P]))]

        def wv(l):
            return wraw[:, 4 * l + 2, :] if l < 2 else wvo3[:, 0, :]

        def wo(l):
            return wraw[:, 4 * l + 3, :] if l < 2 else wvo3[:, 1, :]

        K_ORDER = (1, 2, 0)

        def kjob(c, l):
            return c * 3 + K_ORDER.index(l)

        def qjob(l, c):
            return 3 * NC + l * NC + c

        def tjob_ctx(c):
            return c

        def tjob_q(l, c):
            return tjob(ST_ATT[l], c)

        def tjob(st, c):
            return NC * (1 + st) + c

        def stored(eng, n):
            eng.wait_ge(s_stored[n % NP], past_dma(n // NP, 3))

        def pe_project(pe, n, ps, w, xs):
            pe.matmul(ps, w, xs, start=True, stop=True).then_inc(s_proj, 1)

        def pe_meansq(pe, m):
            pe.wait_ge(s_sq, past(m))
            pe.wait_ge(s_mse, past(m - 1))
            pe.matmul(bank[4][:], C["headmean"], sq[:], start=True, stop=True).then_inc(s_ms, 1)

        def act_square(act, n, ps, m):
            act.wait_ge(s_proj, past(n))
            act.wait_ge(s_ms, past(m - 1))
            act.activation(sq[:], ps, ACT.Square).then_inc(s_sq, 1)

        def act_root(act, n, m):
            act.wait_ge(s_ms, past(m))
            act.wait_ge(s_lo, past(n - 2))
            act.activation(resid[:, n % 2, :], bank[4][:], ACT.Sqrt, bias=eps6[:, 0:1]).then_inc(s_mse, 1)

        def act_hi(act, n, is_k, ps, bias, m=None):
            if m is None:
                act.wait_ge(s_proj, past(n))
            else:
                act.wait_ge(s_rms, past(m))
            stored(act, n - NP)
            act.activation(parts[:, n % NP, 0 if is_k else 2, :], ps if m is None else resid[:, n % 2, :],
                           ACT.Identity, bias=0.0 if bias is None else bias).then_inc(s_hi, 1)

        def act_mid(act, n):
            act.wait_ge(s_r1, past(n))
            act.activation(parts[:, n % NP, 1, :], resid[:, n % 2, :], ACT.Identity).then_inc(s_mid, 1)

        def dve_heads(dve, n, ps, m, gamma):
            r = resid[:, n % 2, :]
            dve.wait_ge(s_mse, past(m))
            dve.reciprocal(r, r).then_inc(s_inv, 1)
            dve.wait_ge(s_inv, past(m))
            dve.scalar_tensor_tensor(out=r, in0=ps, scalar=gamma, in1=r, op0=ALU.mult, op1=ALU.mult).then_inc(s_rms, 1)

        def dve_r1(dve, n, is_k, ps, bias, m=None):
            r, hi = resid[:, n % 2, :], parts[:, n % NP, 0 if is_k else 2, :]
            dve.wait_ge(s_lo, past(n - 2))
            dve.wait_ge(s_hi, past(n))
            if bias is None:
                dve.tensor_tensor(r, ps if m is None else r, hi, ALU.subtract).then_inc(s_r1, 1)
            else:
                dve.scalar_tensor_tensor(out=r, in0=ps, scalar=bias, in1=hi,
                                         op0=ALU.add, op1=ALU.subtract).then_inc(s_r1, 1)

        def dve_lo(dve, n, is_k):
            dve.wait_ge(s_mid, past(n))
            dve.tensor_tensor(parts[:, n % NP, 2 if is_k else 0, :], resid[:, n % 2, :], parts[:, n % NP, 1, :],
                              ALU.subtract).then_inc(s_lo, 1)

        def sp_store(sp, n, is_k, dst):
            u = n % NP
            sp.wait_ge(s_lo, past(n))
            for t0, k in ((0, 3), (3, 2), (5, 1)):
                k0 = 0 if is_k else 3 - k
                sp.dma_start(dst[t0:t0 + k].rearrange("k b p t -> p (k b) t"),
                             parts[:, u, k0:k0 + k, :].rearrange("p k (b t) -> p (k b) t", b=CB)
                             ).then_inc(s_stored[u], 16)

        def sp_load(sp, l, c, k):
            b = c * CB + k
            sp.wait_ge(s_av, past(NG * (B * l + b - NS) + NG - 1))
            sp.sem_inc(s_sp, 1)
            for half in range(2):
                for w in range(2):
                    sp.dma_start(stk[64 * half + 16:64 * half + 64, k, w].rearrange("p h t -> p (h t)"),
                                 qk_dram[l][w, c, :, k, 64 * half:64 * half + 64].rearrange("s (d h) t -> s d (h t)", h=8)
                                 ).then_inc(s_stk[k], 16)
            sp.dma_start(v_in[:, k].rearrange("p h w -> p (h w)"), v_dram[l][b]).then_inc(s_stk[k], 16)

        def pe_scores(pe, l, b, k, turn, pair):
            U = NG * (B * l + b) + 2 * pair
            if pair == 0:
                pe.wait_ge(s_stk[k], past_dma(NC * l + turn, 5))
                pe.wait_ge(s_mz, past(B * l + b - NS))
            pe.wait_ge(s_max, past(U - 1))
            for j in range(GH):
                for half in range(2):
                    h = GH * pair + j
                    r = slice(64 * half, 64 * half + 64)
                    mm = pe.matmul(bank[half][:, j * P:(j + 1) * P], qstk[r, k, h, :], kstk[r, k, h, :],
                                   start=True, stop=True)
                    if j == GH - 1:
                        mm.then_inc(s_sc, 1)

        def pe_maxT(pe, l, b, u):
            n = B * l + b
            pe.wait_ge(s_mparts, past(n))
            pe.wait_ge(s_mt, past(n - 1))
            pe.wait_ge(s_mt2, past(n - 1))
            pe.transpose(maxT_ps, mpad[:, u, :], identb[:]).then_inc(s_mtp, 1)

        def pe_scoresT(pe, l, b, k, u, pair):
            U = NG * (B * l + b) + 2 * pair
            if pair == 0:
                pe.wait_ge(s_mt, past(B * l + b))
                pe.wait_ge(s_mt2, past(B * l + b))
            pe.wait_ge(s_exp, past(U - 1))
            for j in range(GH):
                h = GH * pair + j
                for half in range(2):
                    r = slice(64 * half, 64 * half + 64)
                    mm = pe.matmul(bank[2 + half][:, j * P:(j + 1) * P], kstk[r, k, h, :], qstk[r, k, h, :],
                                   start=True, stop=True)
                    if j == GH - 1:
                        mm.then_inc(s_st, 1)

        def pe_values(pe, l, b, k, g):
            U = NG * (B * l + b) + g
            pe.wait_ge(s_exp, past(U))
            if g == 0:
                pe.wait_ge(s_oc, past(B * l + b - 1))
            blk = block_of(g)
            for j in range(GH):
                mm = pe.matmul(bank[4][OW * j:OW * j + VW, blk * P:(blk + 1) * P], v_in[:, k, GH * blk + j, :],
                               probs[:, g, j * P:(j + 1) * P], start=True, stop=True)
            mm.then_inc(s_av, 1)

        def pe_rows_of_heads(pe, l, b):
            n = B * l + b
            pe.wait_ge(s_oc, past(n))
            pe.wait_ge(s_norm, past(n - 1))
            for g in range(NG):
                mm = pe.transpose(bank[6][:, g * P:(g + 1) * P], o_sb[:, g * P:(g + 1) * P], ident)
            mm.then_inc(s_or, 1)

        def pe_attT(pe, l, b, u):
            n = B * l + b
            pe.wait_ge(s_norm, past(n))
            pe.wait_ge(s_xup, past(upd(ST_ATT[l], b) - 1))
            pe.transpose(attT_ps, att[:, u, :], ident).then_inc(s_atp, 1)

        def pe_outproj(pe, l, b, u):
            n = B * l + b
            pe.wait_ge(s_atc, past(n))
            pe.matmul(y_ps, attT[:, u, :], wo(l), start=True, stop=True).then_inc(s_y, 1)

        o_ps = bank[6][:].rearrange("p (h w) -> p h w", w=OW)
        maxT_ps = bank[5][:, 0:P // 2].bitcast(BF16)
        attT_ps = bank[7][:, 0:P]
        y_ps = bank[7][:, P:2 * P]

        def dve_max(dve, l, b, u, g):
            U = NG * (B * l + b) + g
            dve.wait_ge(s_sc, past(U))
            half, h0 = slots(g)[0]
            dve.tensor_reduce(negm[:, u, half, h0:h0 + GH], bank[g % 2][:].rearrange("p (h k) -> p h k", h=GH),
                              AX.X, ALU.max, negate=True).then_inc(s_max, 1)

        def dve_maxparts(dve, ch, l, b, u):
            dve.wait_ge(s_max, past(NG * (B * l + b) + NG - 1))
            mp = mpad[:, u, :].rearrange("p (half k h) -> p half k h", half=2, k=8)
            ch.step(dve.tensor_copy(mp[:, :, 0, :], negm[:, u]))
            dve.tensor_tensor(mp[:, :, 1, :], negm[:, u], mp[:, :, 0, :], ALU.subtract).then_inc(s_mparts, 1)

        def maxima(half, k):
            r = slice(64 * half, 64 * half + 16)
            return qstk[r, k], maxT_ps[r].unsqueeze(1).broadcast_to([16, 8, P])

        def act_maxima(act, n, k):
            act.wait_ge(s_mtp, past(n))
            o, i = maxima(0, k)
            act.activation(o, i, ACT.Copy).then_inc(s_mt, 1)

        def dve_maxima(dve, n, k):
            dve.wait_ge(s_mtp, past(n))
            o, i = maxima(1, k)
            dve.tensor_copy(o, i).then_inc(s_mt2, 1)

        def pool_zero(pool, l, b, k):
            pool.wait_ge(s_st, past(NG * (B * l + b) + NG - 1))
            pool.memset(qstk[0:16, k], 0.0)
            pool.memset(qstk[64:80, k], 0.0).then_inc(s_mz, 1)
            pool.wait_ge(s_mz, past(B * l + b))

        def dve_norm(dve, ch, l, b, u):
            n = B * l + b
            dve.wait_ge(s_or, past(n))
            o = o_ps
            ch.step(dve.reciprocal(rden[:], o[:, :, HD]))
            dve.wait_ge(s_atp, past(n - 2))
            dve.tensor_tensor(att[:, u, :].rearrange("p (h d) -> p h d", d=HD), o[:, :, 0:HD],
                              rden[:].unsqueeze(2).broadcast_to([P, H, HD]), ALU.mult).then_inc(s_norm, 1)

        def dve_update(dve, l, b):
            dve.wait_ge(s_y, past(B * l + b))
            dve.tensor_tensor(xnew[:], x_sb[:, b, :], y_ps, ALU.add).then_inc(s_xup, 1)

        def dve_update_stats(dve, ch, l, b):
            dve.wait_ge(s_xup, past(upd(ST_ATT[l], b)))
            dve_stats(dve, ch, b)

        def dve_stats(dve, ch, b):
            ch.step(dve.bn_stats(stats[:], xnew[:]))
            dve.tensor_scalar(x_sb[:, b, :], xnew[:], 1.0, None, ALU.mult)
            ch.step(dve.bn_aggr(mvnew[:], stats[:]))
            dve.tensor_scalar(mv[:, b, :], mvnew[:], 1.0, None, ALU.mult)
            dve.tensor_scalar(vareps[:, bass.ds(b, 1)], mvnew[:, 1:2], EPS, None, ALU.add).then_inc(s_var, 1)

        def dve_stats_of(dve, ch, batches):
            for b in batches:
                ins = dve.bn_stats(stats_all[:, b, :], x_sb[:, b, :])
            ch.step(ins)
            for b in batches:
                ins = dve.bn_aggr(mv[:, b, :], stats_all[:, b, :])
            ch.step(ins)
            bs = slice(batches[0], batches[-1] + 1)
            dve.tensor_scalar(vareps[:, bs], mv[:, bs, 1], EPS, None, ALU.add).then_inc(s_var, len(batches))

        def act_copies(act, src, dst, wait, n, sig):
            act.wait_ge(wait, past(n))
            act.activation(dst, src, ACT.Copy).then_inc(sig, 1)

        def act_exp(act, l, b, g):
            U = NG * (B * l + b) + g
            act.wait_ge(s_st, past(U))
            act.wait_ge(s_av, past(U - NG))
            act.activation(probs[:, g, :], bank[2 + g % 2][:], ACT.Exp, scale=float(1 / np.sqrt(HD))).then_inc(s_exp, 1)

        def pe_step(pe, l, b, k, turn_next, first=False, last=False):
            u, k_next = k % 2, (k + 1) % NS

            if not last:
                pe_scores(pe, l, b + 1, k_next, turn_next, 0)
            pe_scoresT(pe, l, b, k, u, 0)
            if not first:
                pe_rows_of_heads(pe, l, b - 1)
            if not last:
                pe_scores(pe, l, b + 1, k_next, turn_next, 1)
            pe_values(pe, l, b, k, 0)
            pe_values(pe, l, b, k, 1)
            if not first:
                pe_attT(pe, l, b - 1, 1 - u)
            pe_scoresT(pe, l, b, k, u, 1)
            if not first:
                pe_outproj(pe, l, b - 1, 1 - u)
            if not last:
                pe_maxT(pe, l, b + 1, 1 - u)
            pe_values(pe, l, b, k, 2)
            pe_values(pe, l, b, k, 3)

        def dve_step(dve, ch, l, b, k, first, last):
            u = k % 2
            if not last:
                dve_max(dve, l, b + 1, 1 - u, 0)
                dve_max(dve, l, b + 1, 1 - u, 1)
            if not first:
                dve_norm(dve, ch, l, b - 1, 1 - u)
            if not last:
                dve_max(dve, l, b + 1, 1 - u, 2)
                dve_max(dve, l, b + 1, 1 - u, 3)
                dve_maxparts(dve, ch, l, b + 1, 1 - u)
            if not first:
                dve_update(dve, l, b - 1)
            if not last:
                dve_maxima(dve, B * l + b + 1, (k + 1) % NS)
            if not first:
                dve_update_stats(dve, ch, l, b - 1)

        def act_step(act, l, b, k, first, last):
            n, u = B * l + b, k % 2
            if not first:
                act_copies(act, bank[4][:], o_sb[:], s_av, NG * n - 1, s_oc)
            act_exp(act, l, b, 0)
            act_exp(act, l, b, 1)
            if not first:
                act_copies(act, attT_ps, attT[:, 1 - u, :], s_atp, n - 1, s_atc)
            act_exp(act, l, b, 2)
            act_exp(act, l, b, 3)
            if not last:
                act_maxima(act, n + 1, (k + 1) % NS)

        def attention_pe(pe, l):
            pe_columns(pe, tjob_q(l, 0), 0, xn)
            for c in range(NC):
                u, n = c % 2, qjob(l, c)
                if c + 1 < NC:
                    pe_columns(pe, tjob_q(l, c + 1), 1 - u, xn)
                pe.wait_ge(s_xT, past(tjob_q(l, c)))
                pe.wait_ge(s_r1, past(n - 2))
                pe_project(pe, n, bank[2 + u][:], wq[:, l, :], xT[:, u, :])
                if l == 0:
                    pe_meansq(pe, NC + c)
            pe.wait_ge(s_xT, past(tjob_q(l, NC - 1)))
            for pair in range(2):
                pe_scores(pe, l, 0, 0, 0, pair)
            pe.wait_ge(s_r1, past(qjob(l, NC - 1)))
            pe_maxT(pe, l, 0, 0)
            pe_step(pe, l, 0, 0, 0, first=True)
            with pe.Fori(0, NC - 1) as i:
                for k in range(1, CB + 1):
                    pe_step(pe, l, i * CB + k, k % CB, i + (k + 1) // CB)
            for b in range(B - 3, B):
                pe_step(pe, l, b, b % CB, NC - 1, last=b == B - 1)
            pe_rows_of_heads(pe, l, B - 1)
            pe_attT(pe, l, B - 1, 1)
            pe_outproj(pe, l, B - 1, 1)

        def attention_dve(dve, ch, l):
            for c in range(NC):
                dve_rows(dve, ST_ATT[l], c)
            bias = None if l == 0 else colbias[:, 2 * l:2 * l + 1]
            for c in range(NC):
                n, ps = qjob(l, c), bank[2 + c % 2][:]
                if l == 0:
                    dve_heads(dve, n, ps, NC + c, colbias[:, 0:1])
                    if c > 0:
                        dve_lo(dve, n - 1, False)
                    dve_r1(dve, n, False, ps, None, NC + c)
                else:
                    dve_r1(dve, n, False, ps, bias)
                    dve_lo(dve, n, False)
            if l == 0:
                dve_lo(dve, qjob(l, NC - 1), False)
            if l > 0:
                dve.wait_ge(s_xb, l)
            ch.step(dve.memset(bank[4][:], 0.0))
            for g in range(NG):
                dve_max(dve, l, 0, 0, g)
            dve_maxparts(dve, ch, l, 0, 0)
            dve_maxima(dve, B * l, 0)
            dve_step(dve, ch, l, 0, 0, True, False)
            with dve.Fori(0, NC - 1) as i:
                ch.loop(i, 4 * CB)
                for k in range(1, CB + 1):
                    dve_step(dve, ch, l, i * CB + k, k % CB, False, False)
            ch.end(NC - 1)
            for b in range(B - 3, B):
                dve_step(dve, ch, l, b, b % CB, False, b == B - 1)
            dve_norm(dve, ch, l, B - 1, 1)
            dve_update(dve, l, B - 1)
            dve_update_stats(dve, ch, l, B - 1)

        def attention_act(act, l):
            act.wait_ge(s_vp, past(3 * NC - 1))

            def columns(c):
                if c < NC:
                    act.wait_ge(s_proj, past(qjob(l, c) - 2))
                    act_columns(act, tjob_q(l, c), c % 2)

            def squares(c):
                if l == 0 and c < NC:
                    act_square(act, qjob(l, c), bank[2 + c % 2][:], NC + c)
                    act_root(act, qjob(l, c), NC + c)
            bias = None if l == 0 else colbias[:, 2 * l:2 * l + 1]
            columns(0)
            squares(0)
            columns(1)
            for c in range(NC):
                squares(c + 1)
                act_hi(act, qjob(l, c), False, bank[2 + c % 2][:], bias, NC + c if l == 0 else None)
                act_mid(act, qjob(l, c))
                columns(c + 2)
            act_maxima(act, B * l, 0)
            act_step(act, l, 0, 0, True, False)
            with act.Fori(0, NC - 1) as i:
                for k in range(1, CB + 1):
                    act_step(act, l, i * CB + k, k % CB, False, False)
            for b in range(B - 3, B):
                act_step(act, l, b, b % CB, False, b == B - 1)
            act_copies(act, bank[4][:], o_sb[:], s_av, NG * B * (l + 1) - 1, s_oc)
            act_copies(act, attT_ps, attT[:, 1, :], s_atp, B * l + B - 1, s_atc)

        def attention_sp(sp, l):
            def store(c):
                sp_store(sp, qjob(l, c), False, qk_dram[l][0, c])
            store(0)
            stored(sp, qjob(l, 0))
            for k in range(CB):
                sp_load(sp, l, 0, k)
            for c in range(1, NC):
                store(c)
            for c in range(1, NC):
                stored(sp, qjob(l, c))
            if l == 0:
                for t, s in loads5:
                    sp.dma_start(t, s).then_inc(s_w5, 16)
            with sp.Fori(1, NC) as c:
                for k in range(CB):
                    sp_load(sp, l, c, k)

        def chunk_dram(t, c):
            return t[bass.ds(c * CB, CB)] if not isinstance(c, int) else t[c * CB:(c + 1) * CB]

        def rstd_ready(eng, n, c):
            eng.wait_ge(s_rstd, past(NC * n + c))

        def pool_rstd_chunk(pool, n, c):
            cs = slice(c * CB, (c + 1) * CB)
            pool.wait_ge(s_var, past(B * n + c * CB + CB - 1))
            pool.tensor_tensor(rstd[:, cs], vareps[:, cs], neg_half[:, 0:CB], ALU.pow).then_inc(s_rstd, 1)
            rstd_ready(pool, n, c)

        def attention_pool(pool, l):
            n = norm(ST_ATT[l]) + 1
            for c in range(NC):
                for k in range(CB):
                    pool_zero(pool, l, c * CB + k, k)
                if c > 0:
                    pool_rstd_chunk(pool, n, c - 1)
            pool_rstd_chunk(pool, n, NC - 1)

        def dve_rows(dve, st, c):
            u = c % 2
            rstd_ready(dve, norm(st), c)
            dve.wait_ge(s_tr, past(tjob(st, c) - 2))
            for k in range(CB):
                b = c * CB + k
                ins = dve.tensor_scalar(xn[:, u, k, :], x_sb[:, b, :], mv[:, b, 0:1], rstd[:, bass.ds(b, 1)],
                                        ALU.subtract, ALU.mult)
            ins.then_inc(s_xn, 1)

        def pe_columns(pe, t, u, src):
            pe.wait_ge(s_xn, past(t - NC))
            pe.wait_ge(s_xT, past(t - 2))
            for k in range(CB):
                mm = pe.transpose(bank[u][:, k * P:(k + 1) * P], src[:, u, k, :], ident)
            mm.then_inc(s_tr, 1)

        def act_columns(act, t, u):
            act.wait_ge(s_tr, past(t))
            act.activation(xT[:, u, :], bank[u][:], ACT.Copy).then_inc(s_xT, 1)

        def bank_used(st, c):
            return past(upd(st, (c - 2) * CB + CB - 1))

        def pe_rows(pe, st, c, w, n=P):
            u = c % 2
            pe.wait_ge(s_xT, past(tjob(st, c)))
            for k in range(CB):
                mm = pe.matmul(bank[2 + u][:, k * n:(k + 1) * n], xT[:, u, k * P:(k + 1) * P], w,
                               start=True, stop=True)
            mm.then_inc(s_rp, 1)

        def dve_update_chunk(dve, ch, st, c, rp, scale=None):
            u = c % 2
            dve.wait_ge(s_rp, past(rp))
            bs = slice(c * CB, (c + 1) * CB)
            src, xc = bank[2 + u][:], x_sb[:, bs, :].rearrange("p b d -> p (b d)")
            if scale is None:
                ins = dve.tensor_tensor(xc, xc, src, ALU.add)
            else:
                ins = dve.scalar_tensor_tensor(out=xc, in0=src, scalar=scale, in1=xc, op0=ALU.mult, op1=ALU.add)
            ins.then_inc(s_xup, CB)
            dve.wait_ge(s_xup, past(upd(st, c * CB + CB - 1)))
            dve_stats_of(dve, ch, range(c * CB, (c + 1) * CB))

        def flat(t):
            return t.rearrange("p b d -> p (b d)")

        def over(row, n):
            return row.unsqueeze(1).broadcast_to([P, n, row.shape[1]])

        def ffn0_dve(dve, ch):
            st = ST_FFN0
            dve.wait_ge(s_wmid, 16 * len(loads_mid))
            rstd_ready(dve, norm(st), NC - 1)
            ch.step(dve.tensor_copy(rs1[:], rstd[:]))
            ch.step(dve.tensor_tensor(vareps[:], mv[:, :, 1], rs1[:], ALU.mult))
            ch.step(dve.tensor_tensor(vareps[:], vareps[:], rs1[:], ALU.mult))
            dve.tensor_scalar(vareps[:], vareps[:], 1e-3, None, ALU.add).then_inc(s_var, B)
            dve.tensor_reduce(sc[:, 0:1], w_f0[:], AX.X, ALU.add, apply_absolute_value=True).then_inc(s_dve1, 1)
            for c in range(NC):
                cs = slice(c * CB, (c + 1) * CB)
                rstd_ready(dve, norm(st) + 1, c)
                ch.step(dve.tensor_tensor(rs1[:, cs], rs1[:, cs], rstd[:, cs], ALU.mult))
                for k in range(CB):
                    b = c * CB + k
                    ins = dve.tensor_scalar(xall[:, b, :], x_sb[:, b, :], mv[:, b, 0:1], rs1[:, b:b + 1],
                                            ALU.subtract, ALU.mult)
                ch.step(ins)
                xc = xall[:, c * CB:(c + 1) * CB, :]
                ch.step(dve.tensor_tensor(xc, xc, over(lnrow[:, 0, :], CB), ALU.mult))
                ch.step(dve.tensor_tensor(xc, xc, over(lnrow[:, 1, :], CB), ALU.add))
                ch.step(dve.tensor_reduce(amax[:, c:c + 1], flat(xc), AX.X, ALU.max, apply_absolute_value=True))
            dve.tensor_reduce(sc[:, 1:2], amax[:], AX.X, ALU.max).then_inc(s_dve1, 1)
            dve.wait_ge(s_pe1, PE1["amaxT"])
            dve.tensor_reduce(sc[0:1, 2:3], bank[6][0:1, 0:P], AX.X, ALU.max).then_inc(s_dve1, 1)
            beta, gain, lo = sc[:, 3:4], sc[:, 4:5], sc[:, 5:6]
            ch.step(dve.tensor_scalar(beta, bank[5][:, 0:1], 1.0 / (P * P), None, ALU.mult))
            ch.step(dve.tensor_scalar(gain, beta, 1e-5, None, ALU.add))
            ch.step(dve.reciprocal(gain, gain))
            ch.step(dve.tensor_scalar(w_t0[:, 0, :], w_f0[:], gain, 0.5, ALU.mult, ALU.is_gt))
            ch.step(dve.tensor_scalar(w_t0[:, 1, :], w_f0[:], gain, -0.5, ALU.mult, ALU.is_lt))
            ch.step(dve.tensor_tensor(w_t0[:, 0, :], w_t0[:, 0, :], w_t0[:, 1, :], ALU.subtract))
            dve.wait_ge(s_pe1, PE1["amax"])
            gam, to_q, to_y = sc[:, 6:7], sc[:, 7:8], sc[:, 8:9]
            ch.step(dve.tensor_copy(gam, bank[7][:, 0:1]))
            ch.step(dve.reciprocal(to_q, gam))
            ch.step(dve.tensor_scalar(to_q, to_q, 128.0, None, ALU.mult))
            ch.step(dve.tensor_tensor(to_y, gam, beta, ALU.mult))
            ch.step(dve.tensor_scalar(to_y, to_y, 1.0 / 128, None, ALU.mult))
            dve.drain().then_inc(s_dve1, 1)
            lim = float(np.float32(128.0 - 1e-5))

            def rows(c):
                dve.wait_ge(s_tr, past(tjob(st, c) - 2))
                xc = xn[:, c % 2]
                ch.step(dve.tensor_scalar(xc, xall[:, c * CB:(c + 1) * CB, :], to_q, lim, ALU.mult, ALU.min))
                dve.tensor_scalar(xc, xc, -lim, None, ALU.max).then_inc(s_xn, 1)
            for c in range(NC):
                rows(c)
            for c in range(NC):
                dve_update_chunk(dve, ch, st, c, c, scale=to_y)

        def ffn0_pe(pe):
            pe.wait_ge(s_wmid, 16 * len(loads_mid))
            pe.wait_ge(s_dve1, DVE1["wabs0"])
            pe.matmul(bank[5][:, 0:1], ones_sq[:], sc[:, 0:1], start=True, stop=True).then_inc(s_pe1, 1)
            pe.wait_ge(s_dve1, DVE1["amax_col"])
            pe.transpose(bank[6][0:1, 0:P], sc[:, 1:2], ident).then_inc(s_pe1, 1)
            pe.wait_ge(s_dve1, DVE1["amax_row"])
            pe.matmul(bank[7][:, 0:1], ones_row[0:1, :], sc[0:1, 2:3], start=True, stop=True).then_inc(s_pe1, 1)
            pe.wait_ge(s_dve1, DVE1["ternary0"])
            pe_columns(pe, tjob(ST_FFN0, 0), 0, xn)
            for c in range(NC):
                if c + 1 < NC:
                    pe_columns(pe, tjob(ST_FFN0, c + 1), (c + 1) % 2, xn)
                pe.wait_ge(s_xup, bank_used(ST_FFN0, c))
                pe_rows(pe, ST_FFN0, c, w_t0[:, 0, :])

        def columns_act(act, st):
            for c in range(NC):
                act_columns(act, tjob(st, c), c % 2)

        RP_CORR = NC

        def corr_dve(dve, ch):
            st = ST_CORR
            dve_rows(dve, st, 0)
            dve_rows(dve, st, 1)
            for c in range(NC):
                if c + 2 < NC:
                    dve_rows(dve, st, c + 2)
                dve.wait_ge(s_rp, past(RP_CORR + c))
                w = CB * HD
                ins = dve.tensor_tensor(q1[:, c * w:(c + 1) * w].rearrange("p (b d) -> p b d", d=HD),
                                        bank[2 + c % 2][:, 0:w].rearrange("p (b d) -> p b d", d=HD),
                                        over(bq_c[:], CB), ALU.add)
                ins.then_inc(s_q1, 1)
            ch.step(dve.drain())
            dve.drain().then_inc(s_dve1, 1)
            dve.wait_ge(s_pe1, PE1["qkT"])
            dve.tensor_copy(flat(qk1T[:]), bank[5][:, 0:2 * P]).then_inc(s_dve1, 1)
            dve.wait_ge(s_pe1, PE1["corrM"])
            dve.tensor_copy(mm2[:], over(bank[6][:, 0:P], 2)).then_inc(s_dve1, 1)
            dve.wait_ge(s_pe1, PE1["corr"])
            ch.step(dve.tensor_copy(crow[:], bank[7][:, 0:P]))
            top, colv, z = sc[:, 10:11], sc[:, 11:12], sc[:, 12:13]
            ch.step(dve.tensor_tensor(cwork[:, 0, :], crow[:], ident, ALU.mult))
            ch.step(dve.tensor_reduce(colv, cwork[:, 0, :], AX.X, ALU.add))
            dve.tensor_reduce(top, crow[:], AX.X, ALU.max, negate=True).then_inc(s_dve1, 1)
            ch.step(dve.tensor_scalar(cwork[:, 1, :], crow[:], colv, None, ALU.is_equal))
            ch.step(dve.tensor_tensor(cwork[:, 1, :], cwork[:, 1, :], C["tie"], ALU.mult))
            ch.step(dve.tensor_scalar(cwork[:, 0, :], crow[:], colv, None, ALU.is_lt))
            dve.tensor_tensor(cwork[:, 0, :], cwork[:, 0, :], cwork[:, 1, :], ALU.add).then_inc(s_dve1, 1)
            dve.wait_ge(s_pe1, PE1["rank"])
            dve.wait_ge(s_act1, ACT1["corr_exp"])
            ch.step(dve.tensor_scalar(cwork[:, 1, :], bank[5][:, 0:P], K_TOP - 0.5, None, ALU.is_lt))
            ch.step(dve.tensor_tensor(cwork[:, 1, :], cwork[:, 1, :], cwork[:, 2, :], ALU.mult))
            ch.step(dve.tensor_reduce(z, cwork[:, 1, :], AX.X, ALU.add))
            ch.step(dve.reciprocal(z, z))
            dve.tensor_scalar(cwork[:, 0, :], cwork[:, 1, :], z, None, ALU.mult).then_inc(s_dve1, 1)
            dve.wait_ge(s_pe1, PE1["rolled"])
            dve.tensor_copy(rolled[:], bank[6][:, 0:P]).then_inc(s_dve1, 1)
            dve.wait_ge(s_pe1, PE1["rolled_out"])
            ch.step(dve.tensor_tensor(crow[:], bank[7][:, 0:P], bout_c[:], ALU.add))

            def rows(c):
                dve.wait_ge(s_rp, past(RP_CORR + NC + c - 2))
                for k in range(CB):
                    b = c * CB + k
                    ins = dve.tensor_scalar(ymask[:, c % 2, k, :], crow[:], C["own_batch"][:, b:b + 1], None, ALU.mult)
                ins.then_inc(s_ym, 1)
            rows(0)
            for c in range(NC):
                if c + 1 < NC:
                    rows(c + 1)
                dve_update_chunk(dve, ch, st, c, RP_CORR + NC + c)

        s_q1, s_ym = item("s_q1"), item("s_ym")

        def corr_pe(pe):
            st = ST_CORR
            pe_columns(pe, tjob(st, 0), 0, xn)
            for c in range(NC):
                if c + 1 < NC:
                    pe_columns(pe, tjob(st, c + 1), (c + 1) % 2, xn)
                pe.wait_ge(s_q1, past(c - 2))
                pe_rows(pe, st, c, w_c[:], HD)
            pe.wait_ge(s_dve1, DVE1["corr_in"])
            pe.transpose(bank[5][:, 0:P], q1[:], ident)
            pe.transpose(bank[5][:, P:2 * P], k1[:], ident).then_inc(s_pe1, 1)
            pe.wait_ge(s_dve1, DVE1["corr_T"])
            pe.matmul(bank[6][:, 0:P], qk1T[:, 0, :], qk1T[:, 1, :], start=True, stop=True).then_inc(s_pe1, 1)
            pe.wait_ge(s_skew, 32)
            pe.matmul(bank[7][:, 0:P], mean_sq[:], skew[:], start=True, stop=True).then_inc(s_pe1, 1)
            pe.wait_ge(s_dve1, DVE1["corr_G"])
            pe.matmul(bank[5][:, 0:P], ones_sq[:], cwork[:, 0, :], start=True, stop=True).then_inc(s_pe1, 1)
            pe.wait_ge(s_skew, 64)
            pe.matmul(bank[6][:, 0:P], skew[:], k1[:], start=True, stop=True).then_inc(s_pe1, 1)
            pe.wait_ge(s_dve1, DVE1["rolled_sb"])
            pe.matmul(bank[7][:, 0:P], rolled[:], wout_c[:], start=True, stop=True).then_inc(s_pe1, 1)
            for c in range(NC):
                u = c % 2
                pe.wait_ge(s_ym, past(c))
                pe.wait_ge(s_xup, bank_used(st, c))
                pe.matmul(bank[2 + u][:], C["mod8"], flat(ymask[:, u]), start=True, stop=True).then_inc(s_rp, 1)

        def corr_act(act):
            columns_act(act, ST_CORR)
            act.wait_ge(s_dve1, DVE1["corr_negmax"])
            act.activation(cwork[:, 2, :], crow[:], ACT.Exp, bias=sc[:, 10:11]).then_inc(s_act1, 1)

        def corr_sp(sp):
            sp.wait_ge(s_dve1, DVE1["corr_mm"])
            sp.dma_start(corr_dram, mm2[:].rearrange("p a n -> p (a n)")).then_inc(s_skew, 16)
            sp.wait_ge(s_skew, 16)
            sp.dma_start(skew[:], bass.AP(corr_dram.tensor, 0, [[2 * P + 1, P], [1, P]])).then_inc(s_skew, 16)
            sp.wait_ge(s_dve1, DVE1["corr_w"])
            sp.dma_start(wlag_dram, cwork[:, 0, :]).then_inc(s_skew, 16)
            sp.wait_ge(s_skew, 48)
            sp.dma_start(skew[:], bass.AP(wlag_dram.tensor, 0, [[P - 1, P], [1, P]])).then_inc(s_skew, 16)

        def twist_dve(dve, ch):
            st = ST_TWIST
            for k in range(2):
                w = (CN[4], GC[3])[k]
                ch.step(dve.tensor_scalar(w, ones_sq[0:32, :], w4c[:, k:k + 1], None, ALU.mult))
            ar = b_l1[:, 7:8]
            ch.step(dve.tensor_scalar(b_l1[:, 3:4], b_l1[:, 3:4], 0.5, None, ALU.mult))
            ch.step(dve.tensor_scalar(b_l1[:, 6:7], b_l1[:, 6:7], 0.5, None, ALU.mult))
            for c in range(NC):
                dve_rows(dve, st, c)
            for c in range(NC):
                dve.wait_ge(s_xT, past(tjob(st, c)))
                dve.tensor_reduce(gx[:, 0, c * CB:(c + 1) * CB], xall[:, c * CB:(c + 1) * CB, :], AX.X, ALU.add)
            ch.step(dve.drain())
            dve.tensor_scalar(gx[:, 0, :], gx[:, 0, :], 1.0 / P, None, ALU.mult).then_inc(s_dve1, 1)
            dve.wait_ge(s_act1, ACT1["g3"])
            ch.step(dve.tensor_scalar(acoef[:], gx[:, 3, :], ar, 0.7, ALU.mult, ALU.mult))
            ch.step(dve.tensor_scalar(acoef[:], acoef[:], 0.1, None, ALU.add))
            ch.step(dve.tensor_scalar(sc[:, 13:14], ar, 0.3, None, ALU.mult))
            dve.drain().then_inc(s_dve1, 1)
            for y in range(CYCLES):
                for c in range(NC):
                    n, u = NC * y + c, c % 2
                    cols = xcols[:, c * CW:(c + 1) * CW]
                    t3 = tf[:, u, :].rearrange("p (b t) -> p b t", b=CB)
                    dve.wait_ge(s_g4, past(n))
                    ch.step(dve.scalar_tensor_tensor(out=t3, in0=t3, scalar=sc[:, 13:14],
                                                     in1=acoef[:, c * CB:(c + 1) * CB].unsqueeze(2).broadcast_to([P, CB, P]),
                                                     op0=ALU.mult, op1=ALU.add))
                    dve.wait_ge(s_twp, past(n))
                    ch.step(dve.tensor_tensor(tws[:, u, :], bank[6 + u][:], tf[:, u, :], ALU.mult))
                    dve.tensor_tensor(cols, cols, tws[:, u, :], ALU.add).then_inc(s_cyc, 1)
                    if n == 0:
                        bitw_dve_sums(dve)
                    if n == 3:
                        bitw_dve_ternary(dve, ch)
                    if n == 7:
                        bitw_dve_copies(dve)
            for c in range(NC):
                dve_update_chunk(dve, ch, st, c, RP_CORR + 2 * NC + c)

        def twist_pe(pe):
            st = ST_TWIST
            for c in range(NC):
                pe_columns(pe, tjob(st, c), c % 2, xn)
            for k in range(3):
                pe.wait_ge(s_dve1, DVE1["gmean"]) if k == 0 else pe.wait_ge(s_act1, ACT1[f"g{k}"])
                w = GC[k + 1]
                pe.matmul(bank[5][0:w.shape[1], 0:B], w, gx[0:w.shape[0], k, :], start=True, stop=True).then_inc(s_pe1, 1)
            pe.wait_ge(s_act1, ACT1["g3"])
            items = NC * CYCLES

            def cols(n):
                c = n % NC
                return xcols[:, c * CW:(c + 1) * CW]
            for n in range(items + 1):
                u, m, v = n % 2, n - 1, (n - 1) % 2
                if n < items:
                    pe.wait_ge(s_cyc, past(n - NC))
                    pe.wait_ge(s_g1, past(n - 1))
                    pe.matmul(bank[2][:], CN[1], cols(n), start=True, stop=True).then_inc(s_c1, 1)
                if n > 0:
                    pe.wait_ge(s_g2, past(m))
                    pe.wait_ge(s_g3, past(m - 1))
                    pe.matmul(bank[4][0:32, :], CN[3], h2[:, v, :], start=True, stop=True).then_inc(s_c3, 1)
                    pe.wait_ge(s_cyc, past(m - 2))
                    pe.matmul(bank[6 + v][:], C["twist"], cols(m), start=True, stop=True).then_inc(s_twp, 1)
                if n < items:
                    pe.wait_ge(s_g1, past(n))
                    pe.wait_ge(s_g2, past(n - 1))
                    pe.matmul(bank[3][0:64, :], CN[2], h1[:, u, :], start=True, stop=True).then_inc(s_c2, 1)
                if n > 0:
                    pe.wait_ge(s_g3, past(m))
                    pe.wait_ge(s_g4, past(m - 1))
                    pe.matmul(bank[5][:], CN[4], h3[:, v, :], start=True, stop=True).then_inc(s_c4, 1)
                if n == 2:
                    bitw_pe_mean(pe)
                if n == 6:
                    bitw_pe_transpose(pe)
            for c in range(NC):
                u = c % 2
                pe.wait_ge(s_cyc, past(NC * (CYCLES - 1) + c))
                pe.wait_ge(s_g4, past(NC * CYCLES - 1))
                pe.wait_ge(s_xup, bank_used(st, c))
                for k in range(CB):
                    b = c * CB + k
                    mm = pe.transpose(bank[2 + u][:, k * P:(k + 1) * P], xall[:, b, :], ident)
                mm.then_inc(s_rp, 1)

        def twist_act(act):
            st = ST_TWIST
            for c in range(NC):
                act.wait_ge(s_tr, past(tjob(st, c)))
                act.activation(xcols[:, c * CW:(c + 1) * CW], bank[c % 2][:], ACT.Copy).then_inc(s_xT, 1)
            for k, (m, f, s) in enumerate(((64, ACT.Gelu, 1.0), (32, ACT.Gelu, 1.0), (P, ACT.Tanh, 0.5))):
                act.wait_ge(s_pe1, PE1[f"g{k + 1}"])
                act.activation(gx[0:m, k + 1, :], bank[5][0:m, 0:B], f, bias=b_l1[0:m, 4 + k:5 + k], scale=s).then_inc(s_act1, 1)
            for n in range(NC * CYCLES + 1):
                u, m, v = n % 2, n - 1, (n - 1) % 2
                if n < NC * CYCLES:
                    act.wait_ge(s_c1, past(n))
                    act.activation(h1[:, u, :], bank[2][:], ACT.Gelu, bias=b_l1[:, 0:1]).then_inc(s_g1, 1)
                if n > 0:
                    act.wait_ge(s_c3, past(m))
                    act.activation(h3[:, v, :], bank[4][0:32, :], ACT.Gelu, bias=b_l1[0:32, 2:3]).then_inc(s_g3, 1)
                if n < NC * CYCLES:
                    act.wait_ge(s_c2, past(n))
                    act.activation(h2[:, u, :], bank[3][0:64, :], ACT.Gelu, bias=b_l1[0:64, 1:2]).then_inc(s_g2, 1)
                if n > 0:
                    act.wait_ge(s_c4, past(m))
                    act.wait_ge(s_cyc, past(m - 2))
                    act.activation(tf[:, v, :], bank[5][:], ACT.Tanh, bias=b_l1[:, 3:4], scale=0.5).then_inc(s_g4, 1)

        def bitw_dve_sums(dve):
            dve.wait_ge(s_w7, 16 * len(loads7))
            dve.tensor_reduce(bsc[:, 0:2], wb[:], AX.X, ALU.add, apply_absolute_value=True).then_inc(s_dve1, 1)

        def bitw_dve_ternary(dve, ch):
            dve.wait_ge(s_pe1, PE1["bit_mean"])
            ch.step(dve.tensor_scalar(bsc[:, 2:4], bank[0][:, 0:2], 1.0 / (P * FF), 1e-5, ALU.mult, ALU.max))
            ch.step(dve.reciprocal(bsc[:, 4:6], bsc[:, 2:4]))
            for k in range(2):
                ch.step(dve.tensor_scalar(wbt[:, k, :], wb[:, k, :], bsc[:, 4 + k:5 + k], 0.5, ALU.mult, ALU.is_gt))
                ch.step(dve.tensor_scalar(wb[:, k, :], wb[:, k, :], bsc[:, 4 + k:5 + k], -0.5, ALU.mult, ALU.is_lt))
                ins = dve.tensor_tensor(wbt[:, k, :], wbt[:, k, :], wb[:, k, :], ALU.subtract)
                if k == 0:
                    ch.step(ins)
            ins.then_inc(s_dve1, 1)

        def bitw_dve_copies(dve):
            dve.wait_ge(s_pe1, PE1["bit_wT"])
            dve.tensor_copy(w1T[:], bank[0][:, 0:FF // 2].bitcast(BF16))
            dve.tensor_copy(w2T[:], bank[1][:, 0:FF // 2].bitcast(BF16)).then_inc(s_dve1, 1)

        def bitw_pe_mean(pe):
            pe.wait_ge(s_dve1, DVE1["bit_abs"])
            pe.matmul(bank[0][:, 0:2], ones_sq[:], bsc[:, 0:2], start=True, stop=True).then_inc(s_pe1, 1)

        def bitw_pe_transpose(pe):
            pe.wait_ge(s_dve1, DVE1["bit_tern"])
            for k in range(2):
                o = bank[k][:, 0:FF // 2].bitcast(BF16)
                for f in range(FK):
                    mm = pe.transpose(o[:, f * P:(f + 1) * P], wbt[:, k, f * P:(f + 1) * P], identb[:])
            mm.then_inc(s_pe1, 1)

        RP_MOE = RP_CORR + 3 * NC

        def moe_route_dve(dve, ch):
            st = ST_MOE
            for c in range(NC):
                rstd_ready(dve, norm(st), c)
                for k in range(CB):
                    b = c * CB + k
                    ins = dve.tensor_scalar(xall[:, b, :], x_sb[:, b, :], mv[:, b, 0:1], rstd[:, b:b + 1],
                                            ALU.subtract, ALU.mult)
                ins.then_inc(s_xn, 1)
            lg, eq, hot, tot, sa, sbb, cmp, tmp = (rt[:, k] for k in range(8))
            for c in range(NC):
                dve.wait_ge(s_rp, past(RP_MOE + c))
                dve.tensor_copy(lg[:, c * CB:(c + 1) * CB, :],
                                bank[2 + c % 2][:, 0:CB * NE].rearrange("p (b e) -> p b e", e=NE)).then_inc(s_lg, 1)
            ch.step(dve.drain())

            def of_batch(v):
                return v.unsqueeze(2).broadcast_to([P, B, NE])
            ch.step(dve.tensor_reduce(rs[:, 0, :], lg, AX.X, ALU.max))
            ch.step(dve.tensor_tensor(eq, lg, of_batch(rs[:, 0, :]), ALU.is_equal))
            ch.step(dve.tensor_tensor(eq, eq, over(C["first"], B), ALU.mult))
            ch.step(dve.tensor_reduce(rs[:, 0, :], eq, AX.X, ALU.max))
            dve.tensor_tensor(hot, eq, of_batch(rs[:, 0, :]), ALU.is_equal).then_inc(s_dve1, 1)
            dve.wait_ge(s_pe1, PE1["prefix"])
            earlier = lg
            dve.tensor_copy(earlier, bank[6][:, 0:P].rearrange("p (b e) -> p b e", e=NE))
            dve.tensor_copy(tot, bank[7][:, 0:P].rearrange("p (b e) -> p b e", e=NE)).then_inc(s_dve1, 1)
            dve.wait_ge(s_dve1, DVE1["prefix_read"])
            a = tot
            for step, o in ((1, sa), (2, sbb), (4, sa), (8, sbb)):
                dve.tensor_copy(o[:, 0:step], a[:, 0:step])
                ch.step(dve.tensor_tensor(o[:, step:B], a[:, step:B], a[:, 0:B - step], ALU.add))
                a = o
            n_e = a[:, B - 1, :]
            cm = cmp.rearrange("p b e -> p (b e)").rearrange("p (e k) -> p e k", k=B)
            ch.step(dve.tensor_tensor(cm, n_e.unsqueeze(2).broadcast_to([P, NE, B]), over(C["tile_rows"], NE), ALU.is_gt))
            tiles, e1, e2 = rs[:, 1, 0:NE], rs[:, 2, 0:NE], rs[:, 3, 0:NE]
            ch.step(dve.tensor_reduce(tiles, cm, AX.X, ALU.add))
            s = tiles
            for step, o in ((1, e1), (2, e2), (4, e1)):
                dve.tensor_copy(o[:, 0:step], s[:, 0:step])
                ch.step(dve.tensor_tensor(o[:, step:NE], s[:, step:NE], s[:, 0:NE - step], ALU.add))
                s = o
            start = rs[:, 4, 0:NE]
            ch.step(dve.tensor_tensor(start, e1, tiles, ALU.subtract))
            ch.step(dve.tensor_scalar(start, start, float(P), float(T1 * P), ALU.mult, ALU.add))
            ch.step(dve.tensor_tensor(a, a, tot, ALU.subtract))
            ch.step(dve.tensor_tensor(a, a, earlier, ALU.add))
            ch.step(dve.tensor_tensor(a, a, over(start, B), ALU.add))
            ch.step(dve.tensor_tensor(a, a, hot, ALU.mult))
            ch.step(dve.tensor_reduce(rs[:, 5, :], a, AX.X, ALU.add))
            dve.tensor_copy(pos[:], rs[:, 5, :])
            dve.tensor_scalar(pos_y[:], rs[:, 5, :], float(-T1 * P), None, ALU.add)
            x3 = rx[:].rearrange("p (j e) -> p j e", e=NE)
            ch.step(dve.tensor_tensor(x3, C["tile_no"].unsqueeze(2).broadcast_to([P, NX, NE]), over(e1, NX), ALU.is_ge))
            tj = rt[:, 7].rearrange("p b e -> p (b e)")[:, 0:NX]
            ch.step(dve.tensor_reduce(tj, x3, AX.X, ALU.add))
            dve.tensor_scalar(etab[:], tj, float(NE - 1), None, ALU.min).then_inc(s_dve1, 1)

        def moe_route_pe(pe):
            st = ST_MOE
            def columns(c):
                if c < NC:
                    pe.wait_ge(s_xn, past(tjob(st, c) - NC))
                    pe.wait_ge(s_xT, past(tjob(st, c) - 2))
                    for k in range(CB):
                        mm = pe.transpose(bank[c % 2][:, k * P:(k + 1) * P], xall[:, c * CB + k, :], ident)
                    mm.then_inc(s_tr, 1)
            columns(0)
            for c in range(NC):
                columns(c + 1)
                pe.wait_ge(s_lg, past(c - 2))
                pe_rows(pe, st, c, w_g[:], NE)
            pe.wait_ge(s_dve1, DVE1["onehot"])
            hot = rt[:, 2].rearrange("p b e -> p (b e)")
            pe.matmul(bank[6][:, 0:P], C["before"], hot, start=True, stop=True)
            pe.matmul(bank[7][:, 0:P], ones_sq[:], hot, start=True, stop=True).then_inc(s_pe1, 1)

        def expert(pe, n):
            return pe.value_load(etab[0:1, bass.ds(n - T1, 1)] if not isinstance(n, int) else etab[0:1, n - T1:n - T1 + 1],
                                 min_val=0, max_val=NE - 1)

        def wslice(e, at, n):
            if isinstance(e, int):
                return wmoe[:, e, at:at + n]
            return wmoe[:].rearrange("p e w -> p (e w)")[:, bass.ds(e * (3 * FF) + at, n)]

        def pe_tileT(pe, n, u, turn):
            pe.wait_ge(s_rl[u], past_dma(turn))
            pe.wait_ge(s_xs, past(n - 1))
            pe.transpose(bank[6][:, 0:P], xr[:, u, :], ident).then_inc(s_xtp, 1)

        def pe_up(pe, n, u, shared, e=None):
            pe.wait_ge(s_xs, past(n))
            pe.wait_ge(s_gl, past(n - 2))
            pe.wait_ge(s_g, past(n - 2))
            if e is None:
                e = NE if shared else expert(pe, n)
            pe.matmul(bank[u][:], xs[:, u, :], wslice(e, 0, FF), start=True, stop=True)
            pe.matmul(bank[2 + u][:], xs[:, u, :], wslice(e, FF, FF), start=True, stop=True).then_inc(s_h, 1)

        def pe_gT(pe, n, u):
            pe.wait_ge(s_g, past(n))
            pe.wait_ge(s_gt, past(n - 2))
            for f in range(FK):
                mm = pe.transpose(bank[4 + u][:, f * P:(f + 1) * P], gl[:, u, f * P:(f + 1) * P], ident)
            mm.then_inc(s_gtp, 1)

        def pe_down(pe, n, u, shared):
            pe.wait_ge(s_gt, past(n))
            pe.wait_ge(s_yo, past(n - 1))
            e = NE if shared else expert(pe, n)
            for f in range(FK):
                mm = pe.matmul(bank[7][:, 0:P], gT[:, u, f * P:(f + 1) * P], wslice(e, 2 * FF + f * P, P),
                               start=(f == 0), stop=(f == FK - 1))
            mm.then_inc(s_o, 1)

        def moe_pe(pe):
            def step(j, u, turn, up, down, e=None, ahead=False):
                if up is not None:
                    pe_up(pe, j + 1, 1 - u, up, e)
                if turn is not None:
                    pe_tileT(pe, j + 2, u, turn)
                if down is not None:
                    pe_down(pe, j - 1, 1 - u, down)
                e = expert(pe, j + 2) if ahead else None
                pe_gT(pe, j, u)
                return e
            pe.wait_ge(s_dve1, DVE1["prefix_read"])
            pe_tileT(pe, 0, 0, 0)
            pe_tileT(pe, 1, 1, 0)
            pe_up(pe, 0, 0, True)
            step(0, 0, 1, True, None)

            def steps(first, last, up, down):
                a = first % 2
                with pe.Fori(0, (last + 1 - first) // 2) as i:
                    e = None
                    for k in range(2):
                        u = (a + k) % 2
                        e = step(i * 2 + (first + k), u, i + (first + k + 2) // 2, up, down,
                                 e, ahead=not up and k == 0)
            steps(1, T1 - 2, True, True)
            pe.wait_ge(s_dve1, DVE1["route"])
            for j in (T1 - 1, T1):
                step(j, j % 2, (j + 2) // 2, False, True)
            steps(T1 + 1, T2 - 3, False, False)
            for j, up in ((T2 - 2, False), (T2 - 1, True), (T2, True)):
                step(j, j % 2, (j + 2) // 2, up, False)
            steps(T2 + 1, NT - 4, True, True)
            step(NT - 3, (NT - 3) % 2, (NT - 1) // 2, True, True)
            step(NT - 2, (NT - 2) % 2, None, True, True)
            step(NT - 1, (NT - 1) % 2, None, None, True)
            pe_down(pe, NT - 1, (NT - 1) % 2, True)

        def act_tile(act, n, u):
            act.wait_ge(s_xtp, past(n))
            act.activation(xs[:, u, :], bank[6][:, 0:P], ACT.Copy).then_inc(s_xs, 1)

        def act_gelu(act, n, u):
            act.wait_ge(s_h, past(n))
            act.wait_ge(s_gtp, past(n - 2))
            act.activation(gl[:, u, :], bank[u][:], ACT.Gelu).then_inc(s_gl, 1)

        def moe_act(act):
            columns_act(act, ST_MOE)
            act_tile(act, 0, 0)
            act_tile(act, 1, 1)
            act_gelu(act, 0, 0)
            with act.Fori(0, (NT - 3) // 2) as i:
                for k in range(2):
                    act_gelu(act, i * 2 + (k + 1), 1 - k)
                    act_tile(act, i * 2 + (k + 2), k)
            act_gelu(act, NT - 2, 1)
            act_tile(act, NT - 1, 0)
            act_gelu(act, NT - 1, 0)

        def moe_dve(dve, ch):
            def mul(n, u):
                dve.wait_ge(s_gl, past(n))
                dve.tensor_tensor(gl[:, u, :], gl[:, u, :], bank[2 + u][:], ALU.mult).then_inc(s_g, 1)

            def copyT(n, u):
                dve.wait_ge(s_gtp, past(n))
                dve.wait_ge(s_o, past(n - 2))
                dve.tensor_copy(gT[:, u, :], bank[4 + u][:]).then_inc(s_gt, 1)

            def down(n, u, turn):
                dve.wait_ge(s_o, past(n))
                dve.wait_ge(s_yst[u], past_dma(turn - 1))
                dve.tensor_copy(yo[:, u, :], bank[7][:, 0:P]).then_inc(s_yo, 1)

            def down_shared(n, b):
                dve.wait_ge(s_o, past(n))
                xb = x_sb[:, bass.ds(b, 1), :].rearrange("p b d -> p (b d)")
                dve.tensor_tensor(xb, xb, bank[7][:, 0:P], ALU.add).then_inc(s_yo, 1)
            mul(0, 0)
            mul(1, 1)
            copyT(0, 0)
            with dve.Fori(0, T1 // 2) as i:
                for k in range(2):
                    mul(i * 2 + (k + 2), k)
                    down_shared(i * 2 + k, i * 2 + k)
                    copyT(i * 2 + (k + 1), 1 - k)
            with dve.Fori(0, NX // 2) as i:
                for k in range(2):
                    mul(i * 2 + (T1 + k + 2), k)
                    down(i * 2 + (T1 + k), k, i)
                    copyT(i * 2 + (T1 + k + 1), 1 - k)
            mul(T2 + 1, 0)
            down(T2 - 1, 0, NX // 2)
            copyT(T2, 1)
            with dve.Fori(0, (NT - 2 - T2) // 2) as i:
                for k in range(2):
                    mul(i * 2 + (T2 + k + 2), 1 - k)
                    down_shared(i * 2 + (T2 + k), i * 2 + (T1 + k))
                    copyT(i * 2 + (T2 + k + 1), k)
            down_shared(NT - 2, B - 2)
            copyT(NT - 1, 0)
            down_shared(NT - 1, B - 1)
            ch.step(dve.drain())
            for c in range(NC):
                dve.wait_ge(s_gath[c], 16 * CB)
                xc = x_sb[:, c * CB:(c + 1) * CB, :]
                dve.tensor_tensor(xc, xc, ygath[:, c * CB:(c + 1) * CB, :], ALU.add).then_inc(s_xup, CB)
                dve.wait_ge(s_xup, past(upd(ST_MOE, c * CB + CB - 1)))
                dve_stats_of(dve, ch, range(c * CB, (c + 1) * CB))

        def moe_sp(sp):
            for c in range(NC):
                tile = c * CB if c * CB < T1 else NX + c * CB
                sp.wait_ge(s_xn, past(tjob(ST_MOE, c) - NC))
                sp.dma_start(rows_dram[tile:tile + CB].rearrange("b t d -> t b d"),
                             xall[:, c * CB:(c + 1) * CB, :]).then_inc(s_rows, 16)
            sp.wait_ge(s_rows, 16 * NC)

            def load(n, u):
                sp.wait_ge(s_xtp, past(n - 2))
                sp.sem_inc(s_sp, 1)
                sp.dma_start(xr[:, u, :], rows_dram[n]).then_inc(s_rl[u], 16)

            def store(n, u):
                sp.wait_ge(s_yo, past(n))
                sp.sem_inc(s_sp, 1)
                r = n - T1
                sp.dma_start(y_dram[bass.ds(r * P, P)] if not isinstance(n, int) else y_dram[r * P:(r + 1) * P],
                             yo[:, u, :]).then_inc(s_yst[u], 16)
            with sp.Fori(0, T1 // 2) as i:
                load(i * 2, 0)
                load(i * 2 + 1, 1)
            sp.wait_ge(s_scat, 16 * B)
            for n in range(T1, T1 + 4):
                load(n, n % 2)
            with sp.Fori(0, (NX - 4) // 2) as i:
                for u in range(2):
                    load(i * 2 + (T1 + u + 4), u)
                    store(i * 2 + (T1 + u), u)
            for n in range(T2 - 5, T2):
                load(n + 4, n % 2)
                store(n, n % 2)
            for n in range(T2 + 4, NT):
                load(n, n % 2)

        def moe_pool(pool):
            pool.wait_ge(s_dve1, DVE1["route"])
            pool.wait_ge(s_zero, 32)
            for b in range(B):
                pool.indirect_dma_start(rows_dram.rearrange("n t d -> (n t) d"),
                                        bass.IndirectOffsetOnAxis(ap=pos[:, b:b + 1], axis=0),
                                        xall[:, b, :], None).then_inc(s_scat, 16)
            pool.wait_ge(s_scat, 16 * B)
            pool.wait_ge(s_rows, 16 * NC)
            for u, n in ((0, NX // 2), (1, NX // 2 - 1)):
                pool.wait_ge(s_yst[u], past_dma(n))
            for b in range(B):
                pool.indirect_dma_start(ygath[:, b, :], None, y_dram,
                                        bass.IndirectOffsetOnAxis(ap=pos_y[:, b:b + 1], axis=0)).then_inc(s_gath[b // CB], 16)

        def bit_dve(dve, ch):
            st = ST_BIT
            rstd_ready(dve, norm(st), NC - 1)
            ch.step(dve.tensor_copy(rs1[:], rstd[:]))
            ch.step(dve.tensor_tensor(vareps[:], mv[:, :, 1], rs1[:], ALU.mult))
            ch.step(dve.tensor_tensor(vareps[:], vareps[:], rs1[:], ALU.mult))
            dve.tensor_scalar(vareps[:], vareps[:], 1e-5, None, ALU.add).then_inc(s_var, B)

            def quant_scales(q, wm):
                ch.step(dve.tensor_scalar(q[:, 0], q[:, 0], 1e-5, None, ALU.max))
                ch.step(dve.reciprocal(q[:, 1], q[:, 0]))
                ch.step(dve.tensor_scalar(q[:, 1], q[:, 1], 127.0, None, ALU.mult))
                ch.step(dve.tensor_scalar(q[:, 2], q[:, 0], 1.0 / 127, wm, ALU.mult, ALU.mult))

            def rows(c):
                u = c % 2
                q = bq[:, c % 3]
                cs = slice(c * CB, (c + 1) * CB)
                rstd_ready(dve, norm(st) + 1, c)
                ch.step(dve.tensor_tensor(rs1[:, cs], rs1[:, cs], rstd[:, cs], ALU.mult))
                xc = xn[:, u]
                for k in range(CB):
                    b = c * CB + k
                    ins = dve.tensor_scalar(xc[:, k, :], x_sb[:, b, :], mv[:, b, 0:1], rs1[:, b:b + 1],
                                            ALU.subtract, ALU.mult)
                ch.step(ins)
                ch.step(dve.tensor_reduce(q[:, 0], xc, AX.X, ALU.max, apply_absolute_value=True))
                quant_scales(q, bsc[:, 2:3])
                for k in range(CB):
                    ins = dve.tensor_scalar(xc[:, k, :], xc[:, k, :], q[:, 1, k:k + 1], 127.0, ALU.mult, ALU.min)
                ch.step(ins)
                ch.step(dve.tensor_scalar(xc, xc, -128.0, MAGIC, ALU.max, ALU.add))
                dve.wait_ge(s_tr, past(tjob(st, c) - 2))
                dve.tensor_scalar(xq[:, u], xc, MAGIC, None, ALU.subtract).then_inc(s_xn, 1)

            def bias(c, k):
                n, q = c * CB + k, bq[:, c % 3]
                dve.wait_ge(s_bh, past(n))
                dve.scalar_tensor_tensor(out=hg[:, c % 2, k, :], in0=bank[2 + n % 2][:], scalar=q[:, 2, k:k + 1],
                                         in1=b1row[:], op0=ALU.mult, op1=ALU.add).then_inc(s_bb, 1)

            def peak(c, k):
                dve.wait_ge(s_bg, past(c * CB + k))
                dve.tensor_reduce(bq[:, c % 3, 3, k:k + 1], hg[:, c % 2, k, :], AX.X, ALU.max, apply_absolute_value=True)

            def squares(c):
                q = bq[:, c % 3]
                dve.wait_ge(s_bsq, past(c * CB + CB - 1))
                dve.tensor_scalar(q[:, 5], q[:, 4], 1.0 / FF, 1e-5, ALU.mult, ALU.add).then_inc(s_bms, 1)

            def scales(c):
                q = bq[:, c % 3]
                dve.wait_ge(s_bpw, past(c))
                ch.step(dve.tensor_tensor(q[:, 0], q[:, 3], q[:, 6], ALU.mult))
                quant_scales(q, bsc[:, 3:4])
                ch.step(dve.tensor_tensor(q[:, 1], q[:, 1], q[:, 6], ALU.mult))

            def quant(c):
                def clip(k):
                    hk = hg[:, c % 2, k, :]
                    dve.tensor_scalar(hk, hk, bq[:, c % 3, 1, k:k + 1], 127.0, ALU.mult, ALU.min).then_inc(s_bclip, 1)
                clip(0)
                for k in range(CB):
                    if k + 1 < CB:
                        clip(k + 1)
                    hk = hg[:, c % 2, k, :]
                    dve.wait_ge(s_bclip, c * CB + k + 1)
                    dve.tensor_scalar(hk, hk, -128.0, MAGIC, ALU.max, ALU.add).then_inc(s_bq, 1)

            def update(c, k):
                n = c * CB + k
                dve.wait_ge(s_bo, past(n))
                dve.scalar_tensor_tensor(out=xall[:, n, :], in0=bank[6 + n % 2][:, 0:P],
                                         scalar=bq[:, c % 3, 2, k:k + 1], in1=xall[:, n, :],
                                         op0=ALU.mult, op1=ALU.add).then_inc(s_bx, 1)
            rows(0)
            dve.wait_ge(s_xb, len(ST_ATT))
            for c in range(NC + 1):
                for k in range(CB + 1):
                    if c < NC and k < CB:
                        bias(c, k)
                    if k == 1 and c + 1 < NC:
                        rows(c + 1)
                    if c > 0 and k > 0:
                        update(c - 1, k - 1)
                    if c < NC and k > 1:
                        peak(c, k - 2)
                if c < NC:
                    peak(c, CB - 1)
                    squares(c)
                    scales(c)
                    quant(c)

        def bit_pe(pe):
            st = ST_BIT
            def columns(c):
                t = tjob(st, c)
                pe.wait_ge(s_xn, past(t - NC))
                pe.wait_ge(s_xT, past(t - 2))
                o = bank[c % 2][:, 0:CW // 2].bitcast(BF16)
                for k in range(CB):
                    mm = pe.transpose(o[:, k * P:(k + 1) * P], xq[:, c % 2, k, :], identb[:])
                mm.then_inc(s_tr, 1)
                pe.wait_ge(s_xT, past(t))

            def inner(c, k):
                n = c * CB + k
                pe.wait_ge(s_bb, past(n - 2))
                pe.matmul(bank[2 + n % 2][:], xqT[:, c % 2, k * P:(k + 1) * P], w1T[:], start=True, stop=True).then_inc(s_bh, 1)

            def transposes(c, k):
                n = c * CB + k
                v = n % 2
                pe.wait_ge(s_bqb, past(n))
                pe.wait_ge(s_bt, past(n - 2))
                o = bank[4 + v][:, 0:FF // 2].bitcast(BF16)
                for f in range(FK):
                    mm = pe.transpose(o[:, f * P:(f + 1) * P], hq[:, v, f * P:(f + 1) * P], identb[:])
                mm.then_inc(s_btp, 1)

            def outer(c, k):
                n = c * CB + k
                v = n % 2
                pe.wait_ge(s_bt, past(n))
                pe.wait_ge(s_bx, past(n - 2))
                for f in range(FK):
                    mm = pe.matmul(bank[6 + v][:, 0:P], hqT[:, v, f * P:(f + 1) * P], w2T[:, f * P:(f + 1) * P],
                                   start=(f == 0), stop=(f == FK - 1))
                mm.then_inc(s_bo, 1)
            for c in range(NC + 1):
                if c < NC:
                    columns(c)
                for k in range(CB + 1):
                    if c < NC and k < CB:
                        inner(c, k)
                    if c > 0 and k < CB:
                        transposes(c - 1, k)
                    if c > 0 and k > 0:
                        outer(c - 1, k - 1)

        def bit_act(act):
            st = ST_BIT

            def gelu(c, k):
                n, u = c * CB + k, c % 2
                act.wait_ge(s_bb, past(n))
                act.activation(hg[:, u, k, :], hg[:, u, k, :], ACT.Gelu).then_inc(s_bg, 1)
                act.wait_ge(s_bg, past(n))
                act.activation(h1[:, 0, :], hg[:, u, k, :], ACT.Square, accum_out=bq[:, c % 3, 4, k:k + 1]).then_inc(s_bsq, 1)

            def rounded(c, k):
                n = c * CB + k
                act.wait_ge(s_bq, past(n))
                act.wait_ge(s_btp, past(n - 2))
                act.activation(hq[:, n % 2, :], hg[:, c % 2, k, :], ACT.Copy, bias=-MAGIC).then_inc(s_bqb, 1)

            def columns(c, k):
                n = c * CB + k
                act.wait_ge(s_btp, past(n))
                act.activation(hqT[:, n % 2, :], bank[4 + n % 2][:, 0:FF // 2].bitcast(BF16), ACT.Copy).then_inc(s_bt, 1)
            for c in range(NC + 1):
                if c < NC:
                    act.wait_ge(s_tr, past(tjob(st, c)))
                    act.activation(xqT[:, c % 2, :], bank[c % 2][:, 0:CW // 2].bitcast(BF16), ACT.Copy).then_inc(s_xT, 1)
                for k in range(CB + 1):
                    if c > 0 and k < CB:
                        rounded(c - 1, k)
                    if c > 0 and k > 0:
                        columns(c - 1, k - 1)
                    if c < NC and k > 0:
                        gelu(c, k - 1)

        def bit_pool(pool):
            for c in range(NC):
                q = bq[:, c % 3]
                if c == 0:
                    pool.tensor_tensor(xall[:], x_sb[:], over(b2row[:], B), ALU.add).then_inc(s_xb, 1)
                pool.wait_ge(s_bms, past(c))
                pool.tensor_tensor(q[:, 6], q[:, 5], neg_half[:, 0:CB], ALU.pow).then_inc(s_bpw, 1)


        def context(eng, c):
            eng.dma_start(ctx_in[:, c % 2], chunk_dram(I["ctx_1024"], c).rearrange("b t d -> t b d")
                          ).then_inc(s_ctx[c % 2], 16)

        @block.sync
        def _(sp):
            early = sum(CWIDTH[:CEARLY])
            sp.dma_start(cst[:, 0:early], I["consts"][:, 0:early]).then_inc(s_cst, 16)
            context(sp, 0)
            for t, s in loads[0::2]:
                sp.dma_start(t, s).then_inc(s_w, 16)
            context(sp, 1)
            sp.dma_start(x_sb[:], I["x"].rearrange("b t d -> t b d")).then_inc(s_x, 16)
            sp.dma_start(cst[:, early:], I["consts"][:, early:]).then_inc(s_cst2, 16)

            def store_k(c, l):
                sp_store(sp, kjob(c, l), True, qk_dram[l][1, c])

            def store_v(c, l):
                n = kjob(c, l)
                sp.wait_ge(s_vb, past(n))
                sp.dma_start(chunk_dram(v_dram[l], c).rearrange("b t w -> t b w"),
                             v_out[:, n % 2].rearrange("p b h w -> p b (h w)")).then_inc(s_vst[n % 2], 16)
            for c in range(NC):
                if c > 0:
                    store_k(c - 1, 0)
                for l in (1, 2):
                    store_v(c, l)
                    store_k(c, l)
                store_v(c, 0)
            store_k(NC - 1, 0)
            for n in range(3 * NC - NP, 3 * NC):
                stored(sp, n)
            for v in range(2):
                sp.wait_ge(s_vst[v], past_dma((3 * NC - 1) // 2))
            attention_sp(sp, 0)
            corr_sp(sp)
            attention_sp(sp, 1)
            moe_sp(sp)
            attention_sp(sp, 2)
            for c in range(NC):
                sp.wait_ge(s_bx, past(c * CB + CB - 1))
                sp.dma_start(out[c * CB:(c + 1) * CB].rearrange("b t d -> t b d"),
                             xall[:, c * CB:(c + 1) * CB, :]).then_inc(s_out, 16)
            sp.wait_ge(s_done, 1)
            sp.wait_ge(s_w1, 16 * len(loads1))
            sp.wait_ge(s_w5, 16 * len(loads5))
            sp.wait_ge(s_w7, 16 * len(loads7))
            sp.wait_ge(s_out, 16 * NC)

        @block.gpsimd
        def _(pool):
            for s, per in s_lead:
                pool.sem_inc(s, LEAD * per)
            pool.memset(neg_half[:], -0.5).then_inc(s_const, 1)
            pool.memset(eps6[:], 1e-6).then_inc(s_const, 1)
            pool.memset(v_out[:], 1.0).then_inc(s_const, 1)
            pool.memset(ones_row[:], 1.0).then_inc(s_const, 1)
            pool.memset(ones_sq[:], 1.0).then_inc(s_const, 1)
            pool.memset(mean_sq[:], 1.0 / (B * HD)).then_inc(s_const, 1)
            pool.memset(mpad[:], 0.0).then_inc(s_const, 1)
            pool.memset(stk[:], 0.0).then_inc(s_const, 1)
            pool.memset(xall[:], 0.0).then_inc(s_const, 1)
            pool.wait_ge(s_const, 9)
            pool.dma_start(rows_dram[T1:T1 + B].rearrange("n t d -> t n d"), xall[:]).then_inc(s_zero, 16)
            pool.dma_start(rows_dram[T1 + B:T2].rearrange("n t d -> t n d"), xall[:, 0:NX - B]).then_inc(s_zero, 16)
            for group, s_group in ((loads_mid, s_wmid), (loads1, s_w1), (loads7, s_w7)):
                for t, s in group:
                    pool.dma_start(t, s).then_inc(s_group, 16)
            pool.wait_ge(s_zero, 32)
            pool.wait_ge(s_wmid, 16 * len(loads_mid))
            after_att = [norm(st) + 1 for st in ST_ATT]
            for n in range(norm(ST_BIT) + 2):
                if n not in after_att:
                    for c in range(NC):
                        pool_rstd_chunk(pool, n, c)
                for l in range(3):
                    if n == norm(ST_ATT[l]):
                        if l > 0:
                            pool.wait_ge(s_xn, past(tjob_q(l, NC - 1) - NC))
                            pool.tensor_tensor(x_sb[:], x_sb[:], over(borow[:, l, :], B), ALU.add).then_inc(s_xb, 1)
                        attention_pool(pool, l)
                if n == norm(ST_MOE):
                    moe_pool(pool)
            bit_pool(pool)

        @block.scalar
        def _(act):
            for t, s in loads[1::2]:
                act.dma_start(t, s).then_inc(s_w, 16)
            def ctx_columns(c):
                if c < NC:
                    act.wait_ge(s_tr, past(tjob_ctx(c)))
                    act.wait_ge(s_vp, past(3 * (c - 1) - 1))
                    act.activation(xT[:, c % 2, :], bank[c % 2][:], ACT.Copy).then_inc(s_xT, 1)
                    if c + 2 < NC:
                        context(act, c + 2)

            def kb(l):
                return colbias[:, 2 * l + 1:2 * l + 2]
            ctx_columns(0)
            act.wait_ge(s_const, 9)
            act.wait_ge(s_wprep, 1)
            for c in range(NC + 1):
                if c > 0:
                    act_hi(act, kjob(c - 1, 0), True, None, None, c - 1)
                if c < NC:
                    act_hi(act, kjob(c, 1), True, bank[2][:], kb(1))
                if c > 0:
                    act_mid(act, kjob(c - 1, 0))
                if c < NC:
                    act_square(act, kjob(c, 0), bank[5][:], c)
                    act_mid(act, kjob(c, 1))
                    act_hi(act, kjob(c, 2), True, bank[3][:], kb(2))
                    ctx_columns(c + 1)
                    act_mid(act, kjob(c, 2))
                    act_root(act, kjob(c, 0), c)
            attention_act(act, 0)
            columns_act(act, ST_FFN0)
            corr_act(act)
            twist_act(act)
            attention_act(act, 1)
            moe_act(act)
            attention_act(act, 2)
            bit_act(act)

        @block.vector
        def _(dve):
            ch = Chain(dve, s_dve)
            dve.wait_ge(s_cst, 16)
            dve.tensor_copy(identb[:], ident)
            dve.wait_ge(s_w, 16 * len(loads))
            for l in range(2):
                for w, k in ((wq, 0), (wk, 1)):
                    dve.tensor_copy(w[:, l, :].rearrange("p (half d h) -> p half d h", half=2, d=8),
                                    wraw[:, 4 * l + k, :].rearrange("p (half h d) -> p half d h", half=2, d=8))
            dve.wait_ge(s_wt, 1)
            for w, k in ((wq, 0), (wk, 1)):
                dve.tensor_copy(w[:, 2, :].rearrange("p (half d h) -> p half d h", half=2, d=8),
                                bank[6][:, k * P:(k + 1) * P].rearrange("p (half h d) -> p half d h", half=2, d=8))
            dve.tensor_copy(wvo3[:].rearrange("p k n -> p (k n)"), bank[6][:, 2 * P:4 * P])
            dve.tensor_copy(colbias[:, 0:6], bank[7][:, 0:6]).then_inc(s_wprep, 1)
            dve.wait_ge(s_const, 9)

            def values(c, l):
                n = kjob(c, l)
                v = n % 2
                dve.wait_ge(s_vp, past(n))
                dve.wait_ge(s_vst[v], past_dma(n // 2 - 1))
                for k in range(CB):
                    o = v_out[:, v, k, :, 0:HD]
                    s = bank[6 + v][:, k * P:(k + 1) * P].rearrange("p (h d) -> p h d", d=HD)
                    if l == 0:
                        ins = dve.tensor_copy(o, s)
                    else:
                        ins = dve.tensor_tensor(o, s, bvrow[:, l, :].rearrange("p (h d) -> p h d", d=HD), ALU.add)
                ins.then_inc(s_vb, 1)
            for c in range(NC + 1):
                if c < NC:
                    dve.wait_ge(s_k1p, past(c))
                    dve.tensor_tensor(k1[:, c * (CB * HD):(c + 1) * (CB * HD)].rearrange("p (b d) -> p b d", d=HD),
                                      bank[4][:, 0:CB * HD].rearrange("p (b d) -> p b d", d=HD),
                                      over(bq_c[:], CB), ALU.add).then_inc(s_k1, 1)
                if c > 0:
                    dve_r1(dve, kjob(c - 1, 0), True, None, None, c - 1)
                if c < NC:
                    dve_r1(dve, kjob(c, 1), True, bank[2][:], colbias[:, 3:4])
                if c > 0:
                    dve_lo(dve, kjob(c - 1, 0), True)
                if c < NC:
                    values(c, 1)
                    dve_lo(dve, kjob(c, 1), True)
                    dve_r1(dve, kjob(c, 2), True, bank[3][:], colbias[:, 5:6])
                    values(c, 2)
                    dve_lo(dve, kjob(c, 2), True)
                    dve_heads(dve, kjob(c, 0), bank[5][:], c, colbias[:, 1:2])
                    values(c, 0)
                if c == 1:
                    dve.wait_ge(s_x, 16)
                    dve_stats_of(dve, ch, range(B))
            dve.wait_ge(s_cst2, 16)
            for half in range(2):
                r = slice(64 * half, 64 * half + 16)
                for k in range(NS):
                    dve.tensor_copy(kstk[r, k].rearrange("p h t -> p (h t)"), C["sel"][r])
            attention_dve(dve, ch, 0)
            ffn0_dve(dve, ch)
            corr_dve(dve, ch)
            dve.wait_ge(s_w1, 16 * len(loads1))
            twist_dve(dve, ch)
            attention_dve(dve, ch, 1)
            moe_route_dve(dve, ch)
            moe_dve(dve, ch)
            attention_dve(dve, ch, 2)
            bit_dve(dve, ch)
            dve.drain().then_inc(s_done, 1)

        @block.tensor
        def _(pe):
            pe.wait_ge(s_cst, 16)
            def ctx_columns(c):
                if c < NC:
                    pe.wait_ge(s_ctx[c % 2], 16 * (c // 2 + 1))
                    pe.wait_ge(s_xT, past(tjob_ctx(c) - 2))
                    for k in range(CB):
                        mm = pe.transpose(bank[c % 2][:, k * P:(k + 1) * P], ctx_in[:, c % 2, k, :], ident)
                    mm.then_inc(s_tr, 1)

            def values(c, l):
                n = kjob(c, l)
                pe.wait_ge(s_vb, past(n - 2))
                for k in range(CB):
                    mm = pe.matmul(bank[6 + n % 2][:, k * P:(k + 1) * P], xT[:, c % 2, k * P:(k + 1) * P], wv(l),
                                   start=True, stop=True)
                mm.then_inc(s_vp, 1)
            ctx_columns(0)
            pe.wait_ge(s_w, 16 * len(loads))
            for k in range(4):
                pe.transpose(bank[6][:, k * P:(k + 1) * P], wraw[:, 8 + k, :], ident)
            pe.matmul(bank[7][:, 2:6], C["perm"], colraw[:, 2:6], start=True, stop=True)
            pe.matmul(bank[7][:, 0:2], C["spread_d"][0:HD, :], colraw[0:HD, 0:2], start=True, stop=True).then_inc(s_wt, 1)
            pe.wait_ge(s_wprep, 1)
            for c in range(NC):
                xs = xT[:, c % 2, :]
                pe.wait_ge(s_xT, past(tjob_ctx(c)))
                pe.wait_ge(s_mse, past(c - 1))
                for k in range(CB):
                    mm = pe.matmul(bank[4][:, k * HD:(k + 1) * HD], xs[:, k * P:(k + 1) * P], w_c[:],
                                   start=True, stop=True)
                mm.then_inc(s_k1p, 1)
                for l in (1, 2):
                    pe.wait_ge(s_r1, past(kjob(c - 1, l)))
                    pe_project(pe, kjob(c, l), bank[1 + l][:], wk[:, l, :], xs)
                pe.wait_ge(s_rms, past(c - 1))
                pe_project(pe, kjob(c, 0), bank[5][:], wk[:, 0, :], xs)
                ctx_columns(c + 1)
                values(c, 1)
                pe.wait_ge(s_k1, past(c))
                pe_meansq(pe, c)
                values(c, 2)
                values(c, 0)
            attention_pe(pe, 0)
            ffn0_pe(pe)
            corr_pe(pe)
            pe.wait_ge(s_w1, 16 * len(loads1))
            twist_pe(pe)
            attention_pe(pe, 1)
            pe.wait_ge(s_w5, 16 * len(loads5))
            moe_route_pe(pe)
            moe_pe(pe)
            attention_pe(pe, 2)
            bit_pe(pe)


def kernel(**inputs):
    import concourse.bacc as _bacc
    from concourse.bass_utils import run_bass_kernel_spmd as _run

    nc = _bacc.Bacc("TRN2", target_bir_lowering=False, num_devices=1)
    arrays, aps = {}, {}
    arrays["consts"] = np.concatenate([CONSTS[k] for k in CORDER], axis=1)
    for name, a in inputs.items():
        arrays[name] = np.ascontiguousarray(a)
    for name, a in arrays.items():
        aps[name] = nc.dram_tensor(f"in_{name}", a.shape, mybir.dt.from_np(a.dtype), kind="ExternalInput").ap()
    out = nc.dram_tensor("out_x", (B, P, P), F32, kind="ExternalOutput").ap()
    build_program(nc, aps, out)
    r = _run(nc, [{f"in_{k}": v for k, v in arrays.items()}], core_ids=[0])
    return r.results[0]["out_x"]
```
